# Optimizing a Trainium2 kernel written in Bass

```python
import numpy as np
import jax
import jax.numpy as jnp

def _softmax(x, axis=-1):
    return jax.nn.softmax(x, axis=axis)

def _gelu(x):
    return jax.nn.gelu(x, approximate=True)

def _silu(x):
    return jax.nn.silu(x)

def _sigmoid(x):
    return jax.nn.sigmoid(x)

def _layernorm(x, axis=-1, eps=1e-05):
    m = jnp.mean(x, axis=axis, keepdims=True)
    v = jnp.var(x, axis=axis, keepdims=True)
    return (x - m) / jnp.sqrt(v + eps)

def _scatter_add(tgt, idx, src, axis=0):
    return tgt.at[idx].add(src)

def _segment_sum(src, seg, n):
    return jax.ops.segment_sum(src, seg, n)
kernel_name = 'mk_decoder_postln_d1_seqx_r8_d79719'

def setup_inputs(seed: int=0):
    np.random.seed(seed)
    _w = jnp.asarray

    def _rec_inputs():
        import jax
        import jax.numpy as jnp
        _rk = jax.random.key(seed)
        x = -0.0003929 + 0.9999 * jax.random.normal(jax.random.fold_in(_rk, 1), (16, 128, 256), jnp.float32)
        _lenS = 128 - jax.random.randint(jax.random.fold_in(_rk, 7), (16,), 0, max(1, 128 // 4) + 1, jnp.int32)
        _lenS2 = 128 - jax.random.randint(jax.random.fold_in(_rk, 8), (16,), 0, max(1, 128 // 4) + 1, jnp.int32)
        _ctx_2048P = jax.random.normal(jax.random.fold_in(_rk, 11), (16, 16, 256), jnp.float32)
        _ctx_2048c = jax.random.dirichlet(jax.random.fold_in(_rk, 511), 0.3 * jnp.ones((16,), jnp.float32), (16, 128))
        _ctx_2048t = jnp.einsum('bsk,bkd->bsd', _ctx_2048c, _ctx_2048P)
        _ctx_2048t = _ctx_2048t * jax.lax.rsqrt(jnp.mean(jnp.square(_ctx_2048t)) + 1e-12) * 0.953939
        ctx_2048 = -1.39393e-06 + 0.999914 * (_ctx_2048t + 0.3 * jax.random.normal(jax.random.fold_in(_rk, 611), (16, 128, 256), jnp.float32))
        itok_BxS_0_1023 = jax.random.randint(jax.random.fold_in(_rk, 12), (16, 128), 0, 128, jnp.int32)
        return (x, ctx_2048, itok_BxS_0_1023)
    x, ctx_2048, itok_BxS_0_1023 = _rec_inputs()

    def _L0_attn_setup():
        import jax, jax.numpy as jnp
        import numpy as np
        N_HEAD = 16
        RMS_EPS = 1.1920929e-07

        def _rotate_half(u):
            u1 = u[..., ::2]
            u2 = u[..., 1::2]
            return jnp.stack((-u2, u1), axis=-1).reshape(u.shape)

        def _rope_sin_cos(T, D):
            inv_freq = 1.0 / 10000.0 ** (jnp.arange(0, D, 2, dtype=jnp.float32) / D)
            t = jnp.arange(T, dtype=jnp.float32)
            freqs = t[:, None] * inv_freq[None, :]
            sin = jnp.repeat(jnp.sin(freqs), 2, axis=-1)
            cos = jnp.repeat(jnp.cos(freqs), 2, axis=-1)
            return (sin[None, None], cos[None, None])

        def _rms_norm(u):
            return u * jax.lax.rsqrt(jnp.mean(u * u, axis=-1, keepdims=True) + RMS_EPS)
        key = jax.random.key(seed)
        k1, k2, k3 = jax.random.split(key, 3)
        B, T, C = (2, 256, 256)
        x = jax.random.normal(k1, (B, T, C), dtype=jnp.float32)
        W_qkv = jax.random.normal(k2, (3 * C, C), dtype=jnp.float32) * 0.02
        W_o = jax.random.normal(k3, (C, C), dtype=jnp.float32) * 0.02
        return {'x': x, 'W_qkv': W_qkv, 'W_o': W_o}
    _L0_attn_all = _L0_attn_setup()
    _L0_attn_in = {k: v for k, v in _L0_attn_all.items() if k in ('W_qkv', 'W_o')}
    del _L0_attn_all

    def _L0_xattn_setup():
        import jax, jax.numpy as jnp
        import numpy as np
        B, Lq, Lk = (2, 512, 128)
        Q_DIM, KV_DIM = (256, 256)
        H, HD = (16, 128)
        KVC, QC, R = (64, 96, 64)
        LOOKBACK = 8
        NEG = -1e+30

        def _rope(x, L):
            half = x.shape[-1] // 2
            inv_freq = 1.0 / 10000.0 ** (jnp.arange(half, dtype=jnp.float32) / half)
            ang = jnp.arange(L, dtype=jnp.float32)[:, None] * inv_freq
            cos, sin = (jnp.cos(ang), jnp.sin(ang))
            x1, x2 = (x[..., :half], x[..., half:])
            return jnp.concatenate([x1 * cos - x2 * sin, x1 * sin + x2 * cos], axis=-1)
        key = jax.random.key(seed)
        ks = jax.random.split(key, 11)

        def w(k, shape, fan_in):
            return jax.random.normal(k, shape, jnp.float32) / np.sqrt(fan_in).astype(np.float32)
        return {'q': jax.random.normal(ks[0], (B, Lq, Q_DIM), jnp.float32), 'kv': jax.random.normal(ks[1], (B, Lk, KV_DIM), jnp.float32), 'seg_id': jnp.sort(jax.random.randint(ks[2], (B, Lq), 0, Lk), axis=-1), 'W_kvc': w(ks[3], (KV_DIM, KVC), KV_DIM), 'W_dq': w(ks[4], (Q_DIM, QC), Q_DIM), 'W_uq': w(ks[5], (QC, H * HD), QC), 'W_qr': w(ks[6], (QC, H * R), QC), 'W_uk': w(ks[7], (KVC, H * HD), KVC), 'W_kr': w(ks[8], (KVC, R), KVC), 'W_uv': w(ks[9], (KVC, H * HD), KVC), 'W_o': w(ks[10], (H * HD, Q_DIM), H * HD)}
    _L0_xattn_all = _L0_xattn_setup()
    _L0_xattn_in = {k: v for k, v in _L0_xattn_all.items() if k in ('W_kvc', 'W_dq', 'W_uq', 'W_qr', 'W_uk', 'W_kr', 'W_uv', 'W_o')}
    del _L0_xattn_all

    def _L0_ffn_setup():
        import jax, jax.numpy as jnp
        import numpy as np
        B, S, H = (1, 256, 256)
        E, K, I = (16, 4, 176)
        IS = 352
        CAP = 128
        key = jax.random.key(seed)
        ks = jax.random.split(key, 8)
        sc = 0.02
        return {'hidden_states': jax.random.normal(ks[0], (B, S, H), jnp.float32), 'gate_w': jax.random.normal(ks[1], (E, H), jnp.float32) * sc, 'w_gate': jax.random.normal(ks[2], (E, H, I), jnp.float32) * sc, 'w_up': jax.random.normal(ks[3], (E, H, I), jnp.float32) * sc, 'w_down': jax.random.normal(ks[4], (E, I, H), jnp.float32) * sc, 'sw_gate': jax.random.normal(ks[5], (H, IS), jnp.float32) * sc, 'sw_up': jax.random.normal(ks[6], (H, IS), jnp.float32) * sc, 'sw_down': jax.random.normal(ks[7], (IS, H), jnp.float32) * sc}
    _L0_ffn_all = _L0_ffn_setup()
    _L0_ffn_in = {k: v for k, v in _L0_ffn_all.items() if k in ('gate_w', 'w_gate', 'w_up', 'w_down', 'sw_gate', 'sw_up', 'sw_down')}
    del _L0_ffn_all
    return {'x': x, 'ctx_2048': ctx_2048, 'itok_BxS_0_1023': itok_BxS_0_1023, 'L0_attn_W_qkv': _L0_attn_in['W_qkv'], 'L0_attn_W_o': _L0_attn_in['W_o'], 'L0_xattn_W_kvc': _L0_xattn_in['W_kvc'], 'L0_xattn_W_dq': _L0_xattn_in['W_dq'], 'L0_xattn_W_uq': _L0_xattn_in['W_uq'], 'L0_xattn_W_qr': _L0_xattn_in['W_qr'], 'L0_xattn_W_uk': _L0_xattn_in['W_uk'], 'L0_xattn_W_kr': _L0_xattn_in['W_kr'], 'L0_xattn_W_uv': _L0_xattn_in['W_uv'], 'L0_xattn_W_o': _L0_xattn_in['W_o'], 'L0_ffn_gate_w': _L0_ffn_in['gate_w'], 'L0_ffn_w_gate': _L0_ffn_in['w_gate'], 'L0_ffn_w_up': _L0_ffn_in['w_up'], 'L0_ffn_w_down': _L0_ffn_in['w_down'], 'L0_ffn_sw_gate': _L0_ffn_in['sw_gate'], 'L0_ffn_sw_up': _L0_ffn_in['sw_up'], 'L0_ffn_sw_down': _L0_ffn_in['sw_down']}

def reference(x, ctx_2048, itok_BxS_0_1023, L0_attn_W_qkv, L0_attn_W_o, L0_xattn_W_kvc, L0_xattn_W_dq, L0_xattn_W_uq, L0_xattn_W_qr, L0_xattn_W_uk, L0_xattn_W_kr, L0_xattn_W_uv, L0_xattn_W_o, L0_ffn_gate_w, L0_ffn_w_gate, L0_ffn_w_up, L0_ffn_w_down, L0_ffn_sw_gate, L0_ffn_sw_up, L0_ffn_sw_down):
    import jax
    import jax.numpy as jnp

    def _L0_attn_ref(x, W_qkv, W_o):
        import jax, jax.numpy as jnp
        import numpy as np
        N_HEAD = 16
        RMS_EPS = 1.1920929e-07

        def _rotate_half(u):
            u1 = u[..., ::2]
            u2 = u[..., 1::2]
            return jnp.stack((-u2, u1), axis=-1).reshape(u.shape)

        def _rope_sin_cos(T, D):
            inv_freq = 1.0 / 10000.0 ** (jnp.arange(0, D, 2, dtype=jnp.float32) / D)
            t = jnp.arange(T, dtype=jnp.float32)
            freqs = t[:, None] * inv_freq[None, :]
            sin = jnp.repeat(jnp.sin(freqs), 2, axis=-1)
            cos = jnp.repeat(jnp.cos(freqs), 2, axis=-1)
            return (sin[None, None], cos[None, None])

        def _rms_norm(u):
            return u * jax.lax.rsqrt(jnp.mean(u * u, axis=-1, keepdims=True) + RMS_EPS)
        B, T, C = x.shape
        H = N_HEAD
        D = C // H
        qkv = jnp.einsum('btc,oc->bto', x, W_qkv).reshape(B, T, 3, H, D)
        q = jnp.transpose(qkv[:, :, 0], (0, 2, 1, 3))
        k = jnp.transpose(qkv[:, :, 1], (0, 2, 1, 3))
        v = jnp.transpose(qkv[:, :, 2], (0, 2, 1, 3))
        sin, cos = _rope_sin_cos(T, D)
        q = q * cos + _rotate_half(q) * sin
        k = k * cos + _rotate_half(k) * sin
        q = _rms_norm(q)
        k = _rms_norm(k)
        scale = 1.0 / jnp.sqrt(jnp.float32(D))
        scores = jnp.einsum('bhqd,bhkd->bhqk', q, k) * scale
        causal = jnp.tril(jnp.ones((T, T), dtype=bool))
        scores = jnp.where(causal[None, None], scores, jnp.float32(-1000000000.0))
        attn = jax.nn.softmax(scores, axis=-1)
        out = jnp.einsum('bhqk,bhkd->bhqd', attn, v)
        out = jnp.transpose(out, (0, 2, 1, 3)).reshape(B, T, C)
        return jnp.einsum('btc,oc->bto', out, W_o)

    def _L0_xattn_ref(q, kv, seg_id, W_kvc, W_dq, W_uq, W_qr, W_uk, W_kr, W_uv, W_o):
        import jax, jax.numpy as jnp
        import numpy as np
        B, Lq, Lk = (2, 512, 128)
        Q_DIM, KV_DIM = (256, 256)
        H, HD = (16, 128)
        KVC, QC, R = (64, 96, 64)
        LOOKBACK = 8
        NEG = -1e+30

        def _rope(x, L):
            half = x.shape[-1] // 2
            inv_freq = 1.0 / 10000.0 ** (jnp.arange(half, dtype=jnp.float32) / half)
            ang = jnp.arange(L, dtype=jnp.float32)[:, None] * inv_freq
            cos, sin = (jnp.cos(ang), jnp.sin(ang))
            x1, x2 = (x[..., :half], x[..., half:])
            return jnp.concatenate([x1 * cos - x2 * sin, x1 * sin + x2 * cos], axis=-1)
        b, lq, _ = q.shape
        lk = kv.shape[1]
        kv_c = kv @ W_kvc
        q_c = q @ W_dq
        q_nope = (q_c @ W_uq).reshape(b, lq, H, HD).transpose(0, 2, 1, 3)
        q_rope = (q_c @ W_qr).reshape(b, lq, H, R).transpose(0, 2, 1, 3)
        k_nope = (kv_c @ W_uk).reshape(b, lk, H, HD)
        v = (kv_c @ W_uv).reshape(b, lk, H, HD)
        k_rope = kv_c @ W_kr
        q_rope = _rope(q_rope, lq)
        k_rope = _rope(k_rope, lk)
        scale = 1.0 / np.sqrt(HD + R).astype(np.float32)
        scores = (jnp.einsum('bhqd,bkhd->bhqk', q_nope, k_nope) + jnp.einsum('bhqr,bkr->bhqk', q_rope, k_rope)) * scale
        k_ids = jnp.arange(lk)[None, None, :]
        qs = seg_id[:, :, None]
        good = (k_ids <= qs) & (k_ids >= qs - LOOKBACK)
        scores = jnp.where(good[:, None, :, :], scores, NEG)
        attn = jax.nn.softmax(scores, axis=-1)
        out = jnp.einsum('bhqk,bkhd->bqhd', attn, v).reshape(b, lq, H * HD)
        return out @ W_o

    def _L0_ffn_ref(hidden_states, gate_w, w_gate, w_up, w_down, sw_gate, sw_up, sw_down):
        import jax, jax.numpy as jnp
        import numpy as np
        B, S, H = (1, 256, 256)
        E, K, I = (16, 4, 176)
        IS = 352
        CAP = 128
        b, s, h = hidden_states.shape
        x = hidden_states.reshape(-1, h)
        T = x.shape[0]
        scores = jax.nn.softmax(x @ gate_w.T, axis=-1)
        topk_w, topk_i = jax.lax.top_k(scores, K)
        topk_w = topk_w / (topk_w.sum(-1, keepdims=True) + 1e-20)
        flat_i = topk_i.reshape(-1)
        flat_w = topk_w.reshape(-1)
        order = jnp.argsort(flat_i)
        se = flat_i[order]
        counts = jax.ops.segment_sum(jnp.ones_like(flat_i), flat_i, num_segments=E)
        starts = jnp.cumsum(counts) - counts
        rank = jnp.arange(T * K) - starts[se]
        tok = order // K
        slot = jnp.where(rank < CAP, rank, CAP)
        buf = jnp.full((E, CAP + 1), T, dtype=jnp.int32).at[se, slot].set(tok)[:, :CAP]
        wbuf = jnp.zeros((E, CAP + 1), x.dtype).at[se, slot].set(flat_w[order])[:, :CAP]
        xpad = jnp.concatenate([x, jnp.zeros((1, h), x.dtype)], axis=0)
        xg = xpad[buf]
        gact = jax.nn.silu(jnp.einsum('ech,ehi->eci', xg, w_gate))
        mid = gact * jnp.einsum('ech,ehi->eci', xg, w_up)
        eout = jnp.einsum('eci,eih->ech', mid, w_down) * wbuf[..., None]
        y = jnp.zeros((T + 1, h), x.dtype).at[buf.reshape(-1)].add(eout.reshape(-1, h))[:T]
        shared = jax.nn.silu(x @ sw_gate) * (x @ sw_up) @ sw_down
        return (y + shared).reshape(b, s, h)
    x = _layernorm(x + _L0_attn_ref(x, L0_attn_W_qkv, L0_attn_W_o), axis=-1)
    x = _layernorm(x + _L0_xattn_ref(x, ctx_2048, itok_BxS_0_1023, L0_xattn_W_kvc, L0_xattn_W_dq, L0_xattn_W_uq, L0_xattn_W_qr, L0_xattn_W_uk, L0_xattn_W_kr, L0_xattn_W_uv, L0_xattn_W_o), axis=-1)
    x = _layernorm(x + _L0_ffn_ref(x, L0_ffn_gate_w, L0_ffn_w_gate, L0_ffn_w_up, L0_ffn_w_down, L0_ffn_sw_gate, L0_ffn_sw_up, L0_ffn_sw_down), axis=-1)
    return x

_drawn_inputs = setup_inputs


def setup_inputs(seed=0):
    import zlib

    import numpy as np

    out = dict(_drawn_inputs(seed))
    spreads = {}
    factors = {'L0_ffn_gate_w': 8.0,
     'L0_ffn_w_gate': 8.0,
     'L0_ffn_w_up': 8.0,
     'L0_ffn_w_down': 8.0,
     'L0_ffn_sw_gate': 2.883,
     'L0_ffn_sw_up': 2.858,
     'L0_ffn_sw_down': 2.856}
    for name, (base, spread) in spreads.items():
        noise = np.random.default_rng([zlib.crc32(name.encode()), seed]).standard_normal(out[name].shape)
        drawn = base * np.exp(spread * noise) if base else spread * noise
        out[name] = jnp.asarray(drawn.astype(out[name].dtype))
    for name, factor in factors.items():
        out[name] = (out[name] * factor).astype(out[name].dtype)
    return out
```

```python
from contextlib import ExitStack

import numpy as np

import concourse.bass as bass
from concourse import mybir

ALU = mybir.AluOpType
ACT = mybir.ActivationFunctionType
AX = mybir.AxisListType
F32 = mybir.dt.float32
BF16 = mybir.dt.bfloat16
I32 = mybir.dt.int32
U32 = mybir.dt.uint32

P = 128
TILES, CM = 16, 256
CC = CM // P
H, HD = 16, 16
VW = HD + 1
KVC, QC, R = 64, 96, 64
XHD = 128
LOOKBACK = 8
NEG = -1e30
E, TOPK, EI, CAP = 16, 4, 176, 128
SI = 352
SH = SI // 2
ROWW = CM + E + 1
NTOK = TILES * P
SCALE_A = HD ** -0.5
SCALE_B = float(np.float32(1.0) / np.sqrt(XHD + R).astype(np.float32))
RMS_EPS = 1.1920929e-07
LN_EPS = 1e-5
NOSLOT = 4096
D_RING = 4


def layer(nc, io, y_out):
    ctx = ExitStack()
    with ctx:
        def sb(name, shape, dt=F32):
            return ctx.enter_context(nc.sbuf_tensor(name, shape, dt))

        def sem(name):
            return ctx.enter_context(nc.semaphore(name))

        slots_dram = nc.dram_tensor("slots_dram", (E * CAP, ROWW), F32, kind="Internal").ap()
        y_dram = nc.dram_tensor("y_dram", (NTOK + P, CM), F32, kind="Internal").ap()

        ident = sb("ident", [P, P])
        cos_a = sb("cos_a", [P, 2 * CM])
        sin_a = sb("sin_a", [P, 2 * CM])
        cos_b = sb("cos_b", [P, P])
        sin_b = sb("sin_b", [P, P])
        key_pos = sb("key_pos", [P, P])
        slot_base = sb("slot_base", [P, E])
        expert_no = sb("expert_no", [P, E])
        minus_half = sb("minus_half", [P, 2 * H])
        earlier = sb("earlier", [P, P], BF16)
        ones_bf = sb("ones_bf", [P, P], BF16)
        wqkv = sb("wqkv", [P, CC, 3 * CM])
        wo = sb("wo", [P, CC, CM])
        wkvc2 = sb("wkvc2", [P, CC, 2 * KVC])
        wdq = sb("wdq", [P, CC, QC])
        wkr2 = sb("wkr2", [KVC, 2, 2 * R])
        wqr = sb("wqr", [QC, 2, H * R])
        wqk = sb("wqk", [QC, H * KVC])
        wvo = sb("wvo", [P, H // 2, CM])
        wgate = sb("wgate", [P, CC, E])
        wsh = sb("wsh", [P, CC, 2 * SI])
        wshd = sb("wshd", [P, 3, CM])

        xT = sb("xT", [P, CC, P])
        x_in = sb("x_in", [P, CM])
        qk_cos = sb("qk_cos", [P, 2 * CM])
        qk_sin = sb("qk_sin", [P, 2 * CM])
        qk_rot = sb("qk_rot", [P, 2 * CM])
        qk_sq = sb("qk_sq", [P, 2 * CM])
        qk_ss = sb("qk_ss", [P, 2 * H])
        qk_ms = sb("qk_ms", [P, 2 * H])
        qk_rs = sb("qk_rs", [P, 2 * H])
        qk_pad = sb("qk_pad", [P, 2 * H, 32])
        v_a = sb("v_a", [P, H, VW])
        qT = sb("qT", [P, 4, P])
        kT = sb("kT", [P, 4, P])
        prob_a = sb("prob_a", [P, H, P])
        rec_a = sb("rec_a", [P, H])
        att_a = sb("att_a", [P, CM])
        att_aT = sb("att_aT", [P, CC, P])
        res_a = sb("res_a", [P, CM])
        x1 = sb("x1", [P, CM])

        ctxT = sb("ctxT", [P, CC, P])
        seg = sb("seg", [P, 1], I32)
        seg_f = sb("seg_f", [P, 1])
        mask_d = sb("mask_d", [P, P])
        mask_b = sb("mask_b", [P, P])
        x1_keep = sb("x1_keep", [P, CM])
        x1T = sb("x1T", [P, CC, P])
        kk_e = sb("kk_e", [P, P])
        kk_o = sb("kk_o", [P, P])
        kr_cos = sb("kr_cos", [P, P])
        kr_sin = sb("kr_sin", [P, P])
        qcT = sb("qcT", [QC, P])
        v_b = sb("v_b", [P, KVC])
        qr_cos = sb("qr_cos", [P, 2, 4 * P])
        qr_sin = sb("qr_sin", [P, 2, 4 * P])
        qq_e = sb("qq_e", [P, H // 2, P])
        qq_o = sb("qq_o", [P, H // 2, P])
        score_b = sb("score_b", [P, H, P])
        max_b = sb("max_b", [P, H])
        negmax_b = sb("negmax_b", [P, H])
        prob_b = sb("prob_b", [P, H, P])
        den_b = sb("den_b", [P, H])
        rec_b = sb("rec_b", [P, H])
        prob_bT = sb("prob_bT", [P, H, P])
        att_b = sb("att_b", [P, H * KVC])
        att_bT = sb("att_bT", [P, H // 2, P])
        res_b = sb("res_b", [P, CM])
        x2 = sb("x2", [P, CM])

        stats = {s: sb(f"stats_{s}", [P, 6]) for s in "abe"}
        mv = {s: sb(f"mv_{s}", [P, 2]) for s in "abe"}
        var_eps = {s: sb(f"var_eps_{s}", [P, 1]) for s in "abe"}
        rstd = {s: sb(f"rstd_{s}", [P, 1]) for s in "abe"}

        row = sb("row", [P, ROWW])
        x2T = sb("x2T", [P, CC, P])
        logit = sb("logit", [P, E])
        neg_top = sb("neg_top", [P, 1])
        gexp = sb("gexp", [P, E])
        gsum = sb("gsum", [P, 1])
        grec = sb("grec", [P, 1])
        gprob = sb("gprob", [P, E])
        top8 = sb("top8", [P, 8])
        top_no = sb("top_no", [P, 8], U32)
        top_nof = sb("top_nof", [P, 8])
        chosen = sb("chosen", [P, 2, E])
        chosen_bf = sb("chosen_bf", [P, E], BF16)
        seen_bf = sb("seen_bf", [P, E], BF16)
        wsel = sb("wsel", [P, E])
        wsum = sb("wsum", [P, 2])
        wrec = sb("wrec", [P, 1])
        slot_u = sb("slot_u", [P, E])
        slot_v = sb("slot_v", [P, E])
        slot_s = sb("slot_s", [P, E])
        slot8 = sb("slot8", [P, 8])
        slot_no = sb("slot_no", [P, 8], U32)
        sh_exp = sb("sh_exp", [P, 2, SH])
        sh_rec = sb("sh_rec", [P, 2, SH])
        sh_act = sb("sh_act", [P, 2, SH])
        sh_mid = sb("sh_mid", [P, SI])
        sh_midT = sb("sh_midT", [P, 3, P])
        y_sb = sb("y_sb", [P, CM])

        ew = sb("ew", [P, D_RING, CC, 2 * EI])
        ewd = sb("ewd", [EI // 2, D_RING, 2, CM])
        ex = sb("ex", [P, D_RING, ROWW])
        exT = sb("exT", [P, 2, CC, P])
        e_exp = sb("e_exp", [P, 2, EI])
        e_rec = sb("e_rec", [P, 2, EI])
        e_act = sb("e_act", [P, 2, EI])
        e_mid = sb("e_mid", [P, 2, EI])
        e_midT = sb("e_midT", [EI // 2, 2, 2, P])
        e_out = sb("e_out", [P, 2, CM])
        uqT = score_b[:, 0:12, :].rearrange("p a b -> p (a b)").rearrange("p (h q) -> p h q", q=QC)
        ukT = prob_b[:, 0:8, :].rearrange("p a b -> p (a b)").rearrange("p (h q) -> p h q", q=KVC)
        uvT = prob_b[:, 8:16, :].rearrange("p a b -> p (a b)").rearrange("p (h q) -> p h q", q=KVC)
        wox_lo = prob_bT[:, :, :].rearrange("p a b -> p (a b)").rearrange("p (h o) -> p h o", o=CM)
        wox_hi = prob_a[:, :, :].rearrange("p a b -> p (a b)").rearrange("p (h o) -> p h o", o=CM)

        empty_row = ex[:, 0, :]
        halves = [t[:, 8 * g:8 * g + 8, :].rearrange("p a b -> p (a b)")
                  for t in (score_b, prob_b, prob_bT, prob_a) for g in range(2)]
        fin_in, fin_out = halves[0:4], halves[4:8]
        fin_mv = sb("fin_mv", [P, 4, 2])
        fin_stats = sb("fin_stats", [P, 4, 6])
        fin_var = sb("fin_var", [P, 4])
        fin_rstd = sb("fin_rstd", [P, 4])

        bank = [ctx.enter_context(nc.psum_tensor(f"bank{i}", [P, 512], F32)) for i in range(8)]
        SA, SB, SC = bank[0:4], bank[4:7], bank[7]

        const_in = sem("const_in")
        waited = sem("waited")
        weights_in = sem("weights_in")
        setup_in = sem("setup_in")
        zeros_out = sem("zeros_out")
        dve_setup = sem("dve_setup")
        pool_zeros = sem("pool_zeros")
        empty_in = sem("empty_in")
        wqk_psum = sem("wqk_psum")
        wqk_sb = sem("wqk_sb")
        wvo_psum = sem("wvo_psum")
        wvo_sb = sem("wvo_sb")
        xT_in, x_in_s, ctxT_in, seg_in = sem("xT_in"), sem("x_in_s"), sem("ctxT_in"), sem("seg_in")
        (chain_a_rope, chain_a_att, chain_a_norm, chain_b_latent, chain_b_mask, chain_b_max, chain_b_att,
         chain_b_norm, chain_c_top, chain_c_choose, chain_c_slot, chain_c_mid, chain_d_mid, chain_e_norm) = (
            sem(f"chain_{n}") for n in ("a_rope", "a_att", "a_norm", "b_latent", "b_mask", "b_max", "b_att",
                                        "b_norm", "c_top", "c_choose", "c_slot", "c_mid", "d_mid", "e_norm"))
        chain_a_rs, chain_a_rstd, chain_b_rstd, chain_e_rstd, chain_seen = (
            sem(f"chain_{n}") for n in ("a_rs", "a_rstd", "b_rstd", "e_rstd", "seen"))
        a_qkv = sem("a_qkv")
        a_ss = sem("a_ss")
        a_v = sem("a_v")
        a_rs = sem("a_rs")
        a_qk = sem("a_qk")
        a_tr = sem("a_tr")
        a_qT = sem("a_qT")
        a_kT = sem("a_kT")
        a_score = sem("a_score")
        a_exp = sem("a_exp")
        a_masked = sem("a_masked")
        a_av = sem("a_av")
        a_att = sem("a_att")
        a_attT_psum = sem("a_attT_psum")
        a_attT = sem("a_attT")
        a_wo = sem("a_wo")
        a_res = sem("a_res")
        a_var = sem("a_var")
        a_rstd = sem("a_rstd")
        a_x1 = sem("a_x1")
        b_keep = sem("b_keep")
        b_in_psum = sem("b_in_psum")
        b_in = sem("b_in")
        b_qc_psum = sem("b_qc_psum")
        b_qc = sem("b_qc")
        b_q_psum = sem("b_q_psum")
        b_rot = sem("b_rot")
        b_rope = sem("b_rope")
        b_nope = sem("b_nope")
        b_mask = sem("b_mask")
        b_score_psum = sem("b_score_psum")
        b_score = sem("b_score")
        b_prob = sem("b_prob")
        b_pT_psum = sem("b_pT_psum")
        b_pT_act = sem("b_pT_act")
        b_pT_dve = sem("b_pT_dve")
        b_av = sem("b_av")
        b_att = sem("b_att")
        b_attT_psum = sem("b_attT_psum")
        b_attT = sem("b_attT")
        b_wo = sem("b_wo")
        b_res = sem("b_res")
        b_var = sem("b_var")
        b_rstd = sem("b_rstd")
        b_x2 = sem("b_x2")
        c_row = sem("c_row")
        c_xT_psum = sem("c_xT_psum")
        c_xT = sem("c_xT")
        c_logit_psum = sem("c_logit_psum")
        c_logit = sem("c_logit")
        c_top = sem("c_top")
        c_gexp = sem("c_gexp")
        c_chosen = sem("c_chosen")
        c_rank = sem("c_rank")
        c_slot = sem("c_slot")
        c_sent = sem("c_sent")
        c_gu_psum = sem("c_gu_psum")
        c_gexp2 = sem("c_gexp2")
        c_mid = sem("c_mid")
        c_midT_psum = sem("c_midT_psum")
        c_midT = sem("c_midT")
        c_down = sem("c_down")
        c_y = sem("c_y")
        y_out_s = sem("y_out_s")
        ew_in = [sem(f"ew_in{i}") for i in range(D_RING)]
        ex_in = [sem(f"ex_in{i}") for i in range(D_RING)]
        d_xT_psum, d_xT = sem("d_xT_psum"), sem("d_xT")
        d_gu_psum, d_exp, d_mid = sem("d_gu_psum"), sem("d_exp"), sem("d_mid")
        d_midT_psum, d_midT = sem("d_midT_psum"), sem("d_midT")
        d_down, d_out, d_added = sem("d_down"), sem("d_out"), sem("d_added")
        yl_in = [sem(f"yl_in{g}") for g in range(4)]
        e_var, e_rstd, e_done, final_out = sem("e_var"), sem("e_rstd"), sem("e_done"), sem("final_out")

        def at(eng, s, value):
            if not isinstance(value, int) or value > 0:
                eng.wait_ge(s, value)

        def link(eng, s, base):
            n = [0]

            def f(ins):
                n[0] += 1
                ins.then_inc(s, 1)
                eng.wait_ge(s, base + n[0])
            return f

        def two_ago(e, i, back):
            if isinstance(i, int):
                return e - 1
            return e - 1 if back <= 2 else e

        def alone(eng):
            eng.sem_inc(waited, 1)

        def run_steps(step, eng):
            step(0, None, None)
            step(1, 0, None)
            step(2, 1, 0)
            with eng.Fori(3, TILES) as i:
                step(i, i - 1, i - 2)
            step(None, TILES - 1, TILES - 2)
            step(None, None, TILES - 1)

        def run_experts(step, eng):
            for k in range(D_RING):
                step(0, k)
            with eng.Fori(1, E // D_RING) as i:
                for k in range(D_RING):
                    step(i, k)
            for k in range(3):
                step(E // D_RING, k)

        def have(i, k, n):
            if isinstance(i, int):
                return 0 <= D_RING * i + k - n < E
            return True

        block = ctx.enter_context(nc.Block())

        @block.sync
        def _(eng):
            for dst, name in ((ident, "ident"), (cos_a, "cos_a"), (sin_a, "sin_a"), (cos_b, "cos_b"),
                              (sin_b, "sin_b"), (key_pos, "key_pos"), (slot_base, "slot_base"),
                              (expert_no, "expert_no"), (earlier, "earlier")):
                eng.dma_start(dst[:, :], io[name]).then_inc(const_in, 16)
            eng.dma_start(row[:, ROWW - 1:ROWW].bitcast(I32), io["token_no"]).then_inc(const_in, 16)
            chunked = "(c p) n -> p c n"
            eng.dma_start(uqT, io["uqT"].rearrange("(h d) q -> d h q", d=XHD)).then_inc(setup_in, 16)
            eng.dma_start(ukT, io["ukT"].rearrange("(h d) q -> d h q", d=XHD)).then_inc(setup_in, 16)
            eng.dma_start(uvT, io["uvT"].rearrange("(h d) q -> d h q", d=XHD)).then_inc(setup_in, 16)
            xo = io["wox"].rearrange("(h d) o -> d h o", d=XHD)
            eng.dma_start(wox_lo, xo[:, 0:H // 2, :]).then_inc(setup_in, 16)
            eng.dma_start(wox_hi, xo[:, H // 2:H, :]).then_inc(setup_in, 16)
            for dst, name in ((wqkv, "wqkvT"), (wo, "woT"), (wkvc2, "wkvc2"), (wdq, "wdq"),
                              (wgate, "wgateT"), (wsh, "wsh")):
                eng.dma_start(dst[:, :, :], io[name].rearrange(chunked, p=P)).then_inc(weights_in, 16)
            eng.dma_start(wkr2[:, :, :], io["wkr2"].rearrange("p (a n) -> p a n", a=2)).then_inc(weights_in, 16)
            eng.dma_start(wqr[:, :, :], io["wqr"].rearrange("p (a n) -> p a n", a=2)).then_inc(weights_in, 16)
            eng.dma_start(wshd[:, 0:2, :], io["wshd"][0:2 * P, :].rearrange(chunked, p=P)).then_inc(weights_in, 16)
            eng.dma_start(wshd[0:SI - 2 * P, 2, :], io["wshd"][2 * P:SI, :]).then_inc(weights_in, 16)
            eng.wait_ge(pool_zeros, 1)
            eng.dma_start(empty_row[:, ROWW - 1:ROWW].bitcast(I32), io["empty_no"]).then_inc(empty_in, 16)
            eng.wait_ge(empty_in, 16)
            for e in range(E):
                eng.dma_start(slots_dram[e * CAP:(e + 1) * CAP, :], empty_row).then_inc(zeros_out, 16)
            eng.dma_start(y_dram[NTOK:NTOK + P, :], empty_row[:, 0:CM]).then_inc(zeros_out, 16)

            def load_expert(i, k):
                e = D_RING * i + k
                at(eng, d_gu_psum, e - D_RING + 1 if not isinstance(i, int) or i else 0)
                eng.dma_start(ew[:, k, :, :], io["ew"][bass.ds(e, 1), :, :].rearrange(
                    "e (c p) n -> p (e c) n", p=P)).then_inc(ew_in[k], 16)
                at(eng, d_down, e - D_RING + 1 if not isinstance(i, int) or i else 0)
                eng.dma_start(ewd[:, k, :, :], io["ewd"][bass.ds(e, 1), :, :].rearrange(
                    "e (c p) n -> p (e c) n", c=2)).then_inc(ew_in[k], 16)

            def load_slots(i, k):
                e = D_RING * i + k
                at(eng, d_added, 16 * (e - D_RING + 1) if not isinstance(i, int) or i else 0)
                eng.dma_start(ex[:, k, :], slots_dram[bass.ds(e * CAP, CAP), :]).then_inc(ex_in[k], 16)

            for k in range(D_RING):
                load_expert(0, k)

            def step(a, b, c):
                if a is not None:
                    at(eng, a_qkv, a)
                    eng.dma_start(xT[:, :, :], io["xT"][bass.ds(a, 1), :, :].rearrange(
                        "b (c p) s -> p (b c) s", p=P)).then_inc(xT_in, 16)
                if b is not None:
                    at(eng, b_in_psum, b)
                    eng.dma_start(ctxT[:, :, :], io["ctxT"][bass.ds(b, 1), :, :].rearrange(
                        "b (c p) s -> p (b c) s", p=P)).then_inc(ctxT_in, 16)
                    at(eng, b_mask, 2 * b)
                    eng.dma_start(seg[:, :], io["seg"][bass.ds(b, 1), :].rearrange("b s -> s b"))\
                       .then_inc(seg_in, 16)
                if a is not None:
                    at(eng, a_res, a)
                    eng.dma_start(x_in[:, :], io["x"][bass.ds(a, 1), :, :].rearrange("b s c -> (b s) c"))\
                       .then_inc(x_in_s, 16)
                if c is not None:
                    eng.wait_ge(c_y, c + 1)
                    eng.dma_start(y_dram[bass.ds(c * P, P), :], y_sb[:, :]).then_inc(y_out_s, 16)

            run_steps(step, eng)

            eng.wait_ge(c_sent, 16 * TOPK * TILES)
            eng.wait_ge(y_out_s, 16 * TILES)
            for k in range(D_RING):
                load_slots(0, k)
            with eng.Fori(1, E // D_RING) as i:
                for k in range(D_RING):
                    load_expert(i, k)
                    load_slots(i, k)

            eng.wait_ge(d_added, 16 * E)
            tokens = "(g p j) c -> g p (j c)"
            yv = y_dram[0:NTOK, :].rearrange(tokens, p=P, j=4)
            ov = y_out.rearrange("b s c -> (b s) c").rearrange(tokens, p=P, j=4)
            for g in range(4):
                eng.dma_start(fin_in[g], yv[g]).then_inc(yl_in[g], 16)
            for g in range(4):
                eng.wait_ge(e_done, g + 1)
                eng.dma_start(ov[g], fin_out[g]).then_inc(final_out, 16)
            eng.wait_ge(final_out, 16 * 4)

        @block.tensor
        def _(eng):
            def turn(out, in_):
                return eng.transpose(out, in_, ident[0:in_.shape[0], 0:in_.shape[0]])

            def a_project(t):
                eng.wait_ge(xT_in, 16 * (t + 1))
                at(eng, a_res, t)
                for c in range(CC):
                    eng.matmul(SA[0][:, :], xT[:, c, :], wqkv[:, c, 0:2 * CM], start=c == 0, stop=c == CC - 1)
                for c in range(CC):
                    mm = eng.matmul(SA[1][:, 0:CM], xT[:, c, :], wqkv[:, c, 2 * CM:3 * CM],
                                    start=c == 0, stop=c == CC - 1)
                mm.then_inc(a_qkv, 1)

            def a_turn(t):
                eng.wait_ge(a_qk, t + 1)
                at(eng, a_attT, t)
                for s in range(2):
                    for g in range(4):
                        heads = qk_pad[:, H * s + 4 * g:H * s + 4 * g + 4, :].rearrange("p h d -> p (h d)")
                        mm = turn(SA[2 + s][:, P * g:P * g + P], heads)
                    mm.then_inc(a_tr, 1)

            def a_scores(t):
                eng.wait_ge(a_qT, t + 1)
                eng.wait_ge(a_kT, t + 1)
                eng.wait_ge(a_v, t + 1)
                for g in range(4):
                    for j in range(4):
                        rows = slice(32 * j, 32 * j + HD)
                        mm = eng.matmul(SA[j][:, P * g:P * g + P], kT[rows, g, :], qT[rows, g, :],
                                        start=True, stop=True)
                mm.then_inc(a_score, 1)

            def a_values(t):
                for j in range(4):
                    eng.wait_ge(a_masked, 4 * t + j + 1)
                    for g in range(4):
                        h = 4 * g + j
                        mm = eng.matmul(SA[0][:, VW * h:VW * h + VW], prob_a[:, 4 * j + g, :], v_a[:, h, :],
                                        start=True, stop=True)
                mm.then_inc(a_av, 1)

            def a_turn_out(t):
                eng.wait_ge(a_att, t + 1)
                for c in range(CC):
                    mm = turn(SA[2][:, P * c:P * c + P], att_a[:, P * c:P * c + P])
                mm.then_inc(a_attT_psum, 1)

            def a_out(t):
                eng.wait_ge(a_attT, t + 1)
                for c in range(CC):
                    mm = eng.matmul(SA[1][:, 0:CM], att_aT[:, c, :], wo[:, c, :], start=c == 0, stop=c == CC - 1)
                mm.then_inc(a_wo, 1)

            def b_input(t):
                eng.wait_ge(a_x1, t + 1)
                eng.wait_ge(ctxT_in, 16 * (t + 1))
                at(eng, b_attT, 2 * t)
                for c in range(CC):
                    turn(SB[0][:, P * c:P * c + P], x1[:, P * c:P * c + P])
                for c in range(CC):
                    mm = eng.matmul(SB[0][:, CM:CM + P], wkvc2[:, c, :], ctxT[:, c, :],
                                    start=c == 0, stop=c == CC - 1)
                mm.then_inc(b_in_psum, 1)

            def b_latent(t):
                eng.wait_ge(b_in, t + 1)
                at(eng, b_attT, 2 * t)
                for c in range(CC):
                    eng.matmul(SB[1][0:QC, 0:P], wdq[:, c, :], x1T[:, c, :], start=c == 0, stop=c == CC - 1)
                for s in range(2):
                    eng.matmul(SB[1][:, P * (1 + s):P * (2 + s)], wkr2[:, s, :], kk_e[0:KVC, :],
                               start=True, stop=True)
                turn(SB[1][:, 3 * P:3 * P + KVC], kk_e[0:KVC, :]).then_inc(b_qc_psum, 1)

            def b_queries(t, half):
                eng.wait_ge(b_qc, t + 1)
                for use, bk in enumerate((SB[2], SB[0], SB[1])):
                    if use == 0:
                        at(eng, b_res, t) if half == 0 else eng.wait_ge(b_rot, 4 * t + 1)
                    elif use == 1:
                        if half == 1:
                            eng.wait_ge(b_rot, 4 * t + 2)
                    elif half == 1:
                        eng.wait_ge(b_nope, 2 * t + 1)
                    for j in range(4):
                        pair = slice(P * (4 * half + j), P * (4 * half + j) + P)
                        w = wqk[:, pair] if use == 2 else wqr[:, use, pair]
                        mm = eng.matmul(bk[:, P * j:P * j + P], w, qcT[:, :], start=True, stop=True)
                    mm.then_inc(b_q_psum, 1)

            def b_bank(use):
                return SB[(2 + use) % 3]

            def b_scores(t, g):
                if g == 0:
                    eng.wait_ge(b_rope, 4 * t + 2)
                    eng.wait_ge(b_nope, 2 * t + 1)
                    eng.wait_ge(b_rot, 4 * t + 3)
                elif g == 1:
                    eng.wait_ge(b_rot, 4 * t + 4)
                elif g == 2:
                    eng.wait_ge(b_rope, 4 * t + 4)
                    eng.wait_ge(b_nope, 2 * t + 2)
                else:
                    eng.wait_ge(b_score, 4 * t + 1)
                for j in range(4):
                    h = 4 * g + j
                    qq, kk = (qq_e, kk_e) if h % 2 == 0 else (qq_o, kk_o)
                    mm = eng.matmul(b_bank(g)[:, P * j:P * j + P], qq[:, h // 2, :], kk[:, :],
                                    start=True, stop=True)
                mm.then_inc(b_score_psum, 1)

            def b_turn(t, g):
                eng.wait_ge(b_prob, 4 * t + g + 1)
                eng.wait_ge(b_score, 4 * t + min(g + 2, 4))
                if g == 3:
                    eng.wait_ge(b_pT_act, 2 * t + 1)
                for j in range(4):
                    mm = turn(b_bank(4 + g)[:, P * j:P * j + P], prob_b[:, 4 * g + j, :])
                mm.then_inc(b_pT_psum, 1)

            def b_values(t, half):
                eng.wait_ge(b_pT_act, 2 * t + half + 1)
                eng.wait_ge(b_pT_dve, 2 * t + half + 1)
                bk = SB[1 + half]
                for j in range(8):
                    mm = eng.matmul(bk[:, KVC * j:KVC * j + KVC], prob_bT[:, 8 * half + j, :], v_b[:, :],
                                    start=True, stop=True)
                mm.then_inc(b_av, 1)

            def b_turn_out(t, half):
                eng.wait_ge(b_att, 2 * t + half + 1)
                bk = SB[half]
                for j in range(4):
                    mm = turn(bk[:, P * j:P * j + P], att_b[:, P * (4 * half + j):P * (4 * half + j) + P])
                mm.then_inc(b_attT_psum, 1)

            def b_out(t):
                eng.wait_ge(b_attT, 2 * t + 2)
                eng.wait_ge(b_att, 2 * t + 2)
                for j in range(H // 2):
                    mm = eng.matmul(SB[2][:, 0:CM], att_bT[:, j, :], wvo[:, j, :],
                                    start=j == 0, stop=j == H // 2 - 1)
                mm.then_inc(b_wo, 1)

            def c_turn(t):
                eng.wait_ge(b_x2, t + 1)
                at(eng, c_y, t)
                for c in range(CC):
                    mm = turn(SC[:, P * c:P * c + P], x2[:, P * c:P * c + P])
                mm.then_inc(c_xT_psum, 1)

            def c_router(t):
                eng.wait_ge(c_xT, t + 1)
                for c in range(CC):
                    mm = eng.matmul(SC[:, 0:E], x2T[:, c, :], wgate[:, c, :], start=c == 0, stop=c == CC - 1)
                mm.then_inc(c_logit_psum, 1)

            def c_up(t, half):
                if half == 0:
                    eng.wait_ge(c_logit, t + 1)
                else:
                    eng.wait_ge(c_mid, 2 * t + 1)
                for c in range(CC):
                    mm = eng.matmul(SC[:, 0:2 * SH], x2T[:, c, :], wsh[:, c, 2 * SH * half:2 * SH * (half + 1)],
                                    start=c == 0, stop=c == CC - 1)
                mm.then_inc(c_gu_psum, 1)

            def c_ranks(t):
                eng.wait_ge(c_chosen, t + 1)
                eng.wait_ge(c_mid, 2 * t + 2)
                eng.matmul(SC[:, 0:E], earlier[:, :], chosen_bf[:, :], start=True, stop=False)
                eng.matmul(SC[:, 0:E], ones_bf[:, :], seen_bf[:, :], start=False, stop=True).then_inc(c_rank, 1)

            def c_turn_mid(t):
                eng.wait_ge(c_slot, t + 1)
                for c in range(3):
                    n = min(P, SI - P * c)
                    mm = turn(SC[0:n, P * c:P * c + P], sh_mid[:, P * c:P * c + n])
                mm.then_inc(c_midT_psum, 1)

            def c_out(t):
                eng.wait_ge(c_midT, t + 1)
                for c in range(3):
                    n = min(P, SI - P * c)
                    mm = eng.matmul(SC[:, 0:CM], sh_midT[0:n, c, :], wshd[0:n, c, :], start=c == 0, stop=c == 2)
                mm.then_inc(c_down, 1)

            eng.wait_ge(setup_in, 16 * 5)
            for h in range(H):
                mm = eng.matmul(bank[h // 8][0:QC, KVC * (h % 8):KVC * (h % 8) + KVC], uqT[:, h, :], ukT[:, h, :],
                                start=True, stop=True)
                if h % 8 == 7:
                    mm.then_inc(wqk_psum, 1)
            for h in range(H):
                j, odd = h // 2, h % 2
                wox = wox_lo if h < H // 2 else wox_hi
                mm = eng.matmul(bank[2 + j // 2][KVC * odd:KVC * odd + KVC, CM * (j % 2):CM * (j % 2) + CM],
                                uvT[:, h, :], wox[:, h % (H // 2), :], start=True, stop=True)
                if h % 4 == 3:
                    mm.then_inc(wvo_psum, 1)
            eng.wait_ge(const_in, 16 * 10)
            eng.wait_ge(weights_in, 16 * 10)
            eng.wait_ge(wqk_sb, 2)
            eng.wait_ge(wvo_sb, 4)

            def step(a, b, c):
                if a is not None:
                    a_project(a)
                if b is not None:
                    b_input(b)
                if c is not None:
                    c_turn(c)
                if b is not None:
                    b_latent(b)
                if c is not None:
                    c_router(c)
                if b is not None:
                    b_queries(b, 0)
                if c is not None:
                    c_up(c, 0)
                if b is not None:
                    b_queries(b, 1)
                if a is not None:
                    a_turn(a)
                if b is not None:
                    b_scores(b, 0)
                    b_scores(b, 1)
                if a is not None:
                    a_scores(a)
                if c is not None:
                    c_up(c, 1)
                if b is not None:
                    b_scores(b, 2)
                    b_scores(b, 3)
                    b_turn(b, 0)
                    b_turn(b, 1)
                if a is not None:
                    a_values(a)
                if b is not None:
                    b_turn(b, 2)
                    b_turn(b, 3)
                if c is not None:
                    c_ranks(c)
                if b is not None:
                    b_values(b, 0)
                if a is not None:
                    a_turn_out(a)
                if b is not None:
                    b_values(b, 1)
                if c is not None:
                    c_turn_mid(c)
                if a is not None:
                    a_out(a)
                if b is not None:
                    b_turn_out(b, 0)
                    b_turn_out(b, 1)
                if c is not None:
                    c_out(c)
                if b is not None:
                    b_out(b)

            run_steps(step, eng)

            def expert(i, k):
                if have(i, k, 0):
                    e = D_RING * i + k
                    eng.wait_ge(ex_in[k], 16 * (i + 1))
                    at(eng, d_xT, two_ago(e, i, 0))
                    for c in range(CC):
                        mm = turn(bank[k % 2][:, P * c:P * c + P], ex[:, k, P * c:P * c + P])
                    mm.then_inc(d_xT_psum, 1)
                if have(i, k, 1):
                    e, s = D_RING * i + k - 1, (k - 1) % D_RING
                    eng.wait_ge(ew_in[s], 16 * 2 * (i + 1 if k >= 1 else i))
                    eng.wait_ge(d_xT, e + 1)
                    at(eng, d_mid, two_ago(e, i, 1 - k))
                    for c in range(CC):
                        mm = eng.matmul(bank[2 + s % 2][:, 0:2 * EI], exT[:, s % 2, c, :], ew[:, s, c, :],
                                        start=c == 0, stop=c == CC - 1)
                    mm.then_inc(d_gu_psum, 1)
                if have(i, k, 2):
                    e, s = D_RING * i + k - 2, (k - 2) % D_RING
                    eng.wait_ge(d_mid, e + 1)
                    at(eng, d_midT, two_ago(e, i, 2 - k))
                    for c in range(2):
                        mm = turn(bank[4 + s % 2][0:EI // 2, P * c:P * c + P],
                                  e_mid[:, s % 2, EI // 2 * c:EI // 2 * (c + 1)])
                    mm.then_inc(d_midT_psum, 1)
                if have(i, k, 3):
                    e, s = D_RING * i + k - 3, (k - 3) % D_RING
                    eng.wait_ge(d_midT, e + 1)
                    at(eng, d_out, two_ago(e, i, 3 - k))
                    for c in range(2):
                        mm = eng.matmul(bank[6 + s % 2][:, 0:CM], e_midT[:, s % 2, c, :], ewd[:, s, c, :],
                                        start=c == 0, stop=c == 1)
                    mm.then_inc(d_down, 1)

            eng.wait_ge(c_y, TILES)
            run_experts(expert, eng)

        @block.scalar
        def _(eng):
            def a_value_copy(t):
                eng.wait_ge(a_qkv, t + 1)
                at(eng, a_av, t)
                eng.activation(v_a[:, :, 0:HD], SA[1][:, 0:CM].rearrange("p (h d) -> p h d", d=HD),
                               ACT.Copy).then_inc(a_v, 1)

            def a_q_copy(t):
                eng.wait_ge(a_tr, 2 * t + 1)
                at(eng, a_score, t)
                eng.activation(qT[:, :, :], SA[2][:, :].rearrange("p (g q) -> p g q", q=P),
                               ACT.Copy).then_inc(a_qT, 1)

            def a_exps(t):
                eng.wait_ge(a_score, t + 1)
                at(eng, a_av, t)
                for j in range(4):
                    eng.activation(prob_a[:, 4 * j:4 * j + 4, :], SA[j][:, :].rearrange("p (g q) -> p g q", q=P),
                                   ACT.Exp, scale=SCALE_A).then_inc(a_exp, 1)

            def a_att_copy(t):
                eng.wait_ge(a_attT_psum, t + 1)
                at(eng, a_wo, t)
                eng.activation(att_aT[:, :, :], SA[2][:, 0:CM].rearrange("p (c q) -> p c q", q=P),
                               ACT.Copy).then_inc(a_attT, 1)

            def b_input_copy(t):
                eng.wait_ge(b_in_psum, t + 1)
                at(eng, b_qc_psum, t)
                at(eng, b_score_psum, 4 * t)
                eng.activation(x1T[:, :, :], SB[0][:, 0:CM].rearrange("p (c q) -> p c q", q=P), ACT.Copy)
                eng.activation(kk_e[0:KVC, :], SB[0][0:KVC, CM:CM + P], ACT.Copy)
                eng.activation(kk_o[KVC:2 * KVC, :], SB[0][KVC:2 * KVC, CM:CM + P], ACT.Copy).then_inc(b_in, 1)

            def b_nope_copy(t, half):
                eng.wait_ge(b_q_psum, 6 * t + 3 * half + 3)
                at(eng, b_score_psum, 4 * t)
                src = SB[1][:, :].rearrange("p (j q) -> p j q", q=P)
                eng.activation(qq_e[0:KVC, 4 * half:4 * half + 4, :], src[0:KVC], ACT.Copy)
                eng.activation(qq_o[KVC:2 * KVC, 4 * half:4 * half + 4, :], src[KVC:2 * KVC],
                               ACT.Copy).then_inc(b_nope, 1)

            def b_exps(t, g):
                eng.wait_ge(b_score, 4 * t + g + 1)
                at(eng, b_pT_psum, 4 * t)
                at(eng, b_att, 2 * t)
                for j in range(4):
                    h = 4 * g + j
                    ins = eng.activation(prob_b[:, h, :], score_b[:, h, :], ACT.Exp, bias=negmax_b[:, h:h + 1],
                                         accum_out=den_b[:, h:h + 1])
                ins.then_inc(b_prob, 1)

            def b_prob_copy(t, g):
                eng.wait_ge(b_pT_psum, 4 * t + g + 1)
                at(eng, b_av, 2 * t)
                eng.activation(prob_bT[:, 4 * g:4 * g + 4, :], SB[(4 + g + 2) % 3][:, :].rearrange(
                    "p (j q) -> p j q", q=P), ACT.Copy).then_inc(b_pT_act, 1)

            def b_att_copy(t, half):
                eng.wait_ge(b_attT_psum, 2 * t + half + 1)
                at(eng, b_wo, t)
                eng.activation(att_bT[:, 4 * half:4 * half + 4, :], SB[half][:, :].rearrange(
                    "p (j q) -> p j q", q=P), ACT.Copy).then_inc(b_attT, 1)

            def c_input_copy(t):
                eng.wait_ge(b_x2, t + 1)
                at(eng, c_sent, 16 * TOPK * t)
                at(eng, c_y, t)
                eng.activation(row[:, 0:CM], x2[:, :], ACT.Copy).then_inc(c_row, 1)
                eng.wait_ge(c_xT_psum, t + 1)
                at(eng, c_gu_psum, 2 * t)
                eng.activation(x2T[:, :, :], SC[:, 0:CM].rearrange("p (c q) -> p c q", q=P),
                               ACT.Copy).then_inc(c_xT, 1)

            def c_router_exp(t):
                eng.wait_ge(c_logit, t + 1)
                eng.wait_ge(c_top, t + 1)
                eng.activation(gexp[:, :], logit[:, :], ACT.Exp, bias=neg_top[:, :],
                               accum_out=gsum[:, :]).then_inc(c_gexp, 1)

            def c_gate_exp(t, half):
                eng.wait_ge(c_gu_psum, 2 * t + half + 1)
                at(eng, c_mid, 2 * t)
                eng.activation(sh_exp[:, half, :], SC[:, 0:SH], ACT.Exp, scale=-1.0).then_inc(c_gexp2, 1)

            def c_mid_copy(t):
                eng.wait_ge(c_midT_psum, t + 1)
                at(eng, c_down, t)
                eng.activation(sh_midT[:, 0:2, :], SC[:, 0:2 * P].rearrange("p (c q) -> p c q", q=P), ACT.Copy)
                eng.activation(sh_midT[0:SI - 2 * P, 2, :], SC[0:SI - 2 * P, 2 * P:3 * P],
                               ACT.Copy).then_inc(c_midT, 1)

            eng.wait_ge(dve_setup, 4)
            for b in range(2):
                eng.wait_ge(wqk_psum, b + 1)
                eng.activation(wqk[:, 512 * b:512 * b + 512], bank[b][0:QC, :], ACT.Copy).then_inc(wqk_sb, 1)
            for b in range(4):
                eng.wait_ge(wvo_psum, b + 1)
                eng.activation(wvo[:, 2 * b:2 * b + 2, :], bank[2 + b][:, :].rearrange("p (j o) -> p j o", o=CM),
                               ACT.Copy).then_inc(wvo_sb, 1)

            def step(a, b, c):
                if a is not None:
                    a_value_copy(a)
                if b is not None:
                    b_input_copy(b)
                if c is not None:
                    c_input_copy(c)
                    c_router_exp(c)
                if b is not None:
                    b_nope_copy(b, 0)
                if c is not None:
                    c_gate_exp(c, 0)
                if b is not None:
                    b_nope_copy(b, 1)
                if a is not None:
                    a_q_copy(a)
                if b is not None:
                    b_exps(b, 0)
                    b_exps(b, 1)
                if a is not None:
                    a_exps(a)
                if c is not None:
                    c_gate_exp(c, 1)
                if b is not None:
                    b_exps(b, 2)
                    b_exps(b, 3)
                    b_prob_copy(b, 0)
                    b_prob_copy(b, 2)
                if a is not None:
                    a_att_copy(a)
                if c is not None:
                    c_mid_copy(c)
                if b is not None:
                    b_att_copy(b, 0)
                    b_att_copy(b, 1)

            run_steps(step, eng)

            def expert(i, k):
                if have(i, k, 0):
                    e = D_RING * i + k
                    eng.wait_ge(d_xT_psum, e + 1)
                    at(eng, d_gu_psum, two_ago(e, i, 0))
                    eng.activation(exT[:, k % 2, :, :], bank[k % 2][:, 0:CM].rearrange("p (c q) -> p c q", q=P),
                                   ACT.Copy).then_inc(d_xT, 1)
                if have(i, k, 1):
                    e, s = D_RING * i + k - 1, (k - 1) % D_RING
                    eng.wait_ge(d_gu_psum, e + 1)
                    at(eng, d_mid, two_ago(e, i, 1 - k))
                    eng.activation(e_exp[:, s % 2, :], bank[2 + s % 2][:, 0:EI], ACT.Exp, scale=-1.0)\
                       .then_inc(d_exp, 1)
                if have(i, k, 2):
                    e, s = D_RING * i + k - 2, (k - 2) % D_RING
                    eng.wait_ge(d_midT_psum, e + 1)
                    at(eng, d_down, two_ago(e, i, 2 - k))
                    eng.activation(e_midT[:, s % 2, :, :], bank[4 + s % 2][0:EI // 2, 0:2 * P].rearrange(
                        "p (c q) -> p c q", q=P), ACT.Copy).then_inc(d_midT, 1)

            run_experts(expert, eng)

        @block.vector
        def _(eng):
            def a_rope(t):
                eng.wait_ge(a_qkv, t + 1)
                then = link(eng, chain_a_rope, 3 * t)
                pairs = "p (i two) -> p i two"
                eng.tensor_tensor(qk_cos[:, :], SA[0][:, :], cos_a[:, :], ALU.mult)
                src = SA[0][:, :].rearrange(pairs, two=2)
                dst = qk_sin[:, :].rearrange(pairs, two=2)
                tab = sin_a[:, :].rearrange(pairs, two=2)
                eng.tensor_tensor(dst[:, :, 0:1], src[:, :, 1:2], tab[:, :, 0:1], ALU.mult)
                then(eng.tensor_tensor(dst[:, :, 1:2], src[:, :, 0:1], tab[:, :, 1:2], ALU.mult))
                then(eng.tensor_tensor(qk_rot[:, :], qk_cos[:, :], qk_sin[:, :], ALU.add))
                then(eng.tensor_tensor(qk_sq[:, :], qk_rot[:, :], qk_rot[:, :], ALU.mult))
                at(eng, a_rs, t)
                eng.tensor_reduce(qk_ss[:, :], qk_sq[:, :].rearrange("p (i d) -> p i d", d=HD), AX.X, ALU.add)\
                   .then_inc(a_ss, 1)

            def a_scale(t):
                eng.wait_ge(a_rs, t + 1)
                at(eng, a_tr, 2 * t)
                eng.tensor_tensor(qk_pad[:, :, 0:HD], qk_rot[:, :].rearrange("p (i d) -> p i d", d=HD),
                                  qk_rs[:, :, None].to_broadcast([P, 2 * H, HD]), ALU.mult).then_inc(a_qk, 1)

            def a_k_copy(t):
                eng.wait_ge(a_tr, 2 * t + 2)
                at(eng, a_score, t)
                eng.tensor_copy(kT[:, :, :], SA[3][:, :].rearrange("p (g q) -> p g q", q=P)).then_inc(a_kT, 1)

            def a_normalise(t):
                eng.wait_ge(a_av, t + 1)
                then = link(eng, chain_a_att, t)
                heads = SA[0][:, 0:H * VW].rearrange("p (h d) -> p h d", d=VW)
                then(eng.reciprocal(rec_a[:, :, None], heads[:, :, HD:VW]))
                at(eng, a_attT_psum, t)
                eng.tensor_tensor(att_a[:, :].rearrange("p (h d) -> p h d", d=HD), heads[:, :, 0:HD],
                                  rec_a[:, :, None].to_broadcast([P, H, HD]), ALU.mult).then_inc(a_att, 1)

            def norm(which, res, out, then, var_s, rstd_s, t, done_s):
                then(eng.bn_stats(stats[which][:, :], res[:, :]))
                alone(eng)
                eng.bn_aggr(mv[which][:, :], stats[which][:, :]).then_inc(var_s, 1)
                eng.wait_ge(rstd_s, t + 1)
                eng.tensor_scalar(out[:, :], res[:, :], mv[which][:, 0:1], rstd[which][:, :],
                                  ALU.subtract, ALU.mult).then_inc(done_s, 1)

            def a_residual(t):
                eng.wait_ge(a_wo, t + 1)
                eng.wait_ge(x_in_s, 16 * (t + 1))
                eng.tensor_tensor(res_a[:, :], SA[1][:, 0:CM], x_in[:, :], ALU.add).then_inc(a_res, 1)
                eng.wait_ge(a_res, t + 1)
                at(eng, b_keep, t)
                at(eng, b_in_psum, t)
                norm("a", res_a, x1, link(eng, chain_a_norm, t), a_var, a_rstd, t, a_x1)

            def b_latent_copy(t):
                eng.wait_ge(b_qc_psum, t + 1)
                at(eng, b_q_psum, 6 * t)
                at(eng, b_av, 2 * t)
                at(eng, b_score_psum, 4 * t)
                then = link(eng, chain_b_latent, t)
                eng.tensor_copy(qcT[:, :], SB[1][0:QC, 0:P])
                eng.tensor_copy(v_b[:, :], SB[1][:, 3 * P:3 * P + KVC])
                eng.tensor_tensor(kr_cos[:, :], SB[1][:, P:2 * P], cos_b[:, :], ALU.mult)
                then(eng.tensor_tensor(kr_sin[:, :], SB[1][:, 2 * P:3 * P], sin_b[:, :], ALU.mult))
                eng.tensor_tensor(kk_e[R:2 * R, :], kr_cos[R:2 * R, :], kr_sin[R:2 * R, :], ALU.add)
                eng.tensor_tensor(kk_o[0:R, :], kr_cos[0:R, :], kr_sin[0:R, :], ALU.add).then_inc(b_qc, 1)

            def b_rotate(t, half):
                at(eng, b_rope, 4 * t)
                for use, dst, tab, bk in ((0, qr_cos, cos_b, SB[2]), (1, qr_sin, sin_b, SB[0])):
                    eng.wait_ge(b_q_psum, 6 * t + 3 * half + use + 1)
                    eng.tensor_tensor(dst[:, half, :].rearrange("p (j q) -> p j q", q=P),
                                      bk[:, :].rearrange("p (j q) -> p j q", q=P),
                                      tab[:, None, :].to_broadcast([P, 4, P]), ALU.mult).then_inc(b_rot, 1)

                eng.wait_ge(b_rot, 4 * t + 2 * half + 2)
                at(eng, b_score_psum, 4 * t)
                for dst, rows in ((qq_e, slice(R, 2 * R)), (qq_o, slice(0, R))):
                    eng.tensor_tensor(dst[rows, 4 * half:4 * half + 4, :].rearrange("p j q -> p (j q)"),
                                      qr_cos[rows, half, :], qr_sin[rows, half, :], ALU.add).then_inc(b_rope, 1)

            def b_window(t):
                eng.wait_ge(seg_in, 16 * (t + 1))
                at(eng, b_score, 4 * t)
                then = link(eng, chain_b_mask, 3 * t)
                then(eng.tensor_copy(seg_f[:, :], seg[:, :]))
                then(eng.tensor_scalar(mask_d[:, :], key_pos[:, :], seg_f[:, :], None, ALU.subtract))
                then(eng.tensor_scalar(mask_b[:, :], mask_d[:, :], 0.0, NEG, ALU.is_gt, ALU.mult))
                eng.tensor_scalar(mask_d[:, :], mask_d[:, :], -float(LOOKBACK), NEG, ALU.is_lt, ALU.mult)\
                   .then_inc(b_mask, 1)
                eng.wait_ge(b_mask, 2 * t + 1)
                eng.tensor_tensor(mask_b[:, :], mask_b[:, :], mask_d[:, :], ALU.add).then_inc(b_mask, 1)
                eng.wait_ge(b_mask, 2 * t + 2)

            def b_maxima(t, g):
                eng.wait_ge(b_score_psum, 4 * t + g + 1)
                at(eng, b_prob, 4 * t)
                then = link(eng, chain_b_max, 4 * t + g)
                alone(eng)
                for j in range(4):
                    h = 4 * g + j
                    ins = eng.tensor_tensor_reduce(score_b[:, h, :], SB[(2 + g) % 3][:, P * j:P * j + P],
                                                   mask_b[:, :], SCALE_B, -3.0e38, ALU.add, ALU.max,
                                                   max_b[:, h:h + 1])
                then(ins)
                eng.tensor_scalar(negmax_b[:, 4 * g:4 * g + 4], max_b[:, 4 * g:4 * g + 4], -1.0, None,
                                  ALU.mult).then_inc(b_score, 1)

            def b_prob_copy(t, g):
                eng.wait_ge(b_pT_psum, 4 * t + g + 1)
                at(eng, b_av, 2 * t)
                eng.tensor_copy(prob_bT[:, 4 * g:4 * g + 4, :], SB[(4 + g + 2) % 3][:, :].rearrange(
                    "p (j q) -> p j q", q=P)).then_inc(b_pT_dve, 1)

            def b_normalise(t, half):
                eng.wait_ge(b_av, 2 * t + half + 1)
                if half == 0:
                    then = link(eng, chain_b_att, t)
                    then(eng.reciprocal(rec_b[:, :], den_b[:, :]))
                    at(eng, b_attT_psum, 2 * t)
                eng.tensor_tensor(att_b[:, 512 * half:512 * half + 512].rearrange("p (h d) -> p h d", d=KVC),
                                  SB[1 + half][:, :].rearrange("p (h d) -> p h d", d=KVC),
                                  rec_b[:, 8 * half:8 * half + 8, None].to_broadcast([P, 8, KVC]),
                                  ALU.mult).then_inc(b_att, 1)

            def b_residual(t):
                eng.wait_ge(b_wo, t + 1)
                eng.wait_ge(b_keep, t + 1)
                eng.tensor_tensor(res_b[:, :], SB[2][:, 0:CM], x1_keep[:, :], ALU.add).then_inc(b_res, 1)
                eng.wait_ge(b_res, t + 1)
                at(eng, c_row, t)
                at(eng, c_xT_psum, t)
                norm("b", res_b, x2, link(eng, chain_b_norm, t), b_var, b_rstd, t, b_x2)

            def c_logits(t):
                eng.wait_ge(c_logit_psum, t + 1)
                at(eng, c_gexp, t)
                eng.tensor_copy(logit[:, :], SC[:, 0:E]).then_inc(c_logit, 1)
                eng.wait_ge(c_logit, t + 1)
                eng.tensor_reduce(neg_top[:, :], logit[:, :], AX.X, ALU.max, negate=True).then_inc(c_top, 1)

            def c_choose(t):
                eng.wait_ge(c_gexp, t + 1)
                then = link(eng, chain_c_choose, 14 * t)
                then(eng.reciprocal(grec[:, :], gsum[:, :]))
                then(eng.tensor_scalar(gprob[:, :], gexp[:, :], grec[:, :], None, ALU.mult))
                alone(eng)
                then(eng.max(top8[:, :], gprob[:, :]))
                alone(eng)
                then(eng.max_index(top_no[:, :], top8[:, :], gprob[:, :]))
                then(eng.tensor_copy(top_nof[:, :], top_no[:, :]))
                then(eng.tensor_scalar(chosen[:, 0, :], expert_no[:, :], top_nof[:, 0:1], None, ALU.is_equal))
                for k in range(1, TOPK):
                    then(eng.scalar_tensor_tensor(chosen[:, k % 2, :], expert_no[:, :], top_nof[:, k:k + 1],
                                                  chosen[:, (k - 1) % 2, :], ALU.is_equal, ALU.add))
                mask = chosen[:, (TOPK - 1) % 2, :]
                at(eng, c_rank, t)
                eng.tensor_copy(chosen_bf[:, :], mask).then_inc(c_chosen, 1)
                then(eng.tensor_tensor(wsel[:, :], gprob[:, :], mask, ALU.mult))
                then(eng.tensor_reduce(wsum[:, 0:1], wsel[:, :], AX.X, ALU.add))
                then(eng.tensor_scalar(wsum[:, 1:2], wsum[:, 0:1], 1e-20, None, ALU.add))
                then(eng.reciprocal(wrec[:, :], wsum[:, 1:2]))
                at(eng, c_sent, 16 * TOPK * t)
                then(eng.tensor_scalar(row[:, CM:CM + E], wsel[:, :], wrec[:, :], None, ALU.mult))
                eng.tensor_scalar(row[:, ROWW - 1:ROWW].bitcast(I32), row[:, ROWW - 1:ROWW].bitcast(I32),
                                  float(P), None, ALU.add).then_inc(c_row, 1)

            def c_slots(t):
                eng.wait_ge(c_rank, t + 1)
                then = link(eng, chain_c_slot, 3 * t)
                eng.tensor_tensor(slot_u[:, :], slot_base[:, :], SC[:, 0:E], ALU.subtract)
                then(eng.scalar_tensor_tensor(slot_v[:, :], SC[:, 0:E], float(CAP), chosen[:, (TOPK - 1) % 2, :],
                                              ALU.is_lt, ALU.mult))
                eng.tensor_tensor(seen_bf[:, :], seen_bf[:, :], chosen_bf[:, :], ALU.add)
                then(eng.tensor_tensor(slot_s[:, :], slot_u[:, :], slot_v[:, :], ALU.mult))
                alone(eng)
                then(eng.max(slot8[:, :], slot_s[:, :]))
                at(eng, c_sent, 16 * TOPK * t)
                eng.tensor_scalar(slot_no[:, :], slot8[:, :], -1.0, float(NOSLOT), ALU.mult, ALU.add)\
                   .then_inc(c_slot, 1)

            def c_middle(t, half):
                eng.wait_ge(c_gexp2, 2 * t + half + 1)
                then = link(eng, chain_c_mid, 3 * (2 * t + half))
                then(eng.tensor_scalar(sh_rec[:, half, :], sh_exp[:, half, :], 1.0, None, ALU.add))
                then(eng.reciprocal(sh_act[:, half, :], sh_rec[:, half, :]))
                then(eng.tensor_tensor(sh_rec[:, half, :], sh_act[:, half, :], SC[:, 0:SH], ALU.mult))
                at(eng, c_midT_psum, t)
                eng.tensor_tensor(sh_mid[:, SH * half:SH * half + SH], sh_rec[:, half, :], SC[:, SH:2 * SH],
                                  ALU.mult).then_inc(c_mid, 1)

            def c_result(t):
                eng.wait_ge(c_down, t + 1)
                at(eng, y_out_s, 16 * t)
                eng.tensor_tensor(y_sb[:, :], SC[:, 0:CM], row[:, 0:CM], ALU.add).then_inc(c_y, 1)

            for tile in (qk_pad, v_a, seen_bf):
                value = 1.0 if tile is v_a else 0.0
                eng.memset(tile[:], value).then_inc(dve_setup, 1)
            eng.memset(ones_bf[:, :], 1.0).then_inc(dve_setup, 1)
            eng.wait_ge(dve_setup, 4)
            eng.wait_ge(const_in, 16 * 10)

            def step(a, b, c):
                if a is not None:
                    a_rope(a)
                if b is not None:
                    b_latent_copy(b)
                if c is not None:
                    c_logits(c)
                if b is not None:
                    b_rotate(b, 0)
                if c is not None:
                    c_choose(c)
                if a is not None:
                    a_scale(a)
                if c is not None:
                    c_middle(c, 0)
                if b is not None:
                    b_rotate(b, 1)
                if a is not None:
                    a_k_copy(a)
                if b is not None:
                    b_window(b)
                    b_maxima(b, 0)
                    b_maxima(b, 1)
                if c is not None:
                    c_middle(c, 1)
                if b is not None:
                    b_maxima(b, 2)
                    b_maxima(b, 3)
                    b_prob_copy(b, 1)
                if a is not None:
                    a_normalise(a)
                if c is not None:
                    c_slots(c)
                if b is not None:
                    b_prob_copy(b, 3)
                    b_normalise(b, 0)
                    b_normalise(b, 1)
                if a is not None:
                    a_residual(a)
                if c is not None:
                    c_result(c)
                if b is not None:
                    b_residual(b)

            run_steps(step, eng)

            def expert(i, k):
                if have(i, k, 1):
                    e, s = D_RING * i + k - 1, (k - 1) % D_RING
                    b = bank[2 + s % 2]
                    eng.wait_ge(d_exp, e + 1)
                    then = link(eng, chain_d_mid, 3 * e)
                    then(eng.tensor_scalar(e_rec[:, s % 2, :], e_exp[:, s % 2, :], 1.0, None, ALU.add))
                    then(eng.reciprocal(e_act[:, s % 2, :], e_rec[:, s % 2, :]))
                    then(eng.tensor_tensor(e_rec[:, s % 2, :], e_act[:, s % 2, :], b[:, 0:EI], ALU.mult))
                    at(eng, d_midT_psum, two_ago(e, i, 1 - k))
                    eng.tensor_tensor(e_mid[:, s % 2, :], e_rec[:, s % 2, :], b[:, EI:2 * EI],
                                      ALU.mult).then_inc(d_mid, 1)
                if have(i, k, 3):
                    e, s = D_RING * i + k - 3, (k - 3) % D_RING
                    eng.wait_ge(d_down, e + 1)
                    at(eng, d_added, 16 * two_ago(e, i, 3 - k))
                    eng.tensor_scalar(e_out[:, s % 2, :], bank[6 + s % 2][:, 0:CM], ex[:, s, bass.ds(e + CM, 1)], None,
                                      ALU.mult).then_inc(d_out, 1)

            run_experts(expert, eng)

            for g in range(4):
                eng.wait_ge(yl_in[g], 16)
                then = link(eng, chain_e_norm, g)
                for j in range(4):
                    ins = eng.bn_stats(fin_stats[:, j, :], fin_in[g][:, CM * j:CM * j + CM])
                then(ins)
                at(eng, e_done, g)
                for j in range(4):
                    ins = eng.bn_aggr(fin_mv[:, j, :], fin_stats[:, j, :])
                ins.then_inc(e_var, 1)
                eng.wait_ge(e_rstd, g + 1)
                for j in range(4):
                    ins = eng.tensor_scalar(fin_out[g][:, CM * j:CM * j + CM], fin_in[g][:, CM * j:CM * j + CM],
                                            fin_mv[:, j, 0:1], fin_rstd[:, j:j + 1], ALU.subtract, ALU.mult)
                ins.then_inc(e_done, 1)

        @block.gpsimd
        def _(eng):
            def root(var_ap, eps_tile, out, chain, base, done_s, eps, scale=None):
                alone(eng)
                if scale is None:
                    ins = eng.tensor_scalar(eps_tile, var_ap, eps, None, ALU.add)
                else:
                    ins = eng.tensor_scalar(eps_tile, var_ap, scale, eps, ALU.mult, ALU.add)
                link(eng, chain, base)(ins)
                n = eps_tile.shape[1]
                eng.tensor_tensor(out, eps_tile, minus_half[:, 0:n], ALU.pow).then_inc(done_s, 1)

            def b_copy(t):
                eng.wait_ge(a_x1, t + 1)
                at(eng, b_res, t)
                alone(eng)
                eng.tensor_copy(x1_keep[:, :], x1[:, :]).then_inc(b_keep, 1)

            def a_root(t):
                eng.wait_ge(a_ss, t + 1)
                at(eng, a_qk, t)
                root(qk_ss[:, :], qk_ms[:, :], qk_rs[:, :], chain_a_rs, t, a_rs, RMS_EPS, 1.0 / HD)

            def a_causal(t):
                for j in range(4):
                    eng.wait_ge(a_exp, 4 * t + j + 1)
                    alone(eng)
                    pj = prob_a[:, 4 * j:4 * j + 4, :]
                    eng.affine_select(out=pj, in_=pj, compare_op=ALU.is_ge, fill=zero, base=0,
                                      pattern=[[0, 4], [1, P]], channel_multiplier=-1).then_inc(a_masked, 1)

            def a_norm_root(t):
                eng.wait_ge(a_var, t + 1)
                at(eng, a_x1, t)
                root(mv["a"][:, 1:2], var_eps["a"][:, :], rstd["a"][:, :], chain_a_rstd, t, a_rstd, LN_EPS)

            def b_norm_root(t):
                eng.wait_ge(b_var, t + 1)
                at(eng, b_x2, t)
                root(mv["b"][:, 1:2], var_eps["b"][:, :], rstd["b"][:, :], chain_b_rstd, t, b_rstd, LN_EPS)

            def c_send(t):
                eng.wait_ge(c_slot, t + 1)
                eng.wait_ge(c_row, 2 * t + 2)
                if isinstance(t, int) and t == 0:
                    eng.wait_ge(zeros_out, 16 * (E + 1))
                alone(eng)
                for k in range(TOPK):
                    eng.indirect_dma_start(
                        out=slots_dram[:, :], out_offset=bass.IndirectOffsetOnAxis(ap=slot_no[:, k:k + 1], axis=0),
                        in_=row[:, :], in_offset=None, bounds_check=last_slot, oob_is_err=False)\
                       .then_inc(c_sent, 16)

            zero = eng.to_reg(0.0)
            last_slot, last_row = eng.to_reg(E * CAP - 1), eng.to_reg(NTOK + P - 1)
            eng.memset(ex[:, :, :], 0.0).then_inc(pool_zeros, 1)
            eng.memset(minus_half[:, :], -0.5).then_inc(pool_zeros, 1)
            eng.wait_ge(pool_zeros, 2)

            def step(a, b, c):
                if b is not None:
                    b_copy(b)
                if a is not None:
                    a_root(a)
                if a is not None:
                    a_causal(a)
                if c is not None:
                    c_send(c)
                if a is not None:
                    a_norm_root(a)
                if b is not None:
                    b_norm_root(b)

            run_steps(step, eng)

            def expert(i, k):
                if have(i, k, 3):
                    e, s = D_RING * i + k - 3, (k - 3) % D_RING
                    eng.wait_ge(d_out, e + 1)
                    at(eng, d_added, 16 * e)
                    alone(eng)
                    eng.indirect_dma_start(
                        out=y_dram[:, :],
                        out_offset=bass.IndirectOffsetOnAxis(ap=ex[:, s, ROWW - 1:ROWW].bitcast(U32), axis=0),
                        in_=e_out[:, s % 2, :], in_offset=None, bounds_check=last_row, oob_is_err=True,
                        compute_op=ALU.add).then_inc(d_added, 16)

            run_experts(expert, eng)
            for g in range(4):
                eng.wait_ge(e_var, g + 1)
                root(fin_mv[:, :, 1], fin_var[:, :], fin_rstd[:, :], chain_e_rstd, g, e_rstd, LN_EPS)


def _tables():
    pos = np.arange(P, dtype=np.float32)
    inv_a = (1.0 / np.float32(10000.0) ** (np.arange(0, HD, 2, dtype=np.float32) / np.float32(HD))).astype(np.float32)
    ang_a = np.repeat(pos[:, None] * inv_a[None, :], 2, axis=1)
    sign_a = np.tile(np.array([-1, 1], np.float32), HD // 2)
    half = R // 2
    inv_b = (1.0 / np.float32(10000.0) ** (np.arange(half, dtype=np.float32) / np.float32(half))).astype(np.float32)
    ang_b = np.tile((pos[:, None] * inv_b[None, :]).T, (4, 1))
    sign_b = np.tile(np.repeat(np.array([-1, 1], np.float32), half), 2)[:, None]
    p = np.arange(P)
    return {
        "ident": np.eye(P, dtype=np.float32),
        "cos_a": np.tile(np.cos(ang_a), (1, 2 * H)).astype(np.float32),
        "sin_a": np.tile(np.sin(ang_a) * sign_a, (1, 2 * H)).astype(np.float32),
        "cos_b": np.cos(ang_b).astype(np.float32),
        "sin_b": (np.sin(ang_b) * sign_b).astype(np.float32),
        "key_pos": np.tile(p.astype(np.float32), (P, 1)),
        "slot_base": np.tile((NOSLOT - CAP * np.arange(E)).astype(np.float32), (P, 1)),
        "expert_no": np.tile(np.arange(E, dtype=np.float32), (P, 1)),
        "earlier": (p[:, None] < p[None, :]).astype(mybir.dt.np(BF16)),
        "token_no": (p - P).astype(np.int32)[:, None],
        "empty_no": (NTOK + p).astype(np.int32)[:, None],
    }


def _layouts(i):
    T = np.ascontiguousarray
    wqr = i["L0_xattn_W_qr"].reshape(QC, H // 2, 2, R)[:, :, ::-1, :]
    swapped = np.concatenate([wqr[..., R // 2:], wqr[..., :R // 2]], axis=-1)
    wkr = i["L0_xattn_W_kr"]
    wkr_s = np.concatenate([wkr[:, R // 2:], wkr[:, :R // 2]], axis=1)
    g, u = i["L0_ffn_sw_gate"], i["L0_ffn_sw_up"]
    return {
        "x": T(i["x"]),
        "xT": T(i["x"].transpose(0, 2, 1)),
        "ctxT": T(i["ctx_2048"].transpose(0, 2, 1)),
        "seg": T(i["itok_BxS_0_1023"]),
        "wqkvT": T(i["L0_attn_W_qkv"].T),
        "woT": T(i["L0_attn_W_o"].T),
        "wkvc2": T(np.concatenate([i["L0_xattn_W_kvc"]] * 2, axis=1)),
        "wdq": T(i["L0_xattn_W_dq"]),
        "wkr2": T(np.concatenate([wkr, wkr, wkr_s, wkr_s], axis=1)),
        "wqr": T(np.concatenate([wqr.reshape(QC, H * R), swapped.reshape(QC, H * R)], axis=1)),
        "uqT": T(i["L0_xattn_W_uq"].T),
        "ukT": T(i["L0_xattn_W_uk"].T),
        "uvT": T(i["L0_xattn_W_uv"].T),
        "wox": T(i["L0_xattn_W_o"]),
        "wgateT": T(i["L0_ffn_gate_w"].T),
        "wsh": T(np.concatenate([g[:, :SH], u[:, :SH], g[:, SH:], u[:, SH:]], axis=1)),
        "wshd": T(i["L0_ffn_sw_down"]),
        "ew": T(np.concatenate([i["L0_ffn_w_gate"], i["L0_ffn_w_up"]], axis=2)),
        "ewd": T(i["L0_ffn_w_down"]),
    }


def kernel(**inputs):
    import concourse.bacc as bacc
    from concourse.bass_utils import run_bass_kernel_spmd

    nc = bacc.Bacc("TRN2", target_bir_lowering=False, num_devices=1)
    arrays, io = {}, {}
    for name, a in {**_layouts({k: np.asarray(v) for k, v in inputs.items()}), **_tables()}.items():
        arrays[f"in_{name}"] = a
        io[name] = nc.dram_tensor(f"in_{name}", a.shape, mybir.dt.from_np(a.dtype), kind="ExternalInput").ap()
    y = nc.dram_tensor("out_y", (TILES, P, CM), F32, kind="ExternalOutput").ap()
    layer(nc, io, y)
    r = run_bass_kernel_spmd(nc, [arrays], core_ids=[0])
    return r.results[0]["out_y"]
```

```python
from contextlib import ExitStack

import numpy as np

import concourse.bass as bass
from concourse import mybir

ALU = mybir.AluOpType
ACT = mybir.ActivationFunctionType
AX = mybir.AxisListType
F32 = mybir.dt.float32
BF16 = mybir.dt.bfloat16
I32 = mybir.dt.int32
U32 = mybir.dt.uint32

P = 128
TILES, CM = 16, 256
CC = CM // P
H, HD = 16, 16
VW = 32
KVC, QC, R = 64, 96, 64
XHD = 128
LOOKBACK = 8
NEG = -1e30
E, TOPK, EI, CAP = 16, 4, 176, 128
SI = 352
SH = SI // 2
ROWW = CM + E + 1
NTOK = TILES * P
SCALE_A = HD ** -0.5
SCALE_B = float(np.float32(1.0) / np.sqrt(XHD + R).astype(np.float32))
RMS_EPS = 1.1920929e-07
LN_EPS = 1e-5
NOSLOT = 4096
D_RING = 4


def layer(nc, io, y_out):
    ctx = ExitStack()
    with ctx:
        def sb(name, shape, dt=F32):
            return ctx.enter_context(nc.sbuf_tensor(name, shape, dt))

        def sem(name):
            return ctx.enter_context(nc.semaphore(name))

        slots_dram = nc.dram_tensor("slots_dram", (E * CAP, ROWW), F32, kind="Internal").ap()
        y_dram = [nc.dram_tensor(f"y{n}_dram", (NTOK + P, CM), F32, kind="Internal").ap() for n in range(2)]

        ident = sb("ident", [P, P])
        cos_a = sb("cos_a", [P, 2 * CM])
        sin_a = sb("sin_a", [P, 2 * CM])
        cos_b = sb("cos_b", [P, P])
        sin_b = sb("sin_b", [P, P])
        key_pos = sb("key_pos", [P, P])
        slot_base = sb("slot_base", [P, E])
        expert_no = sb("expert_no", [P, E])
        minus_half = sb("minus_half", [P, 2 * H])
        earlier = sb("earlier", [P, P], BF16)
        ones_bf = sb("ones_bf", [P, P], BF16)
        wqkv = sb("wqkv", [P, CC, 3 * CM])
        wo = sb("wo", [P, CC, CM])
        wkvc2 = sb("wkvc2", [P, CC, 2 * KVC])
        wdq = sb("wdq", [P, CC, QC])
        wkr2 = sb("wkr2", [KVC, 2, 2 * R])
        wqr = sb("wqr", [QC, 2, H * R])
        wqk = sb("wqk", [QC, H * KVC])
        wvo = sb("wvo", [P, H // 2, CM])
        wgate = sb("wgate", [P, CC, E])
        wsh = sb("wsh", [P, CC, 2 * SI])
        wshd = sb("wshd", [P, 3, CM])

        xT = sb("xT", [P, CC, P])
        x_in = sb("x_in", [P, CM])
        qk_cos = sb("qk_cos", [P, 2 * CM])
        qk_sin = sb("qk_sin", [P, 2 * CM])
        qk_rot = sb("qk_rot", [P, 2 * CM])
        qk_sq = sb("qk_sq", [P, 2 * CM])
        qk_ss = sb("qk_ss", [P, 2 * H])
        qk_ms = sb("qk_ms", [P, 2 * H])
        qk_rs = sb("qk_rs", [P, 2 * H])
        qk_pad = sb("qk_pad", [P, 2 * H, 32])
        v_a = sb("v_a", [P, H, VW])
        qT = sb("qT", [P, 4, P])
        kT = sb("kT", [P, 4, P])
        prob_a = sb("prob_a", [P, H, P])
        rec_a = sb("rec_a", [P, H])
        att_raw = sb("att_raw", [P, 4, P])
        att_a = sb("att_a", [P, CM])
        att_aT = sb("att_aT", [P, CC, P])
        res_a = sb("res_a", [P, CM])
        x1 = sb("x1", [P, CM])

        ctxT = sb("ctxT", [P, CC, P])
        seg = sb("seg", [P, 1], I32)
        seg_f = sb("seg_f", [P, 1])
        mask_d = sb("mask_d", [P, P])
        mask_b = sb("mask_b", [P, P])
        x1_keep = sb("x1_keep", [P, CM])
        x1T = sb("x1T", [P, CC, P])
        kk_e = sb("kk_e", [P, P])
        kk_o = sb("kk_o", [P, P])
        kr_cos = sb("kr_cos", [P, P])
        kr_sin = sb("kr_sin", [P, P])
        qcT = sb("qcT", [QC, P])
        v_b = sb("v_b", [P, KVC])
        qr_cos = sb("qr_cos", [P, 2, 4 * P])
        qr_sin = sb("qr_sin", [P, 2, 4 * P])
        qq_e = sb("qq_e", [P, H // 2, P])
        qq_o = sb("qq_o", [P, H // 2, P])
        score_b = sb("score_b", [P, H, P])
        max_b = sb("max_b", [P, H])
        negmax_b = sb("negmax_b", [P, H])
        prob_b = sb("prob_b", [P, H, P])
        den_b = sb("den_b", [P, H])
        rec_b = sb("rec_b", [P, H])
        prob_bT = sb("prob_bT", [P, H, P])
        att_bT = sb("att_bT", [P, H // 2, P])
        res_b = sb("res_b", [P, CM])
        x2 = sb("x2", [P, CM])

        stats = {s: sb(f"stats_{s}", [P, 6]) for s in "abe"}
        mv = {s: sb(f"mv_{s}", [P, 2]) for s in "abe"}
        var_eps = {s: sb(f"var_eps_{s}", [P, 1]) for s in "abe"}
        rstd = {s: sb(f"rstd_{s}", [P, 1]) for s in "abe"}

        row = sb("row", [P, ROWW])
        x2T = sb("x2T", [P, CC, P])
        logit = sb("logit", [P, E])
        neg_top = sb("neg_top", [P, 1])
        gexp = sb("gexp", [P, E])
        gsum = sb("gsum", [P, 1])
        grec = sb("grec", [P, 1])
        gprob = sb("gprob", [P, E])
        top8 = sb("top8", [P, 8])
        top_no = sb("top_no", [P, 8], U32)
        top_nof = sb("top_nof", [P, 8])
        chosen = sb("chosen", [P, 2, E])
        chosen_bf = sb("chosen_bf", [P, E], BF16)
        seen_bf = sb("seen_bf", [P, E], BF16)
        wsel = sb("wsel", [P, E])
        wsum = sb("wsum", [P, 2])
        wrec = sb("wrec", [P, 1])
        slot_u = sb("slot_u", [P, E])
        slot_v = sb("slot_v", [P, E])
        slot_s = sb("slot_s", [P, E])
        slot8 = sb("slot8", [P, 8])
        slot_no = sb("slot_no", [P, 8], U32)
        sh_exp = sb("sh_exp", [P, 2, SH])
        sh_act = sb("sh_act", [P, 2, SH])
        sh_mid = sb("sh_mid", [P, SI])
        sh_midT = sb("sh_midT", [P, 3, P])
        y_sb = sb("y_sb", [P, CM])

        ew = sb("ew", [P, D_RING, CC, 2 * EI])
        ewd = sb("ewd", [EI // 2, D_RING, 2, CM])
        ex = sb("ex", [P, D_RING, ROWW])
        etok = sb("etok", [P, D_RING], U32)
        e_weight = sb("e_weight", [P, D_RING])
        exT = sb("exT", [P, 2, CC, P])
        e_exp = sb("e_exp", [P, 2, EI])
        e_act = sb("e_act", [P, 2, EI])
        e_mid = sb("e_mid", [P, 2, EI])
        e_midT = sb("e_midT", [EI // 2, 2, 2, P])
        e_out = sb("e_out", [P, 2, CM])
        uqT = score_b[:, 0:12, :].rearrange("p a b -> p (a b)").rearrange("p (h q) -> p h q", q=QC)
        ukT = prob_b[:, 0:8, :].rearrange("p a b -> p (a b)").rearrange("p (h q) -> p h q", q=KVC)
        uvT = prob_b[:, 8:16, :].rearrange("p a b -> p (a b)").rearrange("p (h q) -> p h q", q=KVC)
        wox_lo = prob_bT[:, :, :].rearrange("p a b -> p (a b)").rearrange("p (h o) -> p h o", o=CM)
        wox_hi = [q[:, :, :].rearrange("p a b -> p (a b)").rearrange("p (h o) -> p h o", o=CM) for q in (qq_e, qq_o)]

        empty_row = ex[:, 0, :]
        halves = [t[:, 8 * g:8 * g + 8, :].rearrange("p a b -> p (a b)")
                  for t in (score_b, prob_b, prob_bT, prob_a) for g in range(2)]
        fin_in = (halves[0:4], halves[4:8])
        fin_out = [t[:, :, :].rearrange("p a b -> p (a b)") for t in (qq_e, qq_o)] + [
            qr_cos[:, :, :].rearrange("p a b -> p (a b)"), qr_sin[:, :, :].rearrange("p a b -> p (a b)")]
        fin_mv = sb("fin_mv", [P, 4, 2])
        fin_stats = sb("fin_stats", [P, 4, 6])
        fin_var = sb("fin_var", [P, 4])
        fin_rstd = sb("fin_rstd", [P, 4])

        bank = [ctx.enter_context(nc.psum_tensor(f"bank{i}", [P, 512], F32)) for i in range(8)]
        SA, SB, SC = bank[0:4], bank[4:7], bank[7]

        const_in = sem("const_in")
        waited = sem("waited")
        wqkv_in, wlate_in = sem("wqkv_in"), sem("wlate_in")
        wqk_in, wvo_in = sem("wqk_in"), sem("wvo_in")
        zeros_out = sem("zeros_out")
        dve_setup = sem("dve_setup")
        pool_zeros = sem("pool_zeros")
        empty_in = sem("empty_in")
        wqk_psum = sem("wqk_psum")
        wqk_sb = sem("wqk_sb")
        wvo_psum = sem("wvo_psum")
        wvo_sb = sem("wvo_sb")
        xT_in, x_in_s, ctxT_in, seg_in = sem("xT_in"), sem("x_in_s"), sem("ctxT_in"), sem("seg_in")
        (chain_a_rope, chain_a_att, chain_a_norm, chain_b_latent, chain_b_mask, chain_b_max, chain_b_att,
         chain_b_norm, chain_c_top, chain_c_choose, chain_c_slot, chain_c_mid, chain_d_mid, chain_e_norm) = (
            sem(f"chain_{n}") for n in ("a_rope", "a_att", "a_norm", "b_latent", "b_mask", "b_max", "b_att",
                                        "b_norm", "c_top", "c_choose", "c_slot", "c_mid", "d_mid", "e_norm"))
        chain_a_rs, chain_a_rstd, chain_b_rstd, chain_e_rstd, chain_seen = (
            sem(f"chain_{n}") for n in ("a_rs", "a_rstd", "b_rstd", "e_rstd", "seen"))
        a_qk_psum = sem("a_qk_psum")
        a_qkv = sem("a_qkv")
        a_ss = sem("a_ss")
        a_v = sem("a_v")
        a_rs = sem("a_rs")
        a_qk = sem("a_qk")
        a_tr = sem("a_tr")
        a_qT = sem("a_qT")
        a_kT = sem("a_kT")
        a_score = sem("a_score")
        a_exp = sem("a_exp")
        a_masked = sem("a_masked")
        a_av = sem("a_av")
        a_raw = sem("a_raw")
        a_raw_turned = sem("a_raw_turned")
        a_att = sem("a_att")
        a_attT_psum = sem("a_attT_psum")
        a_attT = sem("a_attT")
        a_wo = sem("a_wo")
        a_res = sem("a_res")
        a_var = sem("a_var")
        a_rstd = sem("a_rstd")
        a_x1 = sem("a_x1")
        b_keep = sem("b_keep")
        b_in_psum = sem("b_in_psum")
        b_in = sem("b_in")
        b_qc_psum = sem("b_qc_psum")
        b_qc = sem("b_qc")
        b_keys = sem("b_keys")
        b_q_psum = sem("b_q_psum")
        b_rot = sem("b_rot")
        b_rope = sem("b_rope")
        b_nope = sem("b_nope")
        b_mask = sem("b_mask")
        b_score_psum = sem("b_score_psum")
        b_score = sem("b_score")
        b_prob = sem("b_prob")
        b_pT_psum = sem("b_pT_psum")
        b_weights = sem("b_weights")
        b_pT = sem("b_pT")
        b_av = sem("b_av")
        b_attT = sem("b_attT")
        b_wo = sem("b_wo")
        b_res = sem("b_res")
        b_var = sem("b_var")
        b_rstd = sem("b_rstd")
        b_x2 = sem("b_x2")
        c_row = sem("c_row")
        c_xT_psum = sem("c_xT_psum")
        c_xT = sem("c_xT")
        c_logit_psum = sem("c_logit_psum")
        c_logit = sem("c_logit")
        c_top = sem("c_top")
        c_gexp = sem("c_gexp")
        c_chosen = sem("c_chosen")
        c_rank = sem("c_rank")
        c_slot = sem("c_slot")
        c_sent = sem("c_sent")
        c_gu_psum = sem("c_gu_psum")
        c_gexp2 = sem("c_gexp2")
        c_mid = sem("c_mid")
        c_midT_psum = sem("c_midT_psum")
        c_midT = sem("c_midT")
        c_down = sem("c_down")
        c_y = sem("c_y")
        y_out_s = sem("y_out_s")
        ew_in = [sem(f"ew_in{i}") for i in range(D_RING)]
        ewd_in = [sem(f"ewd_in{i}") for i in range(D_RING)]
        d_copied = sem("d_copied")
        ex_in = [sem(f"ex_in{i}") for i in range(D_RING)]
        d_xT_psum, d_xT = sem("d_xT_psum"), sem("d_xT")
        d_gu_psum, d_exp, d_mid = sem("d_gu_psum"), sem("d_exp"), sem("d_mid")
        d_midT_psum, d_midT = sem("d_midT_psum"), sem("d_midT")
        d_down, d_out = sem("d_down"), sem("d_out")
        d_added = [sem("d_added0"), sem("d_added1")]
        yl_in = [sem(f"yl_in{g}") for g in range(4)]
        e_var, e_rstd, e_done, final_out = sem("e_var"), sem("e_rstd"), sem("e_done"), sem("final_out")

        def at(eng, s, value):
            if not isinstance(value, int) or value > 0:
                eng.wait_ge(s, value)

        def link(eng, s, base):
            n = [0]

            def f(ins):
                n[0] += 1
                ins.then_inc(s, 1)
                eng.wait_ge(s, base + n[0])
            return f

        def two_ago(e, i, back):
            if isinstance(i, int):
                return e - 1
            return e - 1 if back <= 2 else e

        def alone(eng):
            eng.sem_inc(waited, 1)

        def earlier_pairs(i, k):
            return 2 * i + (k - 3) // 2

        def run_steps(step, eng):
            step(0, None, None)
            step(1, 0, None)
            step(2, 1, 0)
            with eng.Fori(3, TILES) as i:
                step(i, i - 1, i - 2)
            step(None, TILES - 1, TILES - 2)
            step(None, None, TILES - 1)

        def run_experts(step, eng):
            for k in range(D_RING):
                step(0, k)
            with eng.Fori(1, E // D_RING) as i:
                for k in range(D_RING):
                    step(i, k)
            for k in range(3):
                step(E // D_RING, k)

        def have(i, k, n):
            if isinstance(i, int):
                return 0 <= D_RING * i + k - n < E
            return True

        block = ctx.enter_context(nc.Block())

        @block.sync
        def _(eng):
            chunked = "(c p) n -> p c n"

            def load_xT(t):
                eng.dma_start(xT[:, :, :], io["xT"][bass.ds(t, 1), :, :].rearrange(
                    "b (c p) s -> p (b c) s", p=P)).then_inc(xT_in, 16)

            def load(dst, name, s):
                eng.dma_start(dst[:, :, :], io[name].rearrange(chunked, p=P)).then_inc(s, 16)

            load_xT(0)
            load(wqkv, "wqkvT", wqkv_in)
            eng.dma_start(uqT, io["uqT"].rearrange("(h d) q -> d h q", d=XHD)).then_inc(wqk_in, 16)
            eng.dma_start(ukT, io["ukT"].rearrange("(h d) q -> d h q", d=XHD)).then_inc(wqk_in, 16)
            load(wkvc2, "wkvc2", wlate_in)
            load(wdq, "wdq", wlate_in)
            eng.dma_start(wkr2[:, :, :], io["wkr2"].rearrange("p (a n) -> p a n", a=2)).then_inc(wlate_in, 16)
            eng.dma_start(wqr[:, :, :], io["wqr"].rearrange("p (a n) -> p a n", a=2)).then_inc(wlate_in, 16)
            eng.dma_start(uvT, io["uvT"].rearrange("(h d) q -> d h q", d=XHD)).then_inc(wvo_in, 16)
            xo = io["wox"].rearrange("(h d) o -> d h o", d=XHD)
            eng.dma_start(wox_lo, xo[:, 0:8, :]).then_inc(wvo_in, 16)
            for n in range(2):
                eng.dma_start(wox_hi[n], xo[:, 8 + 4 * n:12 + 4 * n, :]).then_inc(wvo_in, 16)
            load(wo, "woT", wlate_in)
            load(wgate, "wgateT", wlate_in)
            load(wsh, "wsh", wlate_in)
            eng.dma_start(wshd[:, 0:2, :], io["wshd"][0:2 * P, :].rearrange(chunked, p=P)).then_inc(wlate_in, 16)
            eng.dma_start(wshd[0:SI - 2 * P, 2, :], io["wshd"][2 * P:SI, :]).then_inc(wlate_in, 16)
            eng.wait_ge(pool_zeros, 1)
            eng.dma_start(empty_row[:, ROWW - 1:ROWW].bitcast(I32), io["empty_no"]).then_inc(empty_in, 16)
            eng.wait_ge(empty_in, 16)
            for e in range(E):
                eng.dma_start(slots_dram[e * CAP:(e + 1) * CAP, :], empty_row).then_inc(zeros_out, 16)
            for y in y_dram:
                eng.dma_start(y[NTOK:NTOK + P, :], empty_row[:, 0:CM]).then_inc(zeros_out, 16)

            def load_expert(i, k):
                e = D_RING * i + k
                at(eng, d_gu_psum, e - D_RING + 1 if not isinstance(i, int) or i else 0)
                eng.dma_start(ew[:, k, :, :], io["ew"][bass.ds(e, 1), :, :].rearrange(
                    "e (c p) n -> p (e c) n", p=P)).then_inc(ew_in[k], 16)

            def load_slots(i, k):
                e = D_RING * i + k
                at(eng, d_copied, e - D_RING + 1 if not isinstance(i, int) or i else 0)
                at(eng, d_xT_psum, e - D_RING + 1 if not isinstance(i, int) or i else 0)
                eng.dma_start(ex[:, k, :], slots_dram[bass.ds(e * CAP, CAP), :]).then_inc(ex_in[k], 16)

            for k in range(D_RING):
                load_expert(0, k)

            def store_shared(t):
                eng.wait_ge(c_y, t + 1)
                eng.dma_start(y_dram[0][bass.ds(t * P, P), :], row[:, 0:CM]).then_inc(y_out_s, 16)
                eng.dma_start(y_dram[1][bass.ds(t * P, P), :], y_sb[:, :]).then_inc(y_out_s, 16)

            def step(a, b, c):
                if a is not None and not (isinstance(a, int) and a == 0):
                    at(eng, a_qkv, a)
                    load_xT(a)
                if b is not None:
                    at(eng, b_in_psum, b)
                    eng.dma_start(ctxT[:, :, :], io["ctxT"][bass.ds(b, 1), :, :].rearrange(
                        "b (c p) s -> p (b c) s", p=P)).then_inc(ctxT_in, 16)
                    at(eng, b_mask, 2 * b)
                    eng.dma_start(seg[:, :], io["seg"][bass.ds(b, 1), :].rearrange("b s -> s b"))\
                       .then_inc(seg_in, 16)
                if a is not None:
                    at(eng, a_res, a)
                    eng.dma_start(x_in[:, :], io["x"][bass.ds(a, 1), :, :].rearrange("b s c -> (b s) c"))\
                       .then_inc(x_in_s, 16)
                if c is not None and not (isinstance(c, int) and c == 0):
                    store_shared(c - 1)

            run_steps(step, eng)
            store_shared(TILES - 1)

            eng.wait_ge(c_sent, 16 * TOPK * TILES)
            for k in range(D_RING):
                load_slots(0, k)
            with eng.Fori(1, E // D_RING) as i:
                for k in range(D_RING):
                    load_slots(i, k)
                    load_expert(i, k)

            for n in range(2):
                eng.wait_ge(d_added[n], 16 * E // 2)
            tokens = "(g p j) c -> g p (j c)"
            ov = y_out.rearrange("b s c -> (b s) c").rearrange(tokens, p=P, j=4)
            for g in range(4):
                for n in range(2):
                    yv = y_dram[n][0:NTOK, :].rearrange(tokens, p=P, j=4)
                    eng.dma_start(fin_in[n][g], yv[g]).then_inc(yl_in[g], 16)
            for g in range(4):
                eng.wait_ge(e_done, g + 1)
                eng.dma_start(ov[g], fin_out[g]).then_inc(final_out, 16)
            eng.wait_ge(final_out, 16 * 4)

        @block.tensor
        def _(eng):
            def turn(out, in_):
                return eng.transpose(out, in_, ident[0:in_.shape[0], 0:in_.shape[0]])

            def a_project(t):
                eng.wait_ge(xT_in, 16 * (t + 1))
                at(eng, a_res, t)
                for c in range(CC):
                    mm = eng.matmul(SA[0][:, :], xT[:, c, :], wqkv[:, c, 0:2 * CM], start=c == 0, stop=c == CC - 1)
                mm.then_inc(a_qk_psum, 1)

            def a_project_v(t):
                for c in range(CC):
                    mm = eng.matmul(SA[1][:, 0:CM], xT[:, c, :], wqkv[:, c, 2 * CM:3 * CM],
                                    start=c == 0, stop=c == CC - 1)
                mm.then_inc(a_qkv, 1)

            def a_turn(t):
                if isinstance(t, int) and t == 0:
                    eng.wait_ge(const_in, 16 * 10)
                eng.wait_ge(a_qk, t + 1)
                at(eng, a_attT, t)
                for s in range(2):
                    for g in range(4):
                        heads = qk_pad[:, H * s + 4 * g:H * s + 4 * g + 4, :].rearrange("p h d -> p (h d)")
                        mm = turn(SA[2 + s][:, P * g:P * g + P], heads)
                    mm.then_inc(a_tr, 1)

            def a_scores(t, g):
                if g == 0:
                    eng.wait_ge(a_qT, t + 1)
                    eng.wait_ge(a_kT, t + 1)
                    eng.wait_ge(a_v, t + 1)
                for j in range(4):
                    rows = slice(32 * j, 32 * j + HD)
                    mm = eng.matmul(SA[j][:, P * g:P * g + P], kT[rows, g, :], qT[rows, g, :],
                                    start=True, stop=True)
                mm.then_inc(a_score, 1)

            def a_values(t):
                eng.wait_ge(a_masked, 4 * t + 4)
                for g in range(4):
                    for j in range(4):
                        mm = eng.matmul(SA[0][VW * j:VW * j + VW, P * g:P * g + P], v_a[:, 4 * g + j, :],
                                        prob_a[:, 4 * j + g, :], start=True, stop=True)
                mm.then_inc(a_av, 1)

            def a_turn_raw(t):
                eng.wait_ge(a_raw, t + 1)
                for g in range(4):
                    mm = turn(SA[2][:, P * g:P * g + P], att_raw[:, g, :])
                mm.then_inc(a_raw_turned, 1)

            def a_turn_out(t):
                eng.wait_ge(a_att, t + 1)
                for c in range(CC):
                    mm = turn(SA[3][:, P * c:P * c + P], att_a[:, P * c:P * c + P])
                mm.then_inc(a_attT_psum, 1)

            def a_out(t):
                if isinstance(t, int) and t == 0:
                    eng.wait_ge(wlate_in, 16 * 9)
                eng.wait_ge(a_attT, t + 1)
                for c in range(CC):
                    mm = eng.matmul(SA[1][:, 0:CM], att_aT[:, c, :], wo[:, c, :], start=c == 0, stop=c == CC - 1)
                mm.then_inc(a_wo, 1)

            def b_input(t):
                if isinstance(t, int) and t == 0:
                    eng.wait_ge(wlate_in, 16 * 9)
                    eng.wait_ge(wqk_sb, 2)
                    eng.wait_ge(wvo_sb, 4)
                eng.wait_ge(a_x1, t + 1)
                eng.wait_ge(ctxT_in, 16 * (t + 1))
                at(eng, b_pT, 4 * t)
                for c in range(CC):
                    turn(SB[2][:, P * c:P * c + P], x1[:, P * c:P * c + P])
                for c in range(CC):
                    mm = eng.matmul(SB[2][:, CM:CM + P], wkvc2[:, c, :], ctxT[:, c, :],
                                    start=c == 0, stop=c == CC - 1)
                mm.then_inc(b_in_psum, 1)

            def b_latent(t):
                eng.wait_ge(b_in, t + 1)
                at(eng, b_res, t)
                for c in range(CC):
                    eng.matmul(SB[0][0:QC, 0:P], wdq[:, c, :], x1T[:, c, :], start=c == 0, stop=c == CC - 1)
                for s in range(2):
                    eng.matmul(SB[0][:, P * (1 + s):P * (2 + s)], wkr2[:, s, :], kk_e[0:KVC, :],
                               start=True, stop=True)
                turn(SB[0][:, 3 * P:3 * P + KVC], kk_e[0:KVC, :]).then_inc(b_qc_psum, 1)

            def b_queries(t, half):
                eng.wait_ge(b_qc, t + 1)
                for use, bk in enumerate((SB[1], SB[2], SB[0])):
                    if half == 1:
                        eng.wait_ge(b_rot, 4 * t + 1 + use) if use < 2 else eng.wait_ge(b_nope, 2 * t + 1)
                    elif use == 0:
                        at(eng, b_attT, 2 * t)
                    elif use == 2:
                        eng.wait_ge(b_keys, t + 1)
                    for j in range(4):
                        pair = slice(P * (4 * half + j), P * (4 * half + j) + P)
                        w = wqk[:, pair] if use == 2 else wqr[:, use, pair]
                        mm = eng.matmul(bk[:, P * j:P * j + P], w, qcT[:, :], start=True, stop=True)
                    mm.then_inc(b_q_psum, 1)

            def b_scores(t, g):
                if g % 2 == 0:
                    eng.wait_ge(b_rope, 4 * t + 2 + g)
                    eng.wait_ge(b_nope, 2 * t + 1 + g // 2)
                if g < 2:
                    eng.wait_ge(b_rot, 4 * t + 3 + g)
                elif g == 3:
                    eng.wait_ge(b_score, 4 * t + 1)
                for j in range(4):
                    h = 4 * g + j
                    qq, kk = (qq_e, kk_e) if h % 2 == 0 else (qq_o, kk_o)
                    mm = eng.matmul(SB[(1 + g) % 3][:, P * j:P * j + P], qq[:, h // 2, :], kk[:, :],
                                    start=True, stop=True)
                mm.then_inc(b_score_psum, 1)

            def b_turn(t, g):
                eng.wait_ge(b_weights, 4 * t + g + 1)
                eng.wait_ge(b_score, 4 * t + min(g + 2, 4))
                if g == 3:
                    eng.wait_ge(b_pT, 4 * t + 1)
                for j in range(4):
                    mm = turn(SB[(2 + g) % 3][:, P * j:P * j + P], prob_b[:, 4 * g + j, :])
                mm.then_inc(b_pT_psum, 1)

            def b_values(t, half):
                eng.wait_ge(b_pT, 4 * t + 2 + 2 * half)
                for odd in range(2):
                    heads = prob_bT[:, 8 * half + odd:8 * half + 8:2, :]
                    mm = eng.matmul(SB[half][KVC * odd:KVC * odd + KVC, :].rearrange("p (j q) -> p j q", q=P),
                                    v_b[:, :], heads, start=True, stop=True)
                mm.then_inc(b_av, 1)

            def b_out(t, half):
                eng.wait_ge(b_attT, 2 * t + half + 1)
                for j in range(4 * half, 4 * half + 4):
                    mm = eng.matmul(SB[0][:, 0:CM], att_bT[:, j, :], wvo[:, j, :],
                                    start=j == 0, stop=j == H // 2 - 1)
                if half == 1:
                    mm.then_inc(b_wo, 1)

            def c_turn(t):
                eng.wait_ge(b_x2, t + 1)
                at(eng, c_y, t)
                for c in range(CC):
                    mm = turn(SC[:, P * c:P * c + P], x2[:, P * c:P * c + P])
                mm.then_inc(c_xT_psum, 1)

            def c_router(t):
                eng.wait_ge(c_xT, t + 1)
                for c in range(CC):
                    mm = eng.matmul(SC[:, 0:E], x2T[:, c, :], wgate[:, c, :], start=c == 0, stop=c == CC - 1)
                mm.then_inc(c_logit_psum, 1)

            def c_up(t, half):
                if half == 0:
                    eng.wait_ge(c_logit, t + 1)
                else:
                    eng.wait_ge(c_mid, 2 * t + 1)
                for c in range(CC):
                    mm = eng.matmul(SC[:, 0:2 * SH], x2T[:, c, :], wsh[:, c, 2 * SH * half:2 * SH * (half + 1)],
                                    start=c == 0, stop=c == CC - 1)
                mm.then_inc(c_gu_psum, 1)

            def c_ranks(t):
                eng.wait_ge(c_chosen, t + 1)
                eng.wait_ge(c_mid, 2 * t + 2)
                eng.matmul(SC[:, 0:E], earlier[:, :], chosen_bf[:, :], start=True, stop=False)
                eng.matmul(SC[:, 0:E], ones_bf[:, :], seen_bf[:, :], start=False, stop=True).then_inc(c_rank, 1)

            def c_turn_mid(t):
                eng.wait_ge(c_slot, t + 1)
                for c in range(3):
                    n = min(P, SI - P * c)
                    mm = turn(SC[0:n, P * c:P * c + P], sh_mid[:, P * c:P * c + n])
                mm.then_inc(c_midT_psum, 1)

            def c_out(t):
                eng.wait_ge(c_midT, t + 1)
                for c in range(3):
                    n = min(P, SI - P * c)
                    mm = eng.matmul(SC[:, 0:CM], sh_midT[0:n, c, :], wshd[0:n, c, :], start=c == 0, stop=c == 2)
                mm.then_inc(c_down, 1)

            def multiply_wqk():
                eng.wait_ge(wqk_in, 16 * 2)
                for h in range(H):
                    mm = eng.matmul(bank[4 + h // 8][0:QC, KVC * (h % 8):KVC * (h % 8) + KVC], uqT[:, h, :],
                                    ukT[:, h, :], start=True, stop=True)
                    if h % 8 == 7:
                        mm.then_inc(wqk_psum, 1)

            def multiply_wvo():
                eng.wait_ge(wvo_in, 16 * 4)
                for h in range(H):
                    j, odd = h // 2, h % 2
                    if h in (8, 12):
                        eng.wait_ge(wqk_sb, h // 4 - 1)
                    wox = wox_lo[:, h, :] if h < 8 else wox_hi[(h - 8) // 4][:, h % 4, :]
                    mm = eng.matmul(bank[(6, 7, 4, 5)[j // 2]][KVC * odd:KVC * odd + KVC, CM * (j % 2):CM * (j % 2) + CM],
                                    uvT[:, h, :], wox, start=True, stop=True)
                    if h % 4 == 3:
                        mm.then_inc(wvo_psum, 1)

            def step(a, b, c):
                if a is not None:
                    a_project(a)
                if b is not None:
                    b_input(b)
                if a is not None:
                    a_project_v(a)
                if b is None and c is None:
                    multiply_wqk()
                if b is not None:
                    b_latent(b)
                if c is not None:
                    c_turn(c)
                if b is not None:
                    b_queries(b, 0)
                if c is not None:
                    c_router(c)
                if b is not None:
                    b_queries(b, 1)
                    b_scores(b, 0)
                    b_scores(b, 1)
                if c is not None:
                    c_up(c, 0)
                if a is not None:
                    a_turn(a)
                if b is not None:
                    b_scores(b, 2)
                    b_scores(b, 3)
                if a is not None:
                    a_scores(a, 0)
                    a_scores(a, 1)
                if b is not None:
                    b_turn(b, 0)
                if a is not None:
                    a_scores(a, 2)
                    a_scores(a, 3)
                if b is None and c is None:
                    multiply_wvo()
                if b is not None:
                    b_turn(b, 1)
                if c is not None:
                    c_up(c, 1)
                if b is not None:
                    b_turn(b, 2)
                    b_turn(b, 3)
                if a is not None:
                    a_values(a)
                if b is not None:
                    b_values(b, 0)
                if a is not None:
                    a_turn_raw(a)
                if b is not None:
                    b_values(b, 1)
                if c is not None:
                    c_ranks(c)
                if a is not None:
                    a_turn_out(a)
                if b is not None:
                    b_out(b, 0)
                if a is not None:
                    a_out(a)
                if b is not None:
                    b_out(b, 1)
                if c is not None:
                    c_turn_mid(c)
                    c_out(c)

            eng.wait_ge(wqkv_in, 16)
            run_steps(step, eng)

            def expert(i, k):
                if have(i, k, 0):
                    e = D_RING * i + k
                    eng.wait_ge(ex_in[k], 16 * (i + 1))
                    at(eng, d_xT, two_ago(e, i, 0))
                    for c in range(CC):
                        mm = turn(bank[k % 2][:, P * c:P * c + P], ex[:, k, P * c:P * c + P])
                    mm.then_inc(d_xT_psum, 1)
                if have(i, k, 1):
                    e, s = D_RING * i + k - 1, (k - 1) % D_RING
                    eng.wait_ge(ew_in[s], 16 * (i + 1 if k >= 1 else i))
                    eng.wait_ge(d_xT, e + 1)
                    at(eng, d_mid, two_ago(e, i, 1 - k))
                    for c in range(CC):
                        mm = eng.matmul(bank[2 + s % 2][:, 0:2 * EI], exT[:, s % 2, c, :], ew[:, s, c, :],
                                        start=c == 0, stop=c == CC - 1)
                    mm.then_inc(d_gu_psum, 1)
                if have(i, k, 2):
                    e, s = D_RING * i + k - 2, (k - 2) % D_RING
                    eng.wait_ge(d_mid, e + 1)
                    at(eng, d_midT, two_ago(e, i, 2 - k))
                    for c in range(2):
                        mm = turn(bank[4 + s % 2][0:EI // 2, P * c:P * c + P],
                                  e_mid[:, s % 2, EI // 2 * c:EI // 2 * (c + 1)])
                    mm.then_inc(d_midT_psum, 1)
                if have(i, k, 3):
                    e, s = D_RING * i + k - 3, (k - 3) % D_RING
                    eng.wait_ge(ewd_in[s], 16 * (i + 1 if k >= 3 else i))
                    eng.wait_ge(d_midT, e + 1)
                    at(eng, d_out, two_ago(e, i, 3 - k))
                    for c in range(2):
                        mm = eng.matmul(bank[6 + s % 2][:, 0:CM], e_midT[:, s % 2, c, :], ewd[:, s, c, :],
                                        start=c == 0, stop=c == 1)
                    mm.then_inc(d_down, 1)

            eng.wait_ge(c_y, TILES)
            run_experts(expert, eng)

        @block.scalar
        def _(eng):
            def a_value_copy(t):
                eng.wait_ge(a_qkv, t + 1)
                at(eng, a_av, t)
                eng.activation(v_a[:, :, 0:HD], SA[1][:, 0:CM].rearrange("p (h d) -> p h d", d=HD),
                               ACT.Copy).then_inc(a_v, 1)

            def a_q_copy(t):
                eng.wait_ge(a_tr, 2 * t + 1)
                at(eng, a_score, 4 * t)
                eng.activation(qT[:, :, :], SA[2][:, :].rearrange("p (g q) -> p g q", q=P),
                               ACT.Copy).then_inc(a_qT, 1)

            def a_k_copy(t):
                eng.wait_ge(a_tr, 2 * t + 2)
                at(eng, a_score, 4 * t)
                eng.activation(kT[:, :, :], SA[3][:, :].rearrange("p (g q) -> p g q", q=P),
                               ACT.Copy).then_inc(a_kT, 1)

            def a_raw_copy(t):
                eng.wait_ge(a_av, t + 1)
                at(eng, a_raw_turned, t)
                eng.activation(att_raw[:, :, :], SA[0][:, :].rearrange("p (g q) -> p g q", q=P),
                               ACT.Copy).then_inc(a_raw, 1)

            def a_exps(t):
                eng.wait_ge(a_score, 4 * t + 4)
                at(eng, a_av, t)
                for j in range(4):
                    eng.activation(prob_a[:, 4 * j:4 * j + 4, :], SA[j][:, :].rearrange("p (g q) -> p g q", q=P),
                                   ACT.Exp, scale=SCALE_A).then_inc(a_exp, 1)

            def a_att_copy(t):
                eng.wait_ge(a_attT_psum, t + 1)
                at(eng, a_wo, t)
                eng.activation(att_aT[:, :, :], SA[3][:, 0:CM].rearrange("p (c q) -> p c q", q=P),
                               ACT.Copy).then_inc(a_attT, 1)

            def b_input_copy(t):
                eng.wait_ge(b_in_psum, t + 1)
                at(eng, b_qc_psum, t)
                at(eng, b_score_psum, 4 * t)
                eng.activation(x1T[:, :, :], SB[2][:, 0:CM].rearrange("p (c q) -> p c q", q=P), ACT.Copy)
                eng.activation(kk_e[0:KVC, :], SB[2][0:KVC, CM:CM + P], ACT.Copy)
                eng.activation(kk_o[KVC:2 * KVC, :], SB[2][KVC:2 * KVC, CM:CM + P], ACT.Copy).then_inc(b_in, 1)

            def b_latent_copy(t):
                eng.wait_ge(b_qc_psum, t + 1)
                at(eng, b_q_psum, 6 * t)
                at(eng, b_av, 2 * t)
                eng.activation(qcT[:, :], SB[0][0:QC, 0:P], ACT.Copy)
                eng.activation(v_b[:, :], SB[0][:, 3 * P:3 * P + KVC], ACT.Copy).then_inc(b_qc, 1)

            def b_nope_copy(t, half):
                eng.wait_ge(b_q_psum, 6 * t + 3 * half + 3)
                at(eng, b_score_psum, 4 * t)
                src = SB[0][:, :].rearrange("p (j q) -> p j q", q=P)
                eng.activation(qq_e[0:KVC, 4 * half:4 * half + 4, :], src[0:KVC], ACT.Copy)
                eng.activation(qq_o[KVC:2 * KVC, 4 * half:4 * half + 4, :], src[KVC:2 * KVC],
                               ACT.Copy).then_inc(b_nope, 1)

            def b_exps(t, g):
                eng.wait_ge(b_score, 4 * t + g + 1)
                at(eng, b_pT_psum, 4 * t)
                for j in range(4):
                    h = 4 * g + j
                    ins = eng.activation(prob_b[:, h, :], score_b[:, h, :], ACT.Exp, bias=negmax_b[:, h:h + 1],
                                         accum_out=den_b[:, h:h + 1])
                ins.then_inc(b_prob, 1)

            def b_prob_copy(t, g):
                eng.wait_ge(b_pT_psum, 4 * t + g + 1)
                at(eng, b_av, 2 * t)
                eng.activation(prob_bT[:, 4 * g:4 * g + 4, :], SB[(2 + g) % 3][:, :].rearrange(
                    "p (j q) -> p j q", q=P), ACT.Copy).then_inc(b_pT, 1)

            def b_att_copy(t, half):
                eng.wait_ge(b_av, 2 * t + half + 1)
                at(eng, b_wo, t)
                eng.activation(att_bT[:, 4 * half:4 * half + 4, :], SB[half][:, :].rearrange(
                    "p (j q) -> p j q", q=P), ACT.Copy).then_inc(b_attT, 1)

            def c_input_copy(t):
                eng.wait_ge(b_x2, t + 1)
                at(eng, c_sent, 16 * TOPK * t)
                at(eng, y_out_s, 32 * t)
                eng.activation(row[:, 0:CM], x2[:, :], ACT.Copy).then_inc(c_row, 1)
                eng.wait_ge(c_xT_psum, t + 1)
                at(eng, c_gu_psum, 2 * t)
                eng.activation(x2T[:, :, :], SC[:, 0:CM].rearrange("p (c q) -> p c q", q=P),
                               ACT.Copy).then_inc(c_xT, 1)

            def c_router_exp(t):
                eng.wait_ge(c_logit, t + 1)
                eng.wait_ge(c_top, t + 1)
                eng.activation(gexp[:, :], logit[:, :], ACT.Exp, bias=neg_top[:, :],
                               accum_out=gsum[:, :]).then_inc(c_gexp, 1)

            def c_gate_exp(t, half):
                eng.wait_ge(c_gu_psum, 2 * t + half + 1)
                at(eng, c_mid, 2 * t)
                eng.activation(sh_exp[:, half, :], SC[:, 0:SH], ACT.Tanh, scale=0.5).then_inc(c_gexp2, 1)

            def c_mid_copy(t):
                eng.wait_ge(c_midT_psum, t + 1)
                at(eng, c_down, t)
                eng.activation(sh_midT[:, 0:2, :], SC[:, 0:2 * P].rearrange("p (c q) -> p c q", q=P), ACT.Copy)
                eng.activation(sh_midT[0:SI - 2 * P, 2, :], SC[0:SI - 2 * P, 2 * P:3 * P],
                               ACT.Copy).then_inc(c_midT, 1)

            def copy_wqk():
                for b in range(2):
                    eng.wait_ge(wqk_psum, b + 1)
                    eng.activation(wqk[:, 512 * b:512 * b + 512], bank[4 + b][0:QC, :], ACT.Copy).then_inc(wqk_sb, 1)

            def copy_wvo():
                for n, b in enumerate((6, 7, 4, 5)):
                    eng.wait_ge(wvo_psum, n + 1)
                    eng.activation(wvo[:, 2 * n:2 * n + 2, :], bank[b][:, :].rearrange("p (j o) -> p j o", o=CM),
                                   ACT.Copy).then_inc(wvo_sb, 1)

            for dst, name in ((cos_a, "cos_a"), (sin_a, "sin_a"), (ident, "ident"), (cos_b, "cos_b"),
                              (sin_b, "sin_b"), (key_pos, "key_pos"), (slot_base, "slot_base"),
                              (expert_no, "expert_no"), (earlier, "earlier")):
                eng.dma_start(dst[:, :], io[name]).then_inc(const_in, 16)
            eng.dma_start(row[:, ROWW - 1:ROWW].bitcast(I32), io["token_no"]).then_inc(const_in, 16)
            eng.wait_ge(dve_setup, 4)

            def step(a, b, c):
                if b is not None:
                    b_input_copy(b)
                if a is not None:
                    a_value_copy(a)
                if b is None and c is None:
                    copy_wqk()
                if b is not None:
                    b_latent_copy(b)
                if c is not None:
                    c_input_copy(c)
                if b is not None:
                    b_nope_copy(b, 0)
                if c is not None:
                    c_router_exp(c)
                if b is not None:
                    b_nope_copy(b, 1)
                    b_exps(b, 0)
                if c is not None:
                    c_gate_exp(c, 0)
                if a is not None:
                    a_q_copy(a)
                    a_k_copy(a)
                if b is not None:
                    b_exps(b, 1)
                    b_exps(b, 2)
                    b_prob_copy(b, 0)
                    b_exps(b, 3)
                    b_prob_copy(b, 1)
                if a is not None:
                    a_exps(a)
                if b is not None:
                    b_prob_copy(b, 2)
                if c is not None:
                    c_gate_exp(c, 1)
                if b is not None:
                    b_prob_copy(b, 3)
                if b is None and c is None:
                    copy_wvo()
                if a is not None:
                    a_raw_copy(a)
                if b is not None:
                    b_att_copy(b, 0)
                    b_att_copy(b, 1)
                if a is not None:
                    a_att_copy(a)
                if c is not None:
                    c_mid_copy(c)

            run_steps(step, eng)

            def load_down(i, k):
                e = D_RING * i + k
                if not isinstance(i, int) or i:
                    eng.wait_ge(d_down, e - D_RING + 1)
                eng.dma_start(ewd[:, k, :, :], io["ewd"][bass.ds(e, 1), :, :].rearrange(
                    "e (c p) n -> p (e c) n", c=2)).then_inc(ewd_in[k], 16)

            def expert(i, k):
                if have(i, k, 0):
                    load_down(i, k)
                    e = D_RING * i + k
                    eng.wait_ge(d_xT_psum, e + 1)
                    at(eng, d_gu_psum, two_ago(e, i, 0))
                    eng.activation(exT[:, k % 2, :, :], bank[k % 2][:, 0:CM].rearrange("p (c q) -> p c q", q=P),
                                   ACT.Copy).then_inc(d_xT, 1)
                if have(i, k, 1):
                    e, s = D_RING * i + k - 1, (k - 1) % D_RING
                    eng.wait_ge(d_gu_psum, e + 1)
                    at(eng, d_mid, two_ago(e, i, 1 - k))
                    eng.activation(e_exp[:, s % 2, :], bank[2 + s % 2][:, 0:EI], ACT.Tanh, scale=0.5)\
                       .then_inc(d_exp, 1)
                if have(i, k, 2):
                    e, s = D_RING * i + k - 2, (k - 2) % D_RING
                    eng.wait_ge(d_midT_psum, e + 1)
                    at(eng, d_down, two_ago(e, i, 2 - k))
                    eng.activation(e_midT[:, s % 2, :, :], bank[4 + s % 2][0:EI // 2, 0:2 * P].rearrange(
                        "p (c q) -> p c q", q=P), ACT.Copy).then_inc(d_midT, 1)

            run_experts(expert, eng)

        @block.vector
        def _(eng):
            def a_rope(t):
                eng.wait_ge(a_qk_psum, t + 1)
                then = link(eng, chain_a_rope, 3 * t)
                pairs = "p (i two) -> p i two"
                eng.tensor_tensor(qk_cos[:, :], SA[0][:, :], cos_a[:, :], ALU.mult)
                src = SA[0][:, :].rearrange(pairs, two=2)
                dst = qk_sin[:, :].rearrange(pairs, two=2)
                tab = sin_a[:, :].rearrange(pairs, two=2)
                eng.tensor_tensor(dst[:, :, 0:1], src[:, :, 1:2], tab[:, :, 0:1], ALU.mult)
                then(eng.tensor_tensor(dst[:, :, 1:2], src[:, :, 0:1], tab[:, :, 1:2], ALU.mult))
                then(eng.tensor_tensor(qk_rot[:, :], qk_cos[:, :], qk_sin[:, :], ALU.add))
                then(eng.tensor_tensor(qk_sq[:, :], qk_rot[:, :], qk_rot[:, :], ALU.mult))
                at(eng, a_rs, t)
                eng.tensor_reduce(qk_ss[:, :], qk_sq[:, :].rearrange("p (i d) -> p i d", d=HD), AX.X, ALU.add)\
                   .then_inc(a_ss, 1)

            def a_scale(t):
                eng.wait_ge(a_rs, t + 1)
                at(eng, a_tr, 2 * t)
                eng.tensor_tensor(qk_pad[:, :, 0:HD], qk_rot[:, :].rearrange("p (i d) -> p i d", d=HD),
                                  qk_rs[:, :, None].to_broadcast([P, 2 * H, HD]), ALU.mult).then_inc(a_qk, 1)

            def a_normalise(t):
                eng.wait_ge(a_raw_turned, t + 1)
                then = link(eng, chain_a_att, t)
                heads = SA[2][:, :].rearrange("p (h d) -> p h d", d=VW)
                then(eng.reciprocal(rec_a[:, :, None], heads[:, :, HD:HD + 1]))
                at(eng, a_attT_psum, t)
                eng.tensor_tensor(att_a[:, :].rearrange("p (h d) -> p h d", d=HD), heads[:, :, 0:HD],
                                  rec_a[:, :, None].to_broadcast([P, H, HD]), ALU.mult).then_inc(a_att, 1)

            def norm(which, res, out, then, var_s, rstd_s, t, done_s):
                then(eng.bn_stats(stats[which][:, :], res[:, :]))
                alone(eng)
                eng.bn_aggr(mv[which][:, :], stats[which][:, :]).then_inc(var_s, 1)
                eng.wait_ge(rstd_s, t + 1)
                eng.tensor_scalar(out[:, :], res[:, :], mv[which][:, 0:1], rstd[which][:, :],
                                  ALU.subtract, ALU.mult).then_inc(done_s, 1)

            def a_residual(t):
                eng.wait_ge(a_wo, t + 1)
                eng.wait_ge(x_in_s, 16 * (t + 1))
                eng.tensor_tensor(res_a[:, :], SA[1][:, 0:CM], x_in[:, :], ALU.add).then_inc(a_res, 1)
                eng.wait_ge(a_res, t + 1)
                at(eng, b_keep, t)
                at(eng, b_in_psum, t)
                norm("a", res_a, x1, link(eng, chain_a_norm, t), a_var, a_rstd, t, a_x1)

            def b_rotate_keys(t):
                eng.wait_ge(b_qc, t + 1)
                at(eng, b_score_psum, 4 * t)
                then = link(eng, chain_b_latent, t)
                eng.tensor_tensor(kr_cos[:, :], SB[0][:, P:2 * P], cos_b[:, :], ALU.mult)
                then(eng.tensor_tensor(kr_sin[:, :], SB[0][:, 2 * P:3 * P], sin_b[:, :], ALU.mult))
                eng.tensor_tensor(kk_e[R:2 * R, :], kr_cos[R:2 * R, :], kr_sin[R:2 * R, :], ALU.add)
                eng.tensor_tensor(kk_o[0:R, :], kr_cos[0:R, :], kr_sin[0:R, :], ALU.add).then_inc(b_keys, 1)

            def b_rotate(t, half):
                at(eng, b_rope, 4 * t)
                for use, dst, tab, bk in ((0, qr_cos, cos_b, SB[1]), (1, qr_sin, sin_b, SB[2])):
                    eng.wait_ge(b_q_psum, 6 * t + 3 * half + use + 1)
                    eng.tensor_tensor(dst[:, half, :].rearrange("p (j q) -> p j q", q=P),
                                      bk[:, :].rearrange("p (j q) -> p j q", q=P),
                                      tab[:, None, :].to_broadcast([P, 4, P]), ALU.mult).then_inc(b_rot, 1)

            def b_rotate_add(t, half):
                eng.wait_ge(b_rot, 4 * t + 2 * half + 2)
                at(eng, b_score_psum, 4 * t)
                for dst, rows in ((qq_e, slice(R, 2 * R)), (qq_o, slice(0, R))):
                    eng.tensor_tensor(dst[rows, 4 * half:4 * half + 4, :].rearrange("p j q -> p (j q)"),
                                      qr_cos[rows, half, :], qr_sin[rows, half, :], ALU.add).then_inc(b_rope, 1)

            def b_window(t):
                eng.wait_ge(seg_in, 16 * (t + 1))
                at(eng, b_score, 4 * t)
                then = link(eng, chain_b_mask, 3 * t)
                then(eng.tensor_copy(seg_f[:, :], seg[:, :]))
                then(eng.tensor_scalar(mask_d[:, :], key_pos[:, :], seg_f[:, :], None, ALU.subtract))
                then(eng.tensor_scalar(mask_b[:, :], mask_d[:, :], 0.0, NEG, ALU.is_gt, ALU.mult))
                eng.tensor_scalar(mask_d[:, :], mask_d[:, :], -float(LOOKBACK), NEG, ALU.is_lt, ALU.mult)\
                   .then_inc(b_mask, 1)
                eng.wait_ge(b_mask, 2 * t + 1)
                eng.tensor_tensor(mask_b[:, :], mask_b[:, :], mask_d[:, :], ALU.add).then_inc(b_mask, 1)
                eng.wait_ge(b_mask, 2 * t + 2)

            def b_maxima(t, g):
                eng.wait_ge(b_score_psum, 4 * t + g + 1)
                at(eng, b_prob, 4 * t)
                then = link(eng, chain_b_max, 4 * t + g)
                alone(eng)
                for j in range(4):
                    h = 4 * g + j
                    ins = eng.tensor_tensor_reduce(score_b[:, h, :], SB[(1 + g) % 3][:, P * j:P * j + P],
                                                   mask_b[:, :], SCALE_B, -3.0e38, ALU.add, ALU.max,
                                                   max_b[:, h:h + 1])
                then(ins)
                eng.tensor_scalar(negmax_b[:, 4 * g:4 * g + 4], max_b[:, 4 * g:4 * g + 4], -1.0, None,
                                  ALU.mult).then_inc(b_score, 1)

            def b_weigh(t, g):
                eng.wait_ge(b_prob, 4 * t + g + 1)
                heads = slice(4 * g, 4 * g + 4)
                link(eng, chain_b_att, 4 * t + g)(eng.reciprocal(rec_b[:, heads], den_b[:, heads]))
                eng.tensor_tensor(prob_b[:, heads, :], prob_b[:, heads, :],
                                  rec_b[:, heads, None].to_broadcast([P, 4, P]), ALU.mult).then_inc(b_weights, 1)

            def b_residual(t):
                eng.wait_ge(b_wo, t + 1)
                eng.wait_ge(b_keep, t + 1)
                eng.tensor_tensor(res_b[:, :], SB[0][:, 0:CM], x1_keep[:, :], ALU.add).then_inc(b_res, 1)
                eng.wait_ge(b_res, t + 1)
                at(eng, c_row, t)
                at(eng, c_xT_psum, t)
                norm("b", res_b, x2, link(eng, chain_b_norm, t), b_var, b_rstd, t, b_x2)

            def c_logits(t):
                eng.wait_ge(c_logit_psum, t + 1)
                at(eng, c_gexp, t)
                eng.tensor_copy(logit[:, :], SC[:, 0:E]).then_inc(c_logit, 1)
                eng.wait_ge(c_logit, t + 1)
                eng.tensor_reduce(neg_top[:, :], logit[:, :], AX.X, ALU.max, negate=True).then_inc(c_top, 1)

            def c_choose(t):
                eng.wait_ge(c_gexp, t + 1)
                then = link(eng, chain_c_choose, 14 * t)
                then(eng.reciprocal(grec[:, :], gsum[:, :]))
                then(eng.tensor_scalar(gprob[:, :], gexp[:, :], grec[:, :], None, ALU.mult))
                alone(eng)
                then(eng.max(top8[:, :], gprob[:, :]))
                alone(eng)
                then(eng.max_index(top_no[:, :], top8[:, :], gprob[:, :]))
                then(eng.tensor_copy(top_nof[:, :], top_no[:, :]))
                then(eng.tensor_scalar(chosen[:, 0, :], expert_no[:, :], top_nof[:, 0:1], None, ALU.is_equal))
                for k in range(1, TOPK):
                    then(eng.scalar_tensor_tensor(chosen[:, k % 2, :], expert_no[:, :], top_nof[:, k:k + 1],
                                                  chosen[:, (k - 1) % 2, :], ALU.is_equal, ALU.add))
                mask = chosen[:, (TOPK - 1) % 2, :]
                at(eng, c_rank, t)
                eng.tensor_copy(chosen_bf[:, :], mask).then_inc(c_chosen, 1)
                then(eng.tensor_tensor(wsel[:, :], gprob[:, :], mask, ALU.mult))
                then(eng.tensor_reduce(wsum[:, 0:1], wsel[:, :], AX.X, ALU.add))
                then(eng.tensor_scalar(wsum[:, 1:2], wsum[:, 0:1], 1e-20, None, ALU.add))
                then(eng.reciprocal(wrec[:, :], wsum[:, 1:2]))
                at(eng, c_sent, 16 * TOPK * t)
                then(eng.tensor_scalar(row[:, CM:CM + E], wsel[:, :], wrec[:, :], None, ALU.mult))
                eng.tensor_scalar(row[:, ROWW - 1:ROWW].bitcast(I32), row[:, ROWW - 1:ROWW].bitcast(I32),
                                  float(P), None, ALU.add).then_inc(c_row, 1)

            def c_slots(t):
                eng.wait_ge(c_rank, t + 1)
                then = link(eng, chain_c_slot, 3 * t)
                eng.tensor_tensor(slot_u[:, :], slot_base[:, :], SC[:, 0:E], ALU.subtract)
                then(eng.scalar_tensor_tensor(slot_v[:, :], SC[:, 0:E], float(CAP), chosen[:, (TOPK - 1) % 2, :],
                                              ALU.is_lt, ALU.mult))
                eng.tensor_tensor(seen_bf[:, :], seen_bf[:, :], chosen_bf[:, :], ALU.add)
                then(eng.tensor_tensor(slot_s[:, :], slot_u[:, :], slot_v[:, :], ALU.mult))
                alone(eng)
                then(eng.max(slot8[:, :], slot_s[:, :]))
                at(eng, c_sent, 16 * TOPK * t)
                eng.tensor_scalar(slot_no[:, :], slot8[:, :], -1.0, float(NOSLOT), ALU.mult, ALU.add)\
                   .then_inc(c_slot, 1)

            def c_middle(t, half):
                eng.wait_ge(c_gexp2, 2 * t + half + 1)
                then = link(eng, chain_c_mid, 2 * t + half)
                then(eng.scalar_tensor_tensor(sh_act[:, half, :], sh_exp[:, half, :], 1.0, SC[:, 0:SH],
                                              ALU.add, ALU.mult))
                at(eng, c_midT_psum, t)
                eng.scalar_tensor_tensor(sh_mid[:, SH * half:SH * half + SH], sh_act[:, half, :], 0.5,
                                         SC[:, SH:2 * SH], ALU.mult, ALU.mult).then_inc(c_mid, 1)

            def c_result(t):
                eng.wait_ge(c_down, t + 1)
                at(eng, y_out_s, 32 * t)
                eng.tensor_copy(y_sb[:, :], SC[:, 0:CM]).then_inc(c_y, 1)

            for tile in (qk_pad, v_a, seen_bf):
                eng.memset(tile[:], 0.0).then_inc(dve_setup, 1)
            eng.wait_ge(dve_setup, 3)
            eng.memset(v_a[:, :, HD:HD + 1], 1.0)
            eng.memset(ones_bf[:, :], 1.0).then_inc(dve_setup, 1)
            eng.wait_ge(dve_setup, 4)
            eng.wait_ge(const_in, 16 * 10)

            def step(a, b, c):
                if a is not None:
                    a_rope(a)
                if b is not None:
                    b_rotate_keys(b)
                    b_window(b)
                    b_rotate(b, 0)
                if c is not None:
                    c_logits(c)
                if b is not None:
                    b_rotate_add(b, 0)
                    b_rotate(b, 1)
                    b_maxima(b, 0)
                if a is not None:
                    a_scale(a)
                if b is not None:
                    b_rotate_add(b, 1)
                    b_maxima(b, 1)
                if c is not None:
                    c_middle(c, 0)
                if b is not None:
                    b_weigh(b, 0)
                    b_maxima(b, 2)
                    b_weigh(b, 1)
                    b_maxima(b, 3)
                    b_weigh(b, 2)
                    b_weigh(b, 3)
                if c is not None:
                    c_choose(c)
                    c_middle(c, 1)
                if a is not None:
                    a_normalise(a)
                if c is not None:
                    c_slots(c)
                if a is not None:
                    a_residual(a)
                if b is not None:
                    b_residual(b)
                if c is not None:
                    c_result(c)

            run_steps(step, eng)

            def expert(i, k):
                if have(i, k, 1):
                    e, s = D_RING * i + k - 1, (k - 1) % D_RING
                    b = bank[2 + s % 2]
                    eng.wait_ge(d_exp, e + 1)
                    then = link(eng, chain_d_mid, e)
                    then(eng.scalar_tensor_tensor(e_act[:, s % 2, :], e_exp[:, s % 2, :], 1.0, b[:, 0:EI],
                                                  ALU.add, ALU.mult))
                    at(eng, d_midT_psum, two_ago(e, i, 1 - k))
                    eng.scalar_tensor_tensor(e_mid[:, s % 2, :], e_act[:, s % 2, :], 0.5, b[:, EI:2 * EI],
                                             ALU.mult, ALU.mult).then_inc(d_mid, 1)
                if have(i, k, 1):
                    e, s = D_RING * i + k - 1, (k - 1) % D_RING
                    eng.wait_ge(ex_in[s], 16 * (i + 1 if k >= 1 else i))
                    at(eng, d_added[s % 2], 16 * earlier_pairs(i, k))
                    eng.tensor_copy(etok[:, s:s + 1], ex[:, s, ROWW - 1:ROWW].bitcast(U32))
                    eng.tensor_copy(e_weight[:, s:s + 1], ex[:, s, bass.ds(e + CM, 1)]).then_inc(d_copied, 1)
                if have(i, k, 3):
                    e, s = D_RING * i + k - 3, (k - 3) % D_RING
                    eng.wait_ge(d_copied, e + 1)
                    eng.wait_ge(d_down, e + 1)
                    at(eng, d_added[s % 2], 16 * earlier_pairs(i, k))
                    eng.tensor_scalar(e_out[:, s % 2, :], bank[6 + s % 2][:, 0:CM], e_weight[:, s:s + 1],
                                      None, ALU.mult).then_inc(d_out, 1)

            run_experts(expert, eng)

            for g in range(4):
                eng.wait_ge(yl_in[g], 32)
                then = link(eng, chain_e_norm, 2 * g)
                fin = fin_in[0][g]
                then(eng.tensor_tensor(fin, fin, fin_in[1][g], ALU.add))
                for j in range(4):
                    ins = eng.bn_stats(fin_stats[:, j, :], fin[:, CM * j:CM * j + CM])
                then(ins)
                at(eng, e_done, g)
                for j in range(4):
                    ins = eng.bn_aggr(fin_mv[:, j, :], fin_stats[:, j, :])
                ins.then_inc(e_var, 1)
                eng.wait_ge(e_rstd, g + 1)
                for j in range(4):
                    ins = eng.tensor_scalar(fin_out[g][:, CM * j:CM * j + CM], fin[:, CM * j:CM * j + CM],
                                            fin_mv[:, j, 0:1], fin_rstd[:, j:j + 1], ALU.subtract, ALU.mult)
                ins.then_inc(e_done, 1)

        @block.gpsimd
        def _(eng):
            def root(var_ap, eps_tile, out, chain, base, done_s, eps, scale=None):
                alone(eng)
                if scale is None:
                    ins = eng.tensor_scalar(eps_tile, var_ap, eps, None, ALU.add)
                else:
                    ins = eng.tensor_scalar(eps_tile, var_ap, scale, eps, ALU.mult, ALU.add)
                link(eng, chain, base)(ins)
                n = eps_tile.shape[1]
                eng.tensor_tensor(out, eps_tile, minus_half[:, 0:n], ALU.pow).then_inc(done_s, 1)

            def b_copy(t):
                eng.wait_ge(a_x1, t + 1)
                at(eng, b_res, t)
                alone(eng)
                eng.tensor_copy(x1_keep[:, :], x1[:, :]).then_inc(b_keep, 1)

            def a_root(t):
                eng.wait_ge(a_ss, t + 1)
                at(eng, a_qk, t)
                root(qk_ss[:, :], qk_ms[:, :], qk_rs[:, :], chain_a_rs, t, a_rs, RMS_EPS, 1.0 / HD)

            def a_causal(t):
                for j in range(4):
                    eng.wait_ge(a_exp, 4 * t + j + 1)
                    alone(eng)
                    pj = prob_a[:, 4 * j:4 * j + 4, :]
                    eng.affine_select(out=pj, in_=pj, compare_op=ALU.is_ge, fill=zero, base=0,
                                      pattern=[[0, 4], [1, P]], channel_multiplier=-1).then_inc(a_masked, 1)

            def a_norm_root(t):
                eng.wait_ge(a_var, t + 1)
                at(eng, a_x1, t)
                root(mv["a"][:, 1:2], var_eps["a"][:, :], rstd["a"][:, :], chain_a_rstd, t, a_rstd, LN_EPS)

            def b_norm_root(t):
                eng.wait_ge(b_var, t + 1)
                at(eng, b_x2, t)
                root(mv["b"][:, 1:2], var_eps["b"][:, :], rstd["b"][:, :], chain_b_rstd, t, b_rstd, LN_EPS)

            def c_send(t):
                eng.wait_ge(c_slot, t + 1)
                eng.wait_ge(c_row, 2 * t + 2)
                if isinstance(t, int) and t == 0:
                    eng.wait_ge(zeros_out, 16 * (E + 2))
                alone(eng)
                for k in range(TOPK):
                    eng.indirect_dma_start(
                        out=slots_dram[:, :], out_offset=bass.IndirectOffsetOnAxis(ap=slot_no[:, k:k + 1], axis=0),
                        in_=row[:, :], in_offset=None, bounds_check=last_slot, oob_is_err=False)\
                       .then_inc(c_sent, 16)

            zero = eng.to_reg(0.0)
            last_slot, last_row = eng.to_reg(E * CAP - 1), eng.to_reg(NTOK + P - 1)
            eng.memset(ex[:, :, :], 0.0).then_inc(pool_zeros, 1)
            eng.memset(minus_half[:, :], -0.5).then_inc(pool_zeros, 1)
            eng.wait_ge(pool_zeros, 2)

            def step(a, b, c):
                if b is not None:
                    b_copy(b)
                if a is not None:
                    a_root(a)
                    a_causal(a)
                if c is not None:
                    c_send(c)
                if a is not None:
                    a_norm_root(a)
                if b is not None:
                    b_norm_root(b)

            run_steps(step, eng)

            def expert(i, k):
                if have(i, k, 3):
                    e, s = D_RING * i + k - 3, (k - 3) % D_RING
                    eng.wait_ge(d_out, e + 1)
                    at(eng, d_added[s % 2], 16 * earlier_pairs(i, k))
                    alone(eng)
                    eng.indirect_dma_start(
                        out=y_dram[s % 2][:, :],
                        out_offset=bass.IndirectOffsetOnAxis(ap=etok[:, s:s + 1], axis=0),
                        in_=e_out[:, s % 2, :], in_offset=None, bounds_check=last_row, oob_is_err=True,
                        compute_op=ALU.add).then_inc(d_added[s % 2], 16)

            eng.wait_ge(y_out_s, 32 * TILES)
            run_experts(expert, eng)
            for g in range(4):
                eng.wait_ge(e_var, g + 1)
                root(fin_mv[:, :, 1], fin_var[:, :], fin_rstd[:, :], chain_e_rstd, g, e_rstd, LN_EPS)


def _tables():
    pos = np.arange(P, dtype=np.float32)
    inv_a = (1.0 / np.float32(10000.0) ** (np.arange(0, HD, 2, dtype=np.float32) / np.float32(HD))).astype(np.float32)
    ang_a = np.repeat(pos[:, None] * inv_a[None, :], 2, axis=1)
    sign_a = np.tile(np.array([-1, 1], np.float32), HD // 2)
    half = R // 2
    inv_b = (1.0 / np.float32(10000.0) ** (np.arange(half, dtype=np.float32) / np.float32(half))).astype(np.float32)
    ang_b = np.tile((pos[:, None] * inv_b[None, :]).T, (4, 1))
    sign_b = np.tile(np.repeat(np.array([-1, 1], np.float32), half), 2)[:, None]
    p = np.arange(P)
    return {
        "ident": np.eye(P, dtype=np.float32),
        "cos_a": np.tile(np.cos(ang_a), (1, 2 * H)).astype(np.float32),
        "sin_a": np.tile(np.sin(ang_a) * sign_a, (1, 2 * H)).astype(np.float32),
        "cos_b": np.cos(ang_b).astype(np.float32),
        "sin_b": (np.sin(ang_b) * sign_b).astype(np.float32),
        "key_pos": np.tile(p.astype(np.float32), (P, 1)),
        "slot_base": np.tile((NOSLOT - CAP * np.arange(E)).astype(np.float32), (P, 1)),
        "expert_no": np.tile(np.arange(E, dtype=np.float32), (P, 1)),
        "earlier": (p[:, None] < p[None, :]).astype(mybir.dt.np(BF16)),
        "token_no": (p - P).astype(np.int32)[:, None],
        "empty_no": (NTOK + p).astype(np.int32)[:, None],
    }


def _layouts(i):
    T = np.ascontiguousarray
    wqr = i["L0_xattn_W_qr"].reshape(QC, H // 2, 2, R)[:, :, ::-1, :]
    swapped = np.concatenate([wqr[..., R // 2:], wqr[..., :R // 2]], axis=-1)
    wkr = i["L0_xattn_W_kr"]
    wkr_s = np.concatenate([wkr[:, R // 2:], wkr[:, :R // 2]], axis=1)
    g, u = i["L0_ffn_sw_gate"], i["L0_ffn_sw_up"]
    return {
        "x": T(i["x"]),
        "xT": T(i["x"].transpose(0, 2, 1)),
        "ctxT": T(i["ctx_2048"].transpose(0, 2, 1)),
        "seg": T(i["itok_BxS_0_1023"]),
        "wqkvT": T(i["L0_attn_W_qkv"].T),
        "woT": T(i["L0_attn_W_o"].T),
        "wkvc2": T(np.concatenate([i["L0_xattn_W_kvc"]] * 2, axis=1)),
        "wdq": T(i["L0_xattn_W_dq"]),
        "wkr2": T(np.concatenate([wkr, wkr, wkr_s, wkr_s], axis=1)),
        "wqr": T(np.concatenate([wqr.reshape(QC, H * R), swapped.reshape(QC, H * R)], axis=1)),
        "uqT": T(i["L0_xattn_W_uq"].T),
        "ukT": T(i["L0_xattn_W_uk"].T),
        "uvT": T(i["L0_xattn_W_uv"].T),
        "wox": T(i["L0_xattn_W_o"]),
        "wgateT": T(i["L0_ffn_gate_w"].T),
        "wsh": T(np.concatenate([g[:, :SH], u[:, :SH], g[:, SH:], u[:, SH:]], axis=1)),
        "wshd": T(i["L0_ffn_sw_down"]),
        "ew": T(np.concatenate([i["L0_ffn_w_gate"], i["L0_ffn_w_up"]], axis=2)),
        "ewd": T(i["L0_ffn_w_down"]),
    }


def kernel(**inputs):
    import concourse.bacc as bacc
    from concourse.bass_utils import run_bass_kernel_spmd

    nc = bacc.Bacc("TRN2", target_bir_lowering=False, num_devices=1)
    arrays, io = {}, {}
    for name, a in {**_layouts({k: np.asarray(v) for k, v in inputs.items()}), **_tables()}.items():
        arrays[f"in_{name}"] = a
        io[name] = nc.dram_tensor(f"in_{name}", a.shape, mybir.dt.from_np(a.dtype), kind="ExternalInput").ap()
    y = nc.dram_tensor("out_y", (TILES, P, CM), F32, kind="ExternalOutput").ap()
    layer(nc, io, y)
    r = run_bass_kernel_spmd(nc, [arrays], core_ids=[0])
    return r.results[0]["out_y"]
```

```python
from contextlib import ExitStack

import numpy as np

import concourse.bass as bass
from concourse import mybir

ALU = mybir.AluOpType
ACT = mybir.ActivationFunctionType
AX = mybir.AxisListType
F32 = mybir.dt.float32
BF16 = mybir.dt.bfloat16
I32 = mybir.dt.int32
U32 = mybir.dt.uint32

P = 128
TILES, CM = 16, 256
CC = CM // P
H, HD = 16, 16
VW = 32
KVC, QC, R = 64, 96, 64
XHD = 128
LOOKBACK = 8
NEG = -1e30
E, TOPK, EI, CAP = 16, 4, 176, 128
SI = 352
SH = SI // 2
ROWW = CM + E + 1
NTOK = TILES * P
SCALE_A = HD ** -0.5
SCALE_B = float(np.float32(1.0) / np.sqrt(XHD + R).astype(np.float32))
RMS_EPS = 1.1920929e-07
LN_EPS = 1e-5
NOSLOT = 4096
D_RING = 4
FJ = 2
FG = NTOK // (P * FJ)


def layer(nc, io, y_out):
    ctx = ExitStack()
    with ctx:
        def sb(name, shape, dt=F32):
            return ctx.enter_context(nc.sbuf_tensor(name, shape, dt))

        def sem(name):
            return ctx.enter_context(nc.semaphore(name))

        slots_dram = nc.dram_tensor("slots_dram", (E * CAP, ROWW), F32, kind="Internal").ap()
        y_dram = [nc.dram_tensor(f"y{n}_dram", (NTOK + P, CM), F32, kind="Internal").ap() for n in range(2)]

        ident = sb("ident", [P, P])
        cos_a = sb("cos_a", [P, 2 * CM])
        sin_a = sb("sin_a", [P, 2 * CM])
        cos_b = sb("cos_b", [P, P])
        sin_b = sb("sin_b", [P, P])
        key_pos = sb("key_pos", [P, P])
        slot_base = sb("slot_base", [P, E])
        expert_no = sb("expert_no", [P, E])
        minus_half = sb("minus_half", [P, 2 * H])
        earlier = sb("earlier", [P, P], BF16)
        ones_bf = sb("ones_bf", [P, P], BF16)
        wqkv = sb("wqkv", [P, CC, 3 * CM])
        wo = sb("wo", [P, CC, CM])
        wkvc2 = sb("wkvc2", [P, CC, 2 * KVC])
        wdq = sb("wdq", [P, CC, QC])
        wkr2 = sb("wkr2", [KVC, 2, 2 * R])
        wqr = sb("wqr", [QC, 2, H * R])
        wqk = sb("wqk", [QC, H * KVC])
        wvo = sb("wvo", [P, H // 2, CM])
        wgate = sb("wgate", [P, CC, E])
        wsh = sb("wsh", [P, CC, 2 * SI])
        wshd = sb("wshd", [P, 3, CM])

        xT = sb("xT", [P, CC, P])
        x_in = sb("x_in", [P, CM])
        qk_cos = sb("qk_cos", [P, 2 * CM])
        qk_sin = sb("qk_sin", [P, 2 * CM])
        qk_rot = sb("qk_rot", [P, 2 * CM])
        qk_sq = sb("qk_sq", [P, 2 * CM])
        qk_ss = sb("qk_ss", [P, 2 * H])
        qk_ms = sb("qk_ms", [P, 2 * H])
        qk_rs = sb("qk_rs", [P, 2 * H])
        qk_pad = sb("qk_pad", [P, 2 * H, 32])
        v_a = sb("v_a", [P, H, VW])
        qT = sb("qT", [P, 4, P])
        kT = sb("kT", [P, 4, P])
        prob_a = sb("prob_a", [P, H, P])
        rec_a = sb("rec_a", [P, H])
        att_raw = sb("att_raw", [P, 4, P])
        att_a = sb("att_a", [P, CM])
        att_aT = sb("att_aT", [P, CC, P])
        res_a = sb("res_a", [P, CM])
        x1 = sb("x1", [P, CM])

        ctxT = sb("ctxT", [P, CC, P])
        seg = sb("seg", [P, 1], I32)
        seg_f = sb("seg_f", [P, 1])
        mask_d = sb("mask_d", [P, P])
        mask_b = sb("mask_b", [P, P])
        x1_keep = sb("x1_keep", [P, CM])
        x1T = sb("x1T", [P, CC, P])
        kk_e = sb("kk_e", [P, P])
        kk_o = sb("kk_o", [P, P])
        kr_cos = sb("kr_cos", [P, P])
        kr_sin = sb("kr_sin", [P, P])
        qcT = sb("qcT", [QC, P])
        v_b = sb("v_b", [P, KVC])
        qr_cos = sb("qr_cos", [P, 2, 4 * P])
        qr_sin = sb("qr_sin", [P, 2, 4 * P])
        qq_e = sb("qq_e", [P, H // 2, P])
        qq_o = sb("qq_o", [P, H // 2, P])
        score_b = sb("score_b", [P, H, P])
        max_b = sb("max_b", [P, H])
        negmax_b = sb("negmax_b", [P, H])
        prob_b = sb("prob_b", [P, H, P])
        den_b = sb("den_b", [P, H])
        rec_b = sb("rec_b", [P, H])
        prob_bT = sb("prob_bT", [P, H, P])
        att_bT = sb("att_bT", [P, H // 2, P])
        res_b = sb("res_b", [P, CM])
        x2 = sb("x2", [P, CM])

        stats = {s: sb(f"stats_{s}", [P, 6]) for s in "abe"}
        mv = {s: sb(f"mv_{s}", [P, 2]) for s in "abe"}
        var_eps = {s: sb(f"var_eps_{s}", [P, 1]) for s in "abe"}
        rstd = {s: sb(f"rstd_{s}", [P, 1]) for s in "abe"}

        row = sb("row", [P, ROWW])
        x2T = sb("x2T", [P, CC, P])
        logit = sb("logit", [P, E])
        neg_top = sb("neg_top", [P, 1])
        gexp = sb("gexp", [P, E])
        gsum = sb("gsum", [P, 1])
        grec = sb("grec", [P, 1])
        gprob = sb("gprob", [P, E])
        top8 = sb("top8", [P, 8])
        top_no = sb("top_no", [P, 8], U32)
        top_nof = sb("top_nof", [P, 8])
        matches = sb("matches", [P, E, TOPK])
        chosen = sb("chosen", [P, E])
        chosen_bf = sb("chosen_bf", [P, E], BF16)
        seen_bf = sb("seen_bf", [P, E], BF16)
        wsum = sb("wsum", [P, 2])
        wrec = sb("wrec", [P, 1])
        slot_u = sb("slot_u", [P, E])
        slot_v = sb("slot_v", [P, E])
        slot_s = sb("slot_s", [P, E])
        slot8 = sb("slot8", [P, 8])
        slot_no = sb("slot_no", [P, 8], U32)
        sh_exp = sb("sh_exp", [P, 2, SH])
        sh_act = sb("sh_act", [P, 2, SH])
        sh_mid = sb("sh_mid", [P, SI])
        sh_midT = sb("sh_midT", [P, 3, P])
        y_sb = sb("y_sb", [P, CM])

        ew = sb("ew", [P, D_RING, CC, 2 * EI])
        ewd = sb("ewd", [P, D_RING, 2, CM])
        ex = sb("ex", [P, D_RING, ROWW])
        etok = sb("etok", [P, D_RING], U32)
        e_weight = sb("e_weight", [P, D_RING])
        exT = sb("exT", [P, 2, CC, P])
        e_exp = sb("e_exp", [P, 2, EI])
        e_act = sb("e_act", [P, 2, EI])
        e_mid = sb("e_mid", [P, 2, EI])
        e_midT = sb("e_midT", [EI // 2, 2, 2, P])
        e_out = sb("e_out", [P, 2, CM])
        uqT = score_b[:, 0:12, :].rearrange("p a b -> p (a b)").rearrange("p (h q) -> p h q", q=QC)
        ukT = prob_b[:, 0:8, :].rearrange("p a b -> p (a b)").rearrange("p (h q) -> p h q", q=KVC)
        uvT = ew[:, :, :, :].rearrange("p a b c -> p (a b c)")[:, 0:H * KVC].rearrange("p (h q) -> p h q", q=KVC)
        wox_lo = prob_bT[:, :, :].rearrange("p a b -> p (a b)").rearrange("p (h o) -> p h o", o=CM)
        wox_hi = ewd[:, :, :, :].rearrange("p a b o -> p (a b) o")

        empty_row = ex[:, 0, :]
        def cut(tiles):
            flat = [t[:, :, :].rearrange("p a b -> p (a b)") for t in tiles]
            return [f[:, n:n + FJ * CM] for f in flat for n in range(0, f.shape[1], FJ * CM)]

        fin_in = (cut((score_b, prob_b)), cut((prob_bT, prob_a)))
        fin_out = cut((qq_e, qq_o, qr_cos, qr_sin))
        fin_mv = sb("fin_mv", [P, FG, FJ, 2])
        fin_stats = sb("fin_stats", [P, FG, FJ, 6])
        fin_neg = sb("fin_neg", [P, FG, FJ])
        fin_var = sb("fin_var", [P, FG, FJ])
        fin_rstd = sb("fin_rstd", [P, FG, FJ])
        fin_bias = sb("fin_bias", [P, FG, FJ])

        bank = [ctx.enter_context(nc.psum_tensor(f"bank{i}", [P, 512], F32)) for i in range(8)]
        SA, SB, SC = bank[0:4], bank[4:7], bank[7]

        const_a_in, const_in = sem("const_a_in"), sem("const_in")
        waited = sem("waited")
        wqkv_in, wo_in, wlatent_in, wffn_in = sem("wqkv_in"), sem("wo_in"), sem("wlatent_in"), sem("wffn_in")
        wqk_in, wvo_in = sem("wqk_in"), sem("wvo_in")
        zeros_out = sem("zeros_out")
        dve_setup = sem("dve_setup")
        pool_zeros = sem("pool_zeros")
        empty_in = sem("empty_in")
        wqk_psum = sem("wqk_psum")
        wqk_sb = sem("wqk_sb")
        wvo_psum = sem("wvo_psum")
        wvo_sb = sem("wvo_sb")
        xT_in, x_in_s, ctxT_in, seg_in = sem("xT_in"), sem("x_in_s"), sem("ctxT_in"), sem("seg_in")
        (chain_a_rope, chain_a_att, chain_a_norm, chain_b_latent, chain_b_mask, chain_b_max, chain_b_att,
         chain_b_norm, chain_c_choose, chain_c_slot, chain_c_mid, chain_d_mid, chain_e_norm) = (
            sem(f"chain_{n}") for n in ("a_rope", "a_att", "a_norm", "b_latent", "b_mask", "b_max", "b_att",
                                        "b_norm", "c_choose", "c_slot", "c_mid", "d_mid", "e_norm"))
        chain_a_rs, chain_a_rstd, chain_b_rstd, chain_e_rstd = (
            sem(f"chain_{n}") for n in ("a_rs", "a_rstd", "b_rstd", "e_rstd"))
        a_qk_psum = sem("a_qk_psum")
        a_qkv = sem("a_qkv")
        a_ss = sem("a_ss")
        a_v = sem("a_v")
        a_rs = sem("a_rs")
        a_qk = sem("a_qk")
        a_tr = sem("a_tr")
        a_qT = sem("a_qT")
        a_kT = sem("a_kT")
        a_score = sem("a_score")
        a_exp = sem("a_exp")
        a_masked = sem("a_masked")
        a_av = sem("a_av")
        a_raw = sem("a_raw")
        a_raw_turned = sem("a_raw_turned")
        a_att = sem("a_att")
        a_attT_psum = sem("a_attT_psum")
        a_attT = sem("a_attT")
        a_wo = sem("a_wo")
        a_res = sem("a_res")
        a_var = sem("a_var")
        a_rstd = sem("a_rstd")
        a_x1 = sem("a_x1")
        b_keep = sem("b_keep")
        b_in_psum = sem("b_in_psum")
        b_in = sem("b_in")
        b_qc_psum = sem("b_qc_psum")
        b_qc = sem("b_qc")
        b_keys = sem("b_keys")
        b_v = sem("b_v")
        b_q_psum = sem("b_q_psum")
        b_rot = sem("b_rot")
        b_rope = sem("b_rope")
        b_nope = sem("b_nope")
        b_mask = sem("b_mask")
        b_score_psum = sem("b_score_psum")
        b_score = sem("b_score")
        b_prob = sem("b_prob")
        b_pT_psum = sem("b_pT_psum")
        b_weights = sem("b_weights")
        b_pT = sem("b_pT")
        b_av = sem("b_av")
        b_attT = sem("b_attT")
        b_wo = sem("b_wo")
        b_res = sem("b_res")
        b_var = sem("b_var")
        b_rstd = sem("b_rstd")
        b_x2 = sem("b_x2")
        c_row, c_row_x = sem("c_row"), sem("c_row_x")
        c_xT_psum = sem("c_xT_psum")
        c_xT = sem("c_xT")
        c_logit_psum = sem("c_logit_psum")
        c_logit = sem("c_logit")
        c_top = sem("c_top")
        c_gexp = sem("c_gexp")
        c_chosen = sem("c_chosen")
        c_rank = sem("c_rank")
        c_slot = sem("c_slot")
        c_sent = sem("c_sent")
        c_gu_psum = sem("c_gu_psum")
        c_gexp2 = sem("c_gexp2")
        c_mid = sem("c_mid")
        c_midT_psum = sem("c_midT_psum")
        c_midT = sem("c_midT")
        c_down = sem("c_down")
        c_y = sem("c_y")
        row_out_s, y_out_s = sem("row_out_s"), sem("y_out_s")
        ew_in = [sem(f"ew_in{i}") for i in range(D_RING)]
        ewd_in = [sem(f"ewd_in{i}") for i in range(D_RING)]
        d_copied = sem("d_copied")
        ex_in = [sem(f"ex_in{i}") for i in range(D_RING)]
        d_xT_psum, d_xT = sem("d_xT_psum"), sem("d_xT")
        d_gu_psum, d_exp, d_mid = sem("d_gu_psum"), sem("d_exp"), sem("d_mid")
        d_midT_psum, d_midT = sem("d_midT_psum"), sem("d_midT")
        d_down, d_out = sem("d_down"), sem("d_out")
        d_added = [sem("d_added0"), sem("d_added1")]
        yl_in = [sem(f"yl_in{g}") for g in range(FG)]
        e_var, e_rstd, e_done, final_out = sem("e_var"), sem("e_rstd"), sem("e_done"), sem("final_out")

        def last(t):
            return isinstance(t, int) and t == TILES - 1

        def bank_c(t):
            return SB[2] if last(t) else SC

        def x2T_of(t):
            return att_aT if last(t) else x2T

        def at(eng, s, value):
            if not isinstance(value, int) or value > 0:
                eng.wait_ge(s, value)

        def link(eng, s, base):
            n = [0]

            def f(ins):
                n[0] += 1
                ins.then_inc(s, 1)
                eng.wait_ge(s, base + n[0])
            return f

        def two_ago(e, i, back):
            if isinstance(i, int):
                return e - 1
            return e - 1 if back <= 2 else e

        def alone(eng):
            eng.sem_inc(waited, 1)

        def earlier_pairs(i, k):
            return 2 * i + (k - 3) // 2

        def run_steps(step, eng):
            step(0, None, None, None)
            step(1, 0, None, None)
            step(2, 1, 0, None)
            step(3, 2, 1, 0)
            with eng.Fori(4, TILES) as i:
                step(i, i - 1, i - 2, i - 3)
            step(None, TILES - 1, TILES - 2, TILES - 3)
            step(None, None, TILES - 1, TILES - 2)
            step(None, None, None, TILES - 1)

        def run_experts(step, eng):
            for i in range(2):
                for k in range(D_RING):
                    step(i, k)
            with eng.Fori(2, E // D_RING) as i:
                for k in range(D_RING):
                    step(i, k)
            for k in range(3):
                step(E // D_RING, k)

        def have(i, k, n):
            if isinstance(i, int):
                return 0 <= D_RING * i + k - n < E
            return True

        block = ctx.enter_context(nc.Block())

        @block.sync
        def _(eng):
            chunked = "(c p) n -> p c n"

            def load_xT(t):
                eng.dma_start(xT[:, :, :], io["xT"][bass.ds(t, 1), :, :].rearrange(
                    "b (c p) s -> p (b c) s", p=P)).then_inc(xT_in, 16)

            def load(dst, name, s):
                eng.dma_start(dst[:, :, :], io[name].rearrange(chunked, p=P)).then_inc(s, 16)

            load_xT(0)
            load(wqkv, "wqkvT", wqkv_in)
            load(wo, "woT", wo_in)
            eng.dma_start(uqT, io["uqT"].rearrange("(h d) q -> d h q", d=XHD)).then_inc(wqk_in, 16)
            eng.dma_start(ukT, io["ukT"].rearrange("(h d) q -> d h q", d=XHD)).then_inc(wqk_in, 16)
            load(wkvc2, "wkvc2", wlatent_in)
            load(wdq, "wdq", wlatent_in)
            eng.dma_start(wkr2[:, :, :], io["wkr2"].rearrange("p (a n) -> p a n", a=2)).then_inc(wlatent_in, 16)
            eng.dma_start(wqr[:, :, :], io["wqr"].rearrange("p (a n) -> p a n", a=2)).then_inc(wlatent_in, 16)

            def load_rest():
                eng.dma_start(uvT, io["uvT"].rearrange("(h d) q -> d h q", d=XHD)).then_inc(wvo_in, 16)
                xo = io["wox"].rearrange("(h d) o -> d h o", d=XHD)
                eng.dma_start(wox_lo, xo[:, 0:8, :]).then_inc(wvo_in, 16)
                eng.dma_start(wox_hi, xo[:, 8:16, :]).then_inc(wvo_in, 16)
                load(wgate, "wgateT", wffn_in)
                load(wsh, "wsh", wffn_in)
                eng.dma_start(wshd[:, 0:2, :], io["wshd"][0:2 * P, :].rearrange(chunked, p=P)).then_inc(wffn_in, 16)
                eng.dma_start(wshd[0:SI - 2 * P, 2, :], io["wshd"][2 * P:SI, :]).then_inc(wffn_in, 16)
                eng.wait_ge(pool_zeros, 1)
                eng.dma_start(empty_row[:, ROWW - 1:ROWW].bitcast(I32), io["empty_no"]).then_inc(empty_in, 16)
                eng.wait_ge(empty_in, 16)
                for e in range(E):
                    eng.dma_start(slots_dram[e * CAP:(e + 1) * CAP, :], empty_row).then_inc(zeros_out, 16)
                for y in y_dram:
                    eng.dma_start(y[NTOK:NTOK + P, :], empty_row[:, 0:CM]).then_inc(zeros_out, 16)

            def load_expert(i, k):
                e = D_RING * i + k
                at(eng, d_gu_psum, e - D_RING + 1 if not isinstance(i, int) or i else 0)
                eng.dma_start(ew[:, k, :, :], io["ew"][bass.ds(e, 1), :, :].rearrange(
                    "e (c p) n -> p (e c) n", p=P)).then_inc(ew_in[k], 16)

            def load_slots(i, k):
                e = D_RING * i + k
                at(eng, d_copied, e - D_RING + 1 if not isinstance(i, int) or i else 0)
                at(eng, d_xT_psum, e - D_RING + 1 if not isinstance(i, int) or i else 0)
                eng.dma_start(ex[:, k, :], slots_dram[bass.ds(e * CAP, CAP), :]).then_inc(ex_in[k], 16)

            def store_shared(t):
                eng.wait_ge(c_row_x, t + 1)
                eng.dma_start(y_dram[0][bass.ds(t * P, P), :], row[:, 0:CM]).then_inc(row_out_s, 16)
                eng.wait_ge(c_y, t + 1)
                eng.dma_start(y_dram[1][bass.ds(t * P, P), :], y_sb[:, :]).then_inc(y_out_s, 16)

            def step(a, b, c, d):
                if a is not None and not (isinstance(a, int) and a == 0):
                    at(eng, a_qkv, a)
                    load_xT(a)
                if b is not None:
                    at(eng, b_in_psum, b)
                    eng.dma_start(ctxT[:, :, :], io["ctxT"][bass.ds(b, 1), :, :].rearrange(
                        "b (c p) s -> p (b c) s", p=P)).then_inc(ctxT_in, 16)
                    at(eng, b_mask, b)
                    eng.dma_start(seg[:, :], io["seg"][bass.ds(b, 1), :].rearrange("b s -> s b"))\
                       .then_inc(seg_in, 16)
                    at(eng, a_res, b)
                    eng.dma_start(x_in[:, :], io["x"][bass.ds(b, 1), :, :].rearrange("b s c -> (b s) c"))\
                       .then_inc(x_in_s, 16)
                if isinstance(a, int) and a == 1:
                    load_rest()
                if isinstance(a, int) and a == 3:
                    eng.wait_ge(wvo_sb, 4)
                    for k in range(D_RING):
                        load_expert(0, k)
                if d is not None and not (isinstance(d, int) and d == 0):
                    store_shared(d - 1)

            run_steps(step, eng)

            eng.wait_ge(c_sent, 16 * TOPK * TILES)
            for k in range(D_RING):
                load_slots(0, k)
            store_shared(TILES - 1)
            with eng.Fori(1, E // D_RING) as i:
                for k in range(D_RING):
                    load_slots(i, k)
                    load_expert(i, k)

            for n in range(2):
                eng.wait_ge(d_added[n], 16 * E // 2)
            tokens = "(g p j) c -> g p (j c)"
            ov = y_out.rearrange("b s c -> (b s) c").rearrange(tokens, p=P, j=FJ)
            for g in range(FG):
                for n in range(2):
                    yv = y_dram[n][0:NTOK, :].rearrange(tokens, p=P, j=FJ)
                    eng.dma_start(fin_in[n][g], yv[g]).then_inc(yl_in[g], 16)
            for g in range(FG):
                eng.wait_ge(e_done, g + 1)
                eng.dma_start(ov[g], fin_out[g]).then_inc(final_out, 16)
            eng.wait_ge(final_out, 16 * FG)

        @block.tensor
        def _(eng):
            def turn(out, in_):
                return eng.transpose(out, in_, ident[0:in_.shape[0], 0:in_.shape[0]])

            def a_project(t):
                eng.wait_ge(xT_in, 16 * (t + 1))
                at(eng, a_raw, t)
                for c in range(CC):
                    mm = eng.matmul(SA[0][:, :], xT[:, c, :], wqkv[:, c, 0:2 * CM], start=c == 0, stop=c == CC - 1)
                mm.then_inc(a_qk_psum, 1)

            def a_project_v(t):
                at(eng, a_res, t)
                for c in range(CC):
                    mm = eng.matmul(SA[1][:, 0:CM], xT[:, c, :], wqkv[:, c, 2 * CM:3 * CM],
                                    start=c == 0, stop=c == CC - 1)
                mm.then_inc(a_qkv, 1)

            def a_turn(t):
                if isinstance(t, int) and t == 0:
                    eng.wait_ge(const_a_in, 16 * 3)
                eng.wait_ge(a_qk, t + 1)
                at(eng, a_attT, t)
                for s in range(2):
                    for g in range(4):
                        heads = qk_pad[:, H * s + 4 * g:H * s + 4 * g + 4, :].rearrange("p h d -> p (h d)")
                        mm = turn(SA[2 + s][:, P * g:P * g + P], heads)
                    mm.then_inc(a_tr, 1)

            def a_scores(t, g):
                if g == 0:
                    eng.wait_ge(a_qT, t + 1)
                    eng.wait_ge(a_kT, t + 1)
                    eng.wait_ge(a_v, t + 1)
                for j in range(4):
                    rows = slice(VW * j, VW * j + VW)
                    mm = eng.matmul(SA[j][:, P * g:P * g + P], kT[rows, g, :], qT[rows, g, :],
                                    start=True, stop=True)
                mm.then_inc(a_score, 1)

            def a_values(t):
                eng.wait_ge(a_masked, 4 * t + 4)
                for g in range(4):
                    for j in range(4):
                        mm = eng.matmul(SA[0][VW * j:VW * j + VW, P * g:P * g + P], v_a[:, 4 * g + j, :],
                                        prob_a[:, 4 * j + g, :], start=True, stop=True)
                mm.then_inc(a_av, 1)

            def a_turn_raw(t):
                eng.wait_ge(a_raw, t + 1)
                for g in range(4):
                    mm = turn(SA[2][:, P * g:P * g + P], att_raw[:, g, :])
                mm.then_inc(a_raw_turned, 1)

            def a_turn_out(t):
                eng.wait_ge(a_att, t + 1)
                for c in range(CC):
                    mm = turn(SA[3][:, P * c:P * c + P], att_a[:, P * c:P * c + P])
                mm.then_inc(a_attT_psum, 1)

            def a_out(t):
                if isinstance(t, int) and t == 0:
                    eng.wait_ge(wo_in, 16)
                eng.wait_ge(a_attT, t + 1)
                for c in range(CC):
                    mm = eng.matmul(SA[1][:, 0:CM], att_aT[:, c, :], wo[:, c, :], start=c == 0, stop=c == CC - 1)
                mm.then_inc(a_wo, 1)

            def b_input(t):
                if isinstance(t, int) and t == 0:
                    eng.wait_ge(wlatent_in, 16 * 4)
                    eng.wait_ge(wqk_sb, 2)
                eng.wait_ge(a_x1, t + 1)
                eng.wait_ge(ctxT_in, 16 * (t + 1))
                at(eng, b_attT, 2 * t)
                for c in range(CC):
                    turn(SB[2][:, P * c:P * c + P], x1[:, P * c:P * c + P])
                for c in range(CC):
                    mm = eng.matmul(SB[2][:, CM:CM + P], wkvc2[:, c, :], ctxT[:, c, :],
                                    start=c == 0, stop=c == CC - 1)
                mm.then_inc(b_in_psum, 1)

            def b_latent(t):
                eng.wait_ge(b_in, t + 1)
                at(eng, b_res, t)
                for c in range(CC):
                    eng.matmul(SB[0][0:QC, 0:P], wdq[:, c, :], x1T[:, c, :], start=c == 0, stop=c == CC - 1)
                for s in range(2):
                    eng.matmul(SB[0][:, P * (1 + s):P * (2 + s)], wkr2[:, s, :], kk_e[0:KVC, :],
                               start=True, stop=True)
                turn(SB[0][:, 3 * P:3 * P + KVC], kk_e[0:KVC, :]).then_inc(b_qc_psum, 1)

            def b_queries(t, half):
                eng.wait_ge(b_qc, t + 1)
                for use, bk in enumerate((SB[1], SB[2], SB[0])):
                    if half == 1:
                        eng.wait_ge(b_rot, 4 * t + 1 + use) if use < 2 else eng.wait_ge(b_nope, 2 * t + 1)
                    elif use == 2:
                        eng.wait_ge(b_keys, t + 1)
                        eng.wait_ge(b_v, t + 1)
                    for j in range(4):
                        pair = slice(P * (4 * half + j), P * (4 * half + j) + P)
                        w = wqk[:, pair] if use == 2 else wqr[:, use, pair]
                        mm = eng.matmul(bk[:, P * j:P * j + P], w, qcT[:, :], start=True, stop=True)
                    mm.then_inc(b_q_psum, 1)

            def b_scores(t, g):
                if g % 2 == 0:
                    eng.wait_ge(b_rope, 4 * t + 2 + g)
                    eng.wait_ge(b_nope, 2 * t + 1 + g // 2)
                if g < 2:
                    eng.wait_ge(b_rot, 4 * t + 3 + g)
                elif g == 3:
                    eng.wait_ge(b_score, 4 * t + 1)
                for j in range(4):
                    h = 4 * g + j
                    qq, kk = (qq_e, kk_e) if h % 2 == 0 else (qq_o, kk_o)
                    mm = eng.matmul(SB[(1 + g) % 3][:, P * j:P * j + P], qq[:, h // 2, :], kk[:, :],
                                    start=True, stop=True)
                mm.then_inc(b_score_psum, 1)

            def b_turn(t, g):
                eng.wait_ge(b_weights, 4 * t + g + 1)
                if g == 0:
                    eng.wait_ge(b_score, 4 * t + 4)
                elif g == 3:
                    eng.wait_ge(b_pT, 4 * t + 1)
                for j in range(4):
                    mm = turn(SB[g % 3][:, P * j:P * j + P], prob_b[:, 4 * g + j, :])
                mm.then_inc(b_pT_psum, 1)

            def b_values(t, half):
                eng.wait_ge(b_pT, 4 * t + 2 + 2 * half)
                for odd in range(2):
                    heads = prob_bT[:, 8 * half + odd:8 * half + 8:2, :]
                    mm = eng.matmul(SB[1 + half][KVC * odd:KVC * odd + KVC, :].rearrange("p (j q) -> p j q", q=P),
                                    v_b[:, :], heads, start=True, stop=True)
                mm.then_inc(b_av, 1)

            def b_out(t, half):
                eng.wait_ge(b_attT, 2 * t + half + 1)
                if isinstance(t, int) and t == 0 and half == 0:
                    eng.wait_ge(wvo_sb, 4)
                if half == 0:
                    eng.wait_ge(b_pT, 4 * t + 4)
                for j in range(4 * half, 4 * half + 4):
                    mm = eng.matmul(SB[0][:, 0:CM], att_bT[:, j, :], wvo[:, j, :],
                                    start=j == 0, stop=j == H // 2 - 1)
                if half == 1:
                    mm.then_inc(b_wo, 1)

            def c_turn(t):
                eng.wait_ge(b_x2, t + 1)
                if not last(t):
                    at(eng, c_y, t)
                for c in range(CC):
                    mm = turn(bank_c(t)[:, P * c:P * c + P], x2[:, P * c:P * c + P])
                mm.then_inc(c_xT_psum, 1)

            def c_router(t):
                if isinstance(t, int) and t == 0:
                    eng.wait_ge(wffn_in, 16 * 4)
                eng.wait_ge(c_xT, t + 1)
                for c in range(CC):
                    mm = eng.matmul(bank_c(t)[:, 0:E], x2T_of(t)[:, c, :], wgate[:, c, :], start=c == 0, stop=c == CC - 1)
                mm.then_inc(c_logit_psum, 1)

            def c_up(t, half):
                if half == 0:
                    eng.wait_ge(c_slot, t + 1)
                else:
                    eng.wait_ge(c_mid, 2 * t + 1)
                for c in range(CC):
                    mm = eng.matmul(bank_c(t)[:, 0:2 * SH], x2T_of(t)[:, c, :], wsh[:, c, 2 * SH * half:2 * SH * (half + 1)],
                                    start=c == 0, stop=c == CC - 1)
                mm.then_inc(c_gu_psum, 1)

            def c_ranks(t):
                eng.wait_ge(c_chosen, t + 1)
                eng.wait_ge(c_logit, t + 1)
                eng.matmul(bank_c(t)[:, 0:E], earlier[:, :], chosen_bf[:, :], start=True, stop=False)
                eng.matmul(bank_c(t)[:, 0:E], ones_bf[:, :], seen_bf[:, :], start=False, stop=True).then_inc(c_rank, 1)

            def c_turn_mid(t):
                eng.wait_ge(c_mid, 2 * t + 2)
                for c in range(3):
                    n = min(P, SI - P * c)
                    mm = turn(bank_c(t)[0:n, P * c:P * c + P], sh_mid[:, P * c:P * c + n])
                mm.then_inc(c_midT_psum, 1)

            def c_out(t):
                eng.wait_ge(c_midT, t + 1)
                for c in range(3):
                    n = min(P, SI - P * c)
                    mm = eng.matmul(bank_c(t)[:, 0:CM], sh_midT[0:n, c, :], wshd[0:n, c, :], start=c == 0, stop=c == 2)
                mm.then_inc(c_down, 1)

            def multiply_wqk():
                eng.wait_ge(wqk_in, 16 * 2)
                for h in range(H):
                    mm = eng.matmul(bank[4 + h // 8][0:QC, KVC * (h % 8):KVC * (h % 8) + KVC], uqT[:, h, :],
                                    ukT[:, h, :], start=True, stop=True)
                    if h % 8 == 7:
                        mm.then_inc(wqk_psum, 1)

            def multiply_wvo(n):
                if n == 0:
                    eng.wait_ge(wvo_in, 16 * 3)
                else:
                    eng.wait_ge(wvo_sb, n)
                for h in range(4 * n, 4 * n + 4):
                    j, odd = h // 2, h % 2
                    wox = wox_lo[:, h, :] if h < 8 else wox_hi[:, h - 8, :]
                    mm = eng.matmul(SC[KVC * odd:KVC * odd + KVC, CM * (j % 2):CM * (j % 2) + CM],
                                    uvT[:, h, :], wox, start=True, stop=True)
                mm.then_inc(wvo_psum, 1)

            def step(a, b, c, d):
                if b is not None:
                    a_values(b)
                if c is not None:
                    b_turn(c, 0)
                if c is not None and d is not None:
                    c_router(d)
                if b is not None:
                    a_turn_raw(b)
                if a is not None:
                    a_project(a)
                if c is not None:
                    b_turn(c, 1)
                    b_turn(c, 2)
                    b_turn(c, 3)
                    b_values(c, 0)
                if isinstance(a, int) and a == 0:
                    multiply_wqk()
                if b is not None:
                    a_turn_out(b)
                    a_out(b)
                if c is not None:
                    b_values(c, 1)
                    b_out(c, 0)
                    b_out(c, 1)
                if a is not None:
                    a_project_v(a)
                if isinstance(a, int) and a == 1:
                    multiply_wvo(0)
                if d is not None:
                    c_ranks(d)
                if b is not None:
                    b_input(b)
                    b_latent(b)
                if a is not None:
                    a_turn(a)
                if d is not None:
                    c_up(d, 0)
                if b is None and c is not None:
                    c_turn(c)
                if b is not None:
                    b_queries(b, 0)
                    b_queries(b, 1)
                if isinstance(a, int) and a == 1:
                    multiply_wvo(1)
                if d is not None:
                    c_up(d, 1)
                if b is None and c is not None:
                    c_router(c)
                if b is not None:
                    b_scores(b, 0)
                if isinstance(a, int) and a == 1:
                    multiply_wvo(2)
                if b is not None:
                    b_scores(b, 1)
                if a is not None:
                    a_scores(a, 0)
                    a_scores(a, 1)
                if d is not None:
                    c_turn_mid(d)
                if a is not None:
                    a_scores(a, 2)
                if isinstance(a, int) and a == 1:
                    multiply_wvo(3)
                if b is not None:
                    b_scores(b, 2)
                if a is not None:
                    a_scores(a, 3)
                if b is not None:
                    b_scores(b, 3)
                if d is not None:
                    c_out(d)
                if b is not None and c is not None:
                    c_turn(c)

            eng.wait_ge(wqkv_in, 16)
            run_steps(step, eng)

            def expert(i, k):
                if have(i, k, 0):
                    e = D_RING * i + k
                    eng.wait_ge(ex_in[k], 16 * (i + 1))
                    at(eng, d_xT, two_ago(e, i, 0))
                    for c in range(CC):
                        mm = turn(bank[k % 2][:, P * c:P * c + P], ex[:, k, P * c:P * c + P])
                    mm.then_inc(d_xT_psum, 1)
                if have(i, k, 1):
                    e, s = D_RING * i + k - 1, (k - 1) % D_RING
                    eng.wait_ge(ew_in[s], 16 * (i + 1 if k >= 1 else i))
                    eng.wait_ge(d_xT, e + 1)
                    at(eng, d_mid, two_ago(e, i, 1 - k))
                    for c in range(CC):
                        mm = eng.matmul(bank[2 + s % 2][:, 0:2 * EI], exT[:, s % 2, c, :], ew[:, s, c, :],
                                        start=c == 0, stop=c == CC - 1)
                    mm.then_inc(d_gu_psum, 1)
                if have(i, k, 2):
                    e, s = D_RING * i + k - 2, (k - 2) % D_RING
                    eng.wait_ge(d_mid, e + 1)
                    at(eng, d_midT, two_ago(e, i, 2 - k))
                    for c in range(2):
                        mm = turn(bank[4 + s % 2][0:EI // 2, P * c:P * c + P],
                                  e_mid[:, s % 2, EI // 2 * c:EI // 2 * (c + 1)])
                    mm.then_inc(d_midT_psum, 1)
                if have(i, k, 3):
                    e, s = D_RING * i + k - 3, (k - 3) % D_RING
                    if isinstance(i, int) and i == 0:
                        eng.wait_ge(c_y, TILES)
                    eng.wait_ge(ewd_in[s], 16 * (i + 1 if k >= 3 else i))
                    eng.wait_ge(d_midT, e + 1)
                    at(eng, d_out, two_ago(e, i, 3 - k))
                    for c in range(2):
                        mm = eng.matmul(bank[6 + s % 2][:, 0:CM], e_midT[:, s % 2, c, :], ewd[0:EI // 2, s, c, :],
                                        start=c == 0, stop=c == 1)
                    mm.then_inc(d_down, 1)

            run_experts(expert, eng)

        @block.scalar
        def _(eng):
            def a_value_copy(t):
                eng.wait_ge(a_qkv, t + 1)
                at(eng, a_av, t)
                eng.activation(v_a[:, :, 0:HD], SA[1][:, 0:CM].rearrange("p (h d) -> p h d", d=HD),
                               ACT.Copy).then_inc(a_v, 1)

            def a_q_copy(t):
                eng.wait_ge(a_tr, 2 * t + 1)
                at(eng, a_score, 4 * t)
                eng.activation(qT[:, :, :], SA[2][:, :].rearrange("p (g q) -> p g q", q=P),
                               ACT.Copy).then_inc(a_qT, 1)

            def a_k_copy(t):
                eng.wait_ge(a_tr, 2 * t + 2)
                at(eng, a_score, 4 * t)
                eng.activation(kT[:, :, :], SA[3][:, :].rearrange("p (g q) -> p g q", q=P),
                               ACT.Copy).then_inc(a_kT, 1)

            def a_raw_copy(t):
                eng.wait_ge(a_av, t + 1)
                at(eng, a_raw_turned, t)
                eng.activation(att_raw[:, :, :], SA[0][:, :].rearrange("p (g q) -> p g q", q=P),
                               ACT.Copy).then_inc(a_raw, 1)

            def a_exps(t):
                eng.wait_ge(a_score, 4 * t + 4)
                at(eng, a_av, t)
                for j in range(4):
                    eng.activation(prob_a[:, 4 * j:4 * j + 4, :], SA[j][:, :].rearrange("p (g q) -> p g q", q=P),
                                   ACT.Exp, scale=SCALE_A).then_inc(a_exp, 1)

            def a_att_copy(t):
                eng.wait_ge(a_attT_psum, t + 1)
                at(eng, a_wo, t)
                eng.activation(att_aT[:, :, :], SA[3][:, 0:CM].rearrange("p (c q) -> p c q", q=P),
                               ACT.Copy).then_inc(a_attT, 1)

            def b_input_copy(t):
                eng.wait_ge(b_in_psum, t + 1)
                at(eng, b_qc_psum, t)
                at(eng, b_score_psum, 4 * t)
                eng.activation(x1T[:, :, :], SB[2][:, 0:CM].rearrange("p (c q) -> p c q", q=P), ACT.Copy)
                eng.activation(kk_e[0:KVC, :], SB[2][0:KVC, CM:CM + P], ACT.Copy)
                eng.activation(kk_o[KVC:2 * KVC, :], SB[2][KVC:2 * KVC, CM:CM + P], ACT.Copy).then_inc(b_in, 1)

            def b_latent_copy(t):
                eng.wait_ge(b_qc_psum, t + 1)
                at(eng, b_q_psum, 6 * t)
                eng.activation(qcT[:, :], SB[0][0:QC, 0:P], ACT.Copy).then_inc(b_qc, 1)

            def b_value_copy(t):
                at(eng, b_av, 2 * t)
                eng.wait_ge(b_keys, t + 1)
                eng.activation(v_b[:, :], SB[0][:, 3 * P:3 * P + KVC], ACT.Copy).then_inc(b_v, 1)

            def b_nope_copy(t, half):
                eng.wait_ge(b_q_psum, 6 * t + 3 * half + 3)
                at(eng, b_score_psum, 4 * t)
                src = SB[0][:, :].rearrange("p (j q) -> p j q", q=P)
                eng.activation(qq_e[0:KVC, 4 * half:4 * half + 4, :], src[0:KVC], ACT.Copy)
                eng.activation(qq_o[KVC:2 * KVC, 4 * half:4 * half + 4, :], src[KVC:2 * KVC],
                               ACT.Copy).then_inc(b_nope, 1)

            def b_exps(t, g):
                eng.wait_ge(b_score, 4 * t + g + 1)
                at(eng, b_pT_psum, 4 * t)
                for j in range(4):
                    h = 4 * g + j
                    ins = eng.activation(prob_b[:, h, :], score_b[:, h, :], ACT.Exp, bias=negmax_b[:, h:h + 1],
                                         accum_out=den_b[:, h:h + 1])
                ins.then_inc(b_prob, 1)

            def b_prob_copy(t, g):
                eng.wait_ge(b_pT_psum, 4 * t + g + 1)
                at(eng, b_av, 2 * t)
                eng.activation(prob_bT[:, 4 * g:4 * g + 4, :], SB[g % 3][:, :].rearrange(
                    "p (j q) -> p j q", q=P), ACT.Copy).then_inc(b_pT, 1)

            def b_att_copy(t, half):
                eng.wait_ge(b_av, 2 * t + half + 1)
                at(eng, b_wo, t)
                eng.activation(att_bT[:, 4 * half:4 * half + 4, :], SB[1 + half][:, :].rearrange(
                    "p (j q) -> p j q", q=P), ACT.Copy).then_inc(b_attT, 1)

            def c_row_copy(t):
                eng.wait_ge(b_x2, t + 1)
                at(eng, c_sent, 16 * TOPK * t)
                at(eng, row_out_s, 16 * t)
                eng.activation(row[:, 0:CM], x2[:, :], ACT.Copy).then_inc(c_row_x, 1)

            def c_input_copy(t):
                eng.wait_ge(c_xT_psum, t + 1)
                if not last(t):
                    at(eng, c_gu_psum, 2 * t)
                eng.activation(x2T_of(t)[:, :, :], bank_c(t)[:, 0:CM].rearrange("p (c q) -> p c q", q=P),
                               ACT.Copy).then_inc(c_xT, 1)

            def c_router_exp(t):
                eng.wait_ge(c_logit, t + 1)
                eng.wait_ge(c_top, t + 1)
                eng.activation(gexp[:, :], logit[:, :], ACT.Exp, bias=neg_top[:, :],
                               accum_out=gsum[:, :]).then_inc(c_gexp, 1)

            def c_gate_exp(t, half):
                eng.wait_ge(c_gu_psum, 2 * t + half + 1)
                at(eng, c_mid, 2 * t)
                eng.activation(sh_exp[:, half, :], bank_c(t)[:, 0:SH], ACT.Tanh, scale=0.5).then_inc(c_gexp2, 1)

            def c_mid_copy(t):
                eng.wait_ge(c_midT_psum, t + 1)
                at(eng, c_down, t)
                eng.activation(sh_midT[:, 0:2, :], bank_c(t)[:, 0:2 * P].rearrange("p (c q) -> p c q", q=P), ACT.Copy)
                eng.activation(sh_midT[0:SI - 2 * P, 2, :], bank_c(t)[0:SI - 2 * P, 2 * P:3 * P],
                               ACT.Copy).then_inc(c_midT, 1)

            def copy_wqk():
                for b in range(2):
                    eng.wait_ge(wqk_psum, b + 1)
                    eng.activation(wqk[:, 512 * b:512 * b + 512], bank[4 + b][0:QC, :], ACT.Copy).then_inc(wqk_sb, 1)

            def copy_wvo(n):
                eng.wait_ge(wvo_psum, n + 1)
                eng.activation(wvo[:, 2 * n:2 * n + 2, :], SC[:, :].rearrange("p (j o) -> p j o", o=CM),
                               ACT.Copy).then_inc(wvo_sb, 1)

            for dst, name in ((cos_a, "cos_a"), (sin_a, "sin_a"), (ident, "ident")):
                eng.dma_start(dst[:, :], io[name]).then_inc(const_a_in, 16)
            for dst, name in ((cos_b, "cos_b"), (sin_b, "sin_b"), (key_pos, "key_pos"), (slot_base, "slot_base"),
                              (expert_no, "expert_no"), (earlier, "earlier")):
                eng.dma_start(dst[:, :], io[name]).then_inc(const_in, 16)
            eng.dma_start(row[:, ROWW - 1:ROWW].bitcast(I32), io["token_no"]).then_inc(const_in, 16)
            eng.wait_ge(dve_setup, 4)

            def step(a, b, c, d):
                if b is not None:
                    a_raw_copy(b)
                if c is not None:
                    b_prob_copy(c, 0)
                    b_prob_copy(c, 1)
                    b_prob_copy(c, 2)
                if c is not None and d is not None:
                    c_router_exp(d)
                if b is not None:
                    a_att_copy(b)
                if c is not None:
                    b_prob_copy(c, 3)
                if c is not None and d is not None:
                    c_row_copy(d)
                if isinstance(a, int) and a == 0:
                    copy_wqk()
                if c is not None:
                    b_att_copy(c, 0)
                    b_att_copy(c, 1)
                if a is not None:
                    a_value_copy(a)
                if b is not None:
                    b_input_copy(b)
                    b_latent_copy(b)
                    b_value_copy(b)
                if a is not None:
                    a_q_copy(a)
                if isinstance(a, int) and a == 1:
                    copy_wvo(0)
                if d is not None:
                    c_gate_exp(d, 0)
                if b is None and c is not None:
                    c_input_copy(c)
                if b is not None:
                    b_nope_copy(b, 0)
                if a is not None:
                    a_k_copy(a)
                if isinstance(a, int) and a == 1:
                    copy_wvo(1)
                    copy_wvo(2)
                if b is not None:
                    b_nope_copy(b, 1)
                if d is not None:
                    c_gate_exp(d, 1)
                if b is None and c is not None:
                    c_router_exp(c)
                    c_row_copy(c)
                if b is not None:
                    b_exps(b, 0)
                if isinstance(a, int) and a == 1:
                    copy_wvo(3)
                if b is not None:
                    b_exps(b, 1)
                if d is not None:
                    c_mid_copy(d)
                if a is not None:
                    a_exps(a)
                if b is not None:
                    b_exps(b, 2)
                if b is not None and c is not None:
                    c_input_copy(c)
                if b is not None:
                    b_exps(b, 3)

            run_steps(step, eng)

            def load_down(i, k):
                e = D_RING * i + k
                if not isinstance(i, int) or i:
                    eng.wait_ge(d_down, e - D_RING + 1)
                eng.dma_start(ewd[0:EI // 2, k, :, :], io["ewd"][bass.ds(e, 1), :, :].rearrange(
                    "e (c p) n -> p (e c) n", c=2)).then_inc(ewd_in[k], 16)

            def expert(i, k):
                if have(i, k, 0):
                    load_down(i, k)
                    e = D_RING * i + k
                    eng.wait_ge(d_xT_psum, e + 1)
                    at(eng, d_gu_psum, two_ago(e, i, 0))
                    eng.activation(exT[:, k % 2, :, :], bank[k % 2][:, 0:CM].rearrange("p (c q) -> p c q", q=P),
                                   ACT.Copy).then_inc(d_xT, 1)
                if have(i, k, 1):
                    e, s = D_RING * i + k - 1, (k - 1) % D_RING
                    eng.wait_ge(d_gu_psum, e + 1)
                    at(eng, d_mid, two_ago(e, i, 1 - k))
                    eng.activation(e_exp[:, s % 2, :], bank[2 + s % 2][:, 0:EI], ACT.Tanh, scale=0.5)\
                       .then_inc(d_exp, 1)
                if have(i, k, 2):
                    e, s = D_RING * i + k - 2, (k - 2) % D_RING
                    eng.wait_ge(d_midT_psum, e + 1)
                    at(eng, d_down, two_ago(e, i, 2 - k))
                    eng.activation(e_midT[:, s % 2, :, :], bank[4 + s % 2][0:EI // 2, 0:2 * P].rearrange(
                        "p (c q) -> p c q", q=P), ACT.Copy).then_inc(d_midT, 1)

            run_experts(expert, eng)

            for g in range(FG):
                eng.wait_ge(e_rstd, g + 1)
                for j in range(FJ):
                    cols = slice(CM * j, CM * j + CM)
                    ins = eng.activation(fin_out[g][:, cols], fin_in[0][g][:, cols], ACT.Identity,
                                         bias=fin_bias[:, g, j:j + 1], scale=fin_rstd[:, g, j:j + 1])
                ins.then_inc(e_done, 1)

        @block.vector
        def _(eng):
            def a_rope(t):
                eng.wait_ge(a_qk_psum, t + 1)
                then = link(eng, chain_a_rope, 3 * t)
                pairs = "p (i two) -> p i two"
                eng.tensor_tensor(qk_cos[:, :], SA[0][:, :], cos_a[:, :], ALU.mult)
                src = SA[0][:, :].rearrange(pairs, two=2)
                dst = qk_sin[:, :].rearrange(pairs, two=2)
                tab = sin_a[:, :].rearrange(pairs, two=2)
                eng.tensor_tensor(dst[:, :, 0:1], src[:, :, 1:2], tab[:, :, 0:1], ALU.mult)
                then(eng.tensor_tensor(dst[:, :, 1:2], src[:, :, 0:1], tab[:, :, 1:2], ALU.mult))
                then(eng.tensor_tensor(qk_rot[:, :], qk_cos[:, :], qk_sin[:, :], ALU.add))
                then(eng.tensor_tensor(qk_sq[:, :], qk_rot[:, :], qk_rot[:, :], ALU.mult))
                at(eng, a_rs, 2 * t)
                eng.tensor_reduce(qk_ss[:, :], qk_sq[:, :].rearrange("p (i d) -> p i d", d=HD), AX.X, ALU.add)\
                   .then_inc(a_ss, 1)

            def a_scale(t):
                eng.wait_ge(a_rs, 2 * t + 2)
                at(eng, a_tr, 2 * t)
                eng.tensor_tensor(qk_pad[:, :, 0:HD], qk_rot[:, :].rearrange("p (i d) -> p i d", d=HD),
                                  qk_rs[:, :, None].to_broadcast([P, 2 * H, HD]), ALU.mult).then_inc(a_qk, 1)

            def a_normalise(t):
                eng.wait_ge(a_raw_turned, t + 1)
                then = link(eng, chain_a_att, t)
                heads = SA[2][:, :].rearrange("p (h d) -> p h d", d=VW)
                then(eng.reciprocal(rec_a[:, :, None], heads[:, :, HD:HD + 1]))
                at(eng, a_attT_psum, t)
                eng.tensor_tensor(att_a[:, :].rearrange("p (h d) -> p h d", d=HD), heads[:, :, 0:HD],
                                  rec_a[:, :, None].to_broadcast([P, H, HD]), ALU.mult).then_inc(a_att, 1)

            def norm_stats(which, res, then, var_s):
                then(eng.bn_stats(stats[which][:, :], res[:, :]))
                alone(eng)
                eng.bn_aggr(mv[which][:, :], stats[which][:, :]).then_inc(var_s, 1)

            def norm_scale(which, res, out, rstd_s, t, done_s):
                eng.wait_ge(rstd_s, t + 1)
                eng.tensor_scalar(out[:, :], res[:, :], mv[which][:, 0:1], rstd[which][:, :],
                                  ALU.subtract, ALU.mult).then_inc(done_s, 1)

            def a_residual(t):
                eng.wait_ge(a_wo, t + 1)
                eng.wait_ge(x_in_s, 16 * (t + 1))
                eng.tensor_tensor(res_a[:, :], SA[1][:, 0:CM], x_in[:, :], ALU.add).then_inc(a_res, 1)
                eng.wait_ge(a_res, t + 1)
                norm_stats("a", res_a, link(eng, chain_a_norm, t), a_var)

            def a_norm(t):
                at(eng, b_keep, t)
                at(eng, b_in_psum, t)
                norm_scale("a", res_a, x1, a_rstd, t, a_x1)

            def b_rotate_keys(t):
                if isinstance(t, int) and t == 0:
                    eng.wait_ge(const_in, 16 * 7)
                eng.wait_ge(b_qc, t + 1)
                at(eng, b_score_psum, 4 * t)
                then = link(eng, chain_b_latent, t)
                eng.tensor_tensor(kr_cos[:, :], SB[0][:, P:2 * P], cos_b[:, :], ALU.mult)
                then(eng.tensor_tensor(kr_sin[:, :], SB[0][:, 2 * P:3 * P], sin_b[:, :], ALU.mult))
                eng.tensor_tensor(kk_e[R:2 * R, :], kr_cos[R:2 * R, :], kr_sin[R:2 * R, :], ALU.add)
                eng.tensor_tensor(kk_o[0:R, :], kr_cos[0:R, :], kr_sin[0:R, :], ALU.add).then_inc(b_keys, 1)

            def b_rotate(t, half):
                at(eng, b_rope, 4 * t)
                for use, dst, tab, bk in ((0, qr_cos, cos_b, SB[1]), (1, qr_sin, sin_b, SB[2])):
                    eng.wait_ge(b_q_psum, 6 * t + 3 * half + use + 1)
                    eng.tensor_tensor(dst[:, half, :].rearrange("p (j q) -> p j q", q=P),
                                      bk[:, :].rearrange("p (j q) -> p j q", q=P),
                                      tab[:, None, :].to_broadcast([P, 4, P]), ALU.mult).then_inc(b_rot, 1)

            def b_rotate_add(t, half):
                eng.wait_ge(b_rot, 4 * t + 2 * half + 2)
                at(eng, b_score_psum, 4 * t)
                for dst, rows in ((qq_e, slice(R, 2 * R)), (qq_o, slice(0, R))):
                    eng.tensor_tensor(dst[rows, 4 * half:4 * half + 4, :].rearrange("p j q -> p (j q)"),
                                      qr_cos[rows, half, :], qr_sin[rows, half, :], ALU.add).then_inc(b_rope, 1)

            def b_maxima(t, g):
                if g == 0:
                    eng.wait_ge(b_mask, t + 1)
                eng.wait_ge(b_score_psum, 4 * t + g + 1)
                at(eng, b_prob, 4 * t)
                then = link(eng, chain_b_max, 4 * t + g)
                alone(eng)
                for j in range(4):
                    h = 4 * g + j
                    ins = eng.tensor_tensor_reduce(score_b[:, h, :], SB[(1 + g) % 3][:, P * j:P * j + P],
                                                   mask_b[:, :], SCALE_B, -3.0e38, ALU.add, ALU.max,
                                                   max_b[:, h:h + 1])
                then(ins)
                eng.tensor_scalar(negmax_b[:, 4 * g:4 * g + 4], max_b[:, 4 * g:4 * g + 4], -1.0, None,
                                  ALU.mult).then_inc(b_score, 1)

            def b_weigh(t, g):
                eng.wait_ge(b_prob, 4 * t + g + 1)
                heads = slice(4 * g, 4 * g + 4)
                link(eng, chain_b_att, 4 * t + g)(eng.reciprocal(rec_b[:, heads], den_b[:, heads]))
                eng.tensor_tensor(prob_b[:, heads, :], prob_b[:, heads, :],
                                  rec_b[:, heads, None].to_broadcast([P, 4, P]), ALU.mult).then_inc(b_weights, 1)

            def b_residual(t):
                eng.wait_ge(b_wo, t + 1)
                eng.wait_ge(b_keep, t + 1)
                eng.tensor_tensor(res_b[:, :], SB[0][:, 0:CM], x1_keep[:, :], ALU.add).then_inc(b_res, 1)
                eng.wait_ge(b_res, t + 1)
                norm_stats("b", res_b, link(eng, chain_b_norm, t), b_var)

            def b_norm(t):
                at(eng, c_row_x, t)
                at(eng, c_xT_psum, t)
                norm_scale("b", res_b, x2, b_rstd, t, b_x2)

            def c_logits(t):
                eng.wait_ge(c_logit_psum, t + 1)
                at(eng, c_gexp, t)
                eng.tensor_copy(logit[:, :], bank_c(t)[:, 0:E]).then_inc(c_logit, 1)
                eng.wait_ge(c_logit, t + 1)
                eng.tensor_reduce(neg_top[:, :], logit[:, :], AX.X, ALU.max, negate=True).then_inc(c_top, 1)

            def c_choose(t):
                eng.wait_ge(c_gexp, t + 1)
                then = link(eng, chain_c_choose, 10 * t)
                then(eng.reciprocal(grec[:, :], gsum[:, :]))
                then(eng.tensor_scalar(gprob[:, :], gexp[:, :], grec[:, :], None, ALU.mult))
                alone(eng)
                then(eng.max(top8[:, :], gprob[:, :]))
                alone(eng)
                then(eng.max_index(top_no[:, :], top8[:, :], gprob[:, :]))

            def c_mask(t):
                then = link(eng, chain_c_choose, 10 * t + 4)
                then(eng.tensor_copy(top_nof[:, :], top_no[:, :]))
                then(eng.tensor_tensor(matches[:, :, :], expert_no[:, :, None].to_broadcast([P, E, TOPK]),
                                       top_nof[:, None, 0:TOPK].to_broadcast([P, E, TOPK]), ALU.is_equal))
                then(eng.tensor_reduce(chosen[:, :], matches[:, :, :], AX.X, ALU.add))
                at(eng, c_rank, t)
                eng.tensor_copy(chosen_bf[:, :], chosen[:, :]).then_inc(c_chosen, 1)

            def c_weights(t):
                then = link(eng, chain_c_choose, 10 * t + 7)
                then(eng.tensor_reduce(wsum[:, 0:1], top8[:, 0:TOPK], AX.X, ALU.add))
                then(eng.tensor_scalar(wsum[:, 1:2], wsum[:, 0:1], 1e-20, None, ALU.add))
                then(eng.reciprocal(wrec[:, :], wsum[:, 1:2]))
                at(eng, c_sent, 16 * TOPK * t)
                eng.scalar_tensor_tensor(row[:, CM:CM + E], gprob[:, :], wrec[:, :], chosen[:, :],
                                         ALU.mult, ALU.mult)
                eng.tensor_scalar(row[:, ROWW - 1:ROWW].bitcast(I32), row[:, ROWW - 1:ROWW].bitcast(I32),
                                  float(P), None, ALU.add).then_inc(c_row, 1)

            def c_slots(t):
                eng.wait_ge(c_rank, t + 1)
                then = link(eng, chain_c_slot, 3 * t)
                eng.tensor_tensor(slot_u[:, :], slot_base[:, :], bank_c(t)[:, 0:E], ALU.subtract)
                then(eng.scalar_tensor_tensor(slot_v[:, :], bank_c(t)[:, 0:E], float(CAP), chosen[:, :],
                                              ALU.is_lt, ALU.mult))
                eng.tensor_tensor(seen_bf[:, :], seen_bf[:, :], chosen_bf[:, :], ALU.add)
                then(eng.tensor_tensor(slot_s[:, :], slot_u[:, :], slot_v[:, :], ALU.mult))
                alone(eng)
                then(eng.max(slot8[:, :], slot_s[:, :]))
                at(eng, c_sent, 16 * TOPK * t)
                eng.tensor_scalar(slot_no[:, :], slot8[:, :], -1.0, float(NOSLOT), ALU.mult, ALU.add)\
                   .then_inc(c_slot, 1)

            def c_middle(t, half):
                eng.wait_ge(c_gexp2, 2 * t + half + 1)
                then = link(eng, chain_c_mid, 2 * t + half)
                then(eng.scalar_tensor_tensor(sh_act[:, half, :], sh_exp[:, half, :], 1.0, bank_c(t)[:, 0:SH],
                                              ALU.add, ALU.mult))
                at(eng, c_midT_psum, t)
                eng.scalar_tensor_tensor(sh_mid[:, SH * half:SH * half + SH], sh_act[:, half, :], 0.5,
                                         bank_c(t)[:, SH:2 * SH], ALU.mult, ALU.mult).then_inc(c_mid, 1)

            def c_result(t):
                eng.wait_ge(c_down, t + 1)
                at(eng, y_out_s, 16 * t)
                eng.tensor_copy(y_sb[:, :], bank_c(t)[:, 0:CM]).then_inc(c_y, 1)

            for tile in (qk_pad, v_a, seen_bf):
                eng.memset(tile[:], 0.0).then_inc(dve_setup, 1)
            eng.wait_ge(dve_setup, 3)
            eng.memset(v_a[:, :, HD:HD + 1], 1.0)
            eng.memset(ones_bf[:, :], 1.0).then_inc(dve_setup, 1)
            eng.wait_ge(dve_setup, 4)
            eng.wait_ge(const_a_in, 16 * 3)

            def step(a, b, c, d):
                if c is not None:
                    b_weigh(c, 3)
                if c is not None and d is not None:
                    c_logits(d)
                if b is not None:
                    a_normalise(b)
                if a is not None:
                    a_rope(a)
                if b is not None:
                    a_residual(b)
                if c is not None and d is not None:
                    c_choose(d)
                    c_mask(d)
                if b is not None:
                    a_norm(b)
                if c is not None:
                    b_residual(c)
                if d is not None:
                    c_slots(d)
                if a is not None:
                    a_scale(a)
                if c is not None:
                    b_norm(c)
                if c is not None and d is not None:
                    c_weights(d)
                if b is not None:
                    b_rotate_keys(b)
                    b_rotate(b, 0)
                if d is not None:
                    c_middle(d, 0)
                if b is None and c is not None:
                    c_logits(c)
                if b is not None:
                    b_rotate_add(b, 0)
                    b_rotate(b, 1)
                    b_rotate_add(b, 1)
                if d is not None:
                    c_middle(d, 1)
                if b is None and c is not None:
                    c_choose(c)
                    c_mask(c)
                    c_weights(c)
                if b is not None:
                    b_maxima(b, 0)
                    b_maxima(b, 1)
                    b_maxima(b, 2)
                    b_weigh(b, 0)
                    b_weigh(b, 1)
                if d is not None:
                    c_result(d)
                if b is not None:
                    b_maxima(b, 3)
                    b_weigh(b, 2)

            run_steps(step, eng)

            def expert(i, k):
                if have(i, k, 1):
                    e, s = D_RING * i + k - 1, (k - 1) % D_RING
                    b = bank[2 + s % 2]
                    eng.wait_ge(d_exp, e + 1)
                    then = link(eng, chain_d_mid, e)
                    then(eng.scalar_tensor_tensor(e_act[:, s % 2, :], e_exp[:, s % 2, :], 1.0, b[:, 0:EI],
                                                  ALU.add, ALU.mult))
                    at(eng, d_midT_psum, two_ago(e, i, 1 - k))
                    eng.scalar_tensor_tensor(e_mid[:, s % 2, :], e_act[:, s % 2, :], 0.5, b[:, EI:2 * EI],
                                             ALU.mult, ALU.mult).then_inc(d_mid, 1)
                if have(i, k, 1):
                    e, s = D_RING * i + k - 1, (k - 1) % D_RING
                    eng.wait_ge(ex_in[s], 16 * (i + 1 if k >= 1 else i))
                    at(eng, d_added[s % 2], 16 * earlier_pairs(i, k))
                    eng.tensor_copy(etok[:, s:s + 1], ex[:, s, ROWW - 1:ROWW].bitcast(U32))
                    eng.tensor_copy(e_weight[:, s:s + 1], ex[:, s, bass.ds(e + CM, 1)]).then_inc(d_copied, 1)
                if have(i, k, 3):
                    e, s = D_RING * i + k - 3, (k - 3) % D_RING
                    eng.wait_ge(d_copied, e + 1)
                    eng.wait_ge(d_down, e + 1)
                    at(eng, d_added[s % 2], 16 * earlier_pairs(i, k))
                    eng.tensor_scalar(e_out[:, s % 2, :], bank[6 + s % 2][:, 0:CM], e_weight[:, s:s + 1],
                                      None, ALU.mult).then_inc(d_out, 1)

            run_experts(expert, eng)

            for g in range(FG):
                eng.wait_ge(yl_in[g], 32)
                then = link(eng, chain_e_norm, 2 * g)
                fin = fin_in[0][g]
                then(eng.tensor_tensor(fin, fin, fin_in[1][g], ALU.add))
                for j in range(FJ):
                    ins = eng.bn_stats(fin_stats[:, g, j, :], fin[:, CM * j:CM * j + CM])
                then(ins)
                for j in range(FJ):
                    ins = eng.bn_aggr(fin_mv[:, g, j, :], fin_stats[:, g, j, :])
                ins.then_inc(e_var, 1)

        @block.gpsimd
        def _(eng):
            def root(var_ap, eps_tile, out, chain, base, done_s, eps, scale=None):
                alone(eng)
                if scale is None:
                    ins = eng.tensor_scalar(eps_tile, var_ap, eps, None, ALU.add)
                else:
                    ins = eng.tensor_scalar(eps_tile, var_ap, scale, eps, ALU.mult, ALU.add)
                link(eng, chain, base)(ins)
                n = eps_tile.shape[1]
                eng.tensor_tensor(out, eps_tile, minus_half[:, 0:n], ALU.pow).then_inc(done_s, 1)

            def b_copy(t):
                eng.wait_ge(a_x1, t + 1)
                at(eng, b_res, t)
                alone(eng)
                eng.tensor_copy(x1_keep[:, :], x1[:, :]).then_inc(b_keep, 1)

            def b_window(t):
                if isinstance(t, int) and t == 0:
                    eng.wait_ge(const_in, 16 * 7)
                eng.wait_ge(seg_in, 16 * (t + 1))
                at(eng, b_score, 4 * t)
                then = link(eng, chain_b_mask, 3 * t)
                alone(eng)
                then(eng.tensor_copy(seg_f[:, :], seg[:, :]))
                alone(eng)
                then(eng.tensor_scalar(mask_d[:, :], key_pos[:, :], seg_f[:, :], None, ALU.subtract))
                then(eng.tensor_tensor(mask_b[:, :], mask_d[:, :], mask_d[:, :], ALU.mult))
                alone(eng)
                eng.tensor_scalar(mask_b[:, :], mask_b[:, :], float(LOOKBACK * LOOKBACK) / 4, NEG,
                                  ALU.is_gt, ALU.mult).then_inc(b_mask, 1)

            def a_root(t, k):
                eng.wait_ge(a_ss, t + 1)
                at(eng, a_qk, t)
                heads = slice(H * k, H * k + H)
                root(qk_ss[:, heads], qk_ms[:, heads], qk_rs[:, heads], chain_a_rs, 2 * t + k, a_rs, RMS_EPS, 1.0 / HD)

            def a_causal(t):
                for j in range(4):
                    eng.wait_ge(a_exp, 4 * t + j + 1)
                    alone(eng)
                    pj = prob_a[:, 4 * j:4 * j + 4, :]
                    eng.affine_select(out=pj, in_=pj, compare_op=ALU.is_ge, fill=zero, base=0,
                                      pattern=[[0, 4], [1, P]], channel_multiplier=-1).then_inc(a_masked, 1)

            def a_norm_root(t):
                eng.wait_ge(a_var, t + 1)
                at(eng, a_x1, t)
                root(mv["a"][:, 1:2], var_eps["a"][:, :], rstd["a"][:, :], chain_a_rstd, t, a_rstd, LN_EPS)

            def b_norm_root(t):
                eng.wait_ge(b_var, t + 1)
                at(eng, b_x2, t)
                root(mv["b"][:, 1:2], var_eps["b"][:, :], rstd["b"][:, :], chain_b_rstd, t, b_rstd, LN_EPS)

            def c_send(t):
                eng.wait_ge(c_slot, t + 1)
                eng.wait_ge(c_row, t + 1)
                eng.wait_ge(c_row_x, t + 1)
                if isinstance(t, int) and t == 0:
                    eng.wait_ge(zeros_out, 16 * (E + 2))
                alone(eng)
                for k in range(TOPK):
                    eng.indirect_dma_start(
                        out=slots_dram[:, :], out_offset=bass.IndirectOffsetOnAxis(ap=slot_no[:, k:k + 1], axis=0),
                        in_=row[:, :], in_offset=None, bounds_check=last_slot, oob_is_err=False)\
                       .then_inc(c_sent, 16)

            zero = eng.to_reg(0.0)
            last_slot, last_row = eng.to_reg(E * CAP - 1), eng.to_reg(NTOK + P - 1)
            eng.memset(ex[:, :, :], 0.0).then_inc(pool_zeros, 1)
            eng.memset(minus_half[:, :], -0.5).then_inc(pool_zeros, 1)
            eng.wait_ge(pool_zeros, 2)

            def step(a, b, c, d):
                if b is not None:
                    b_window(b)
                if a is not None:
                    a_root(a, 0)
                if b is not None:
                    a_norm_root(b)
                if a is not None:
                    a_root(a, 1)
                if c is not None:
                    b_norm_root(c)
                if d is not None:
                    c_send(d)
                if a is not None:
                    a_causal(a)
                if b is not None:
                    b_copy(b)

            run_steps(step, eng)

            def expert(i, k):
                if have(i, k, 3):
                    e, s = D_RING * i + k - 3, (k - 3) % D_RING
                    eng.wait_ge(d_out, e + 1)
                    at(eng, d_added[s % 2], 16 * earlier_pairs(i, k))
                    alone(eng)
                    eng.indirect_dma_start(
                        out=y_dram[s % 2][:, :],
                        out_offset=bass.IndirectOffsetOnAxis(ap=etok[:, s:s + 1], axis=0),
                        in_=e_out[:, s % 2, :], in_offset=None, bounds_check=last_row, oob_is_err=True,
                        compute_op=ALU.add).then_inc(d_added[s % 2], 16)

            eng.wait_ge(row_out_s, 16 * TILES)
            eng.wait_ge(y_out_s, 16 * TILES)
            run_experts(expert, eng)
            for g in range(FG):
                eng.wait_ge(e_var, g + 1)
                then = link(eng, chain_e_rstd, 2 * g)
                eng.tensor_scalar(fin_neg[:, g, :], fin_mv[:, g, :, 0], -1.0, None, ALU.mult)
                then(eng.tensor_scalar(fin_var[:, g, :], fin_mv[:, g, :, 1], LN_EPS, None, ALU.add))
                then(eng.tensor_tensor(fin_rstd[:, g, :], fin_var[:, g, :], minus_half[:, 0:FJ], ALU.pow))
                eng.tensor_tensor(fin_bias[:, g, :], fin_neg[:, g, :], fin_rstd[:, g, :], ALU.mult).then_inc(e_rstd, 1)


def _tables():
    pos = np.arange(P, dtype=np.float32)
    inv_a = (1.0 / np.float32(10000.0) ** (np.arange(0, HD, 2, dtype=np.float32) / np.float32(HD))).astype(np.float32)
    ang_a = np.repeat(pos[:, None] * inv_a[None, :], 2, axis=1)
    sign_a = np.tile(np.array([-1, 1], np.float32), HD // 2)
    half = R // 2
    inv_b = (1.0 / np.float32(10000.0) ** (np.arange(half, dtype=np.float32) / np.float32(half))).astype(np.float32)
    ang_b = np.tile((pos[:, None] * inv_b[None, :]).T, (4, 1))
    sign_b = np.tile(np.repeat(np.array([-1, 1], np.float32), half), 2)[:, None]
    p = np.arange(P)
    return {
        "ident": np.eye(P, dtype=np.float32),
        "cos_a": np.tile(np.cos(ang_a), (1, 2 * H)).astype(np.float32),
        "sin_a": np.tile(np.sin(ang_a) * sign_a, (1, 2 * H)).astype(np.float32),
        "cos_b": np.cos(ang_b).astype(np.float32),
        "sin_b": (np.sin(ang_b) * sign_b).astype(np.float32),
        "key_pos": np.tile((p + LOOKBACK / 2).astype(np.float32), (P, 1)),
        "slot_base": np.tile((NOSLOT - CAP * np.arange(E)).astype(np.float32), (P, 1)),
        "expert_no": np.tile(np.arange(E, dtype=np.float32), (P, 1)),
        "earlier": (p[:, None] < p[None, :]).astype(mybir.dt.np(BF16)),
        "token_no": (p - P).astype(np.int32)[:, None],
        "empty_no": (NTOK + p).astype(np.int32)[:, None],
    }


def _layouts(i):
    T = np.ascontiguousarray
    wqr = i["L0_xattn_W_qr"].reshape(QC, H // 2, 2, R)[:, :, ::-1, :]
    swapped = np.concatenate([wqr[..., R // 2:], wqr[..., :R // 2]], axis=-1)
    wkr = i["L0_xattn_W_kr"]
    wkr_s = np.concatenate([wkr[:, R // 2:], wkr[:, :R // 2]], axis=1)
    g, u = i["L0_ffn_sw_gate"], i["L0_ffn_sw_up"]
    return {
        "x": T(i["x"]),
        "xT": T(i["x"].transpose(0, 2, 1)),
        "ctxT": T(i["ctx_2048"].transpose(0, 2, 1)),
        "seg": T(i["itok_BxS_0_1023"]),
        "wqkvT": T(i["L0_attn_W_qkv"].T),
        "woT": T(i["L0_attn_W_o"].T),
        "wkvc2": T(np.concatenate([i["L0_xattn_W_kvc"]] * 2, axis=1)),
        "wdq": T(i["L0_xattn_W_dq"]),
        "wkr2": T(np.concatenate([wkr, wkr, wkr_s, wkr_s], axis=1)),
        "wqr": T(np.concatenate([wqr.reshape(QC, H * R), swapped.reshape(QC, H * R)], axis=1)),
        "uqT": T(i["L0_xattn_W_uq"].T),
        "ukT": T(i["L0_xattn_W_uk"].T),
        "uvT": T(i["L0_xattn_W_uv"].T),
        "wox": T(i["L0_xattn_W_o"]),
        "wgateT": T(i["L0_ffn_gate_w"].T),
        "wsh": T(np.concatenate([g[:, :SH], u[:, :SH], g[:, SH:], u[:, SH:]], axis=1)),
        "wshd": T(i["L0_ffn_sw_down"]),
        "ew": T(np.concatenate([i["L0_ffn_w_gate"], i["L0_ffn_w_up"]], axis=2)),
        "ewd": T(i["L0_ffn_w_down"]),
    }


def kernel(**inputs):
    import concourse.bacc as bacc
    from concourse.bass_utils import run_bass_kernel_spmd

    nc = bacc.Bacc("TRN2", target_bir_lowering=False, num_devices=1)
    arrays, io = {}, {}
    for name, a in {**_layouts({k: np.asarray(v) for k, v in inputs.items()}), **_tables()}.items():
        arrays[f"in_{name}"] = a
        io[name] = nc.dram_tensor(f"in_{name}", a.shape, mybir.dt.from_np(a.dtype), kind="ExternalInput").ap()
    y = nc.dram_tensor("out_y", (TILES, P, CM), F32, kind="ExternalOutput").ap()
    layer(nc, io, y)
    r = run_bass_kernel_spmd(nc, [arrays], core_ids=[0])
    return r.results[0]["out_y"]
```
